# Optimizing a Trainium2 kernel written in Bass

```python
import numpy as np
import jax
import jax.numpy as jnp

def _softmax(x, axis=-1):
    return jax.nn.softmax(x, axis=axis)

def _gelu(x):
    return jax.nn.gelu(x, approximate=True)

def _silu(x):
    return jax.nn.silu(x)

def _sigmoid(x):
    return jax.nn.sigmoid(x)

def _layernorm(x, axis=-1, eps=1e-05):
    m = jnp.mean(x, axis=axis, keepdims=True)
    v = jnp.var(x, axis=axis, keepdims=True)
    return (x - m) / jnp.sqrt(v + eps)

def _scatter_add(tgt, idx, src, axis=0):
    return tgt.at[idx].add(src)

def _segment_sum(src, seg, n):
    return jax.ops.segment_sum(src, seg, n)
kernel_name = 'mk_adaln_d2_jaxref_r8_da2d8b'

def setup_inputs(seed: int=0):
    np.random.seed(seed)
    _w = jnp.asarray

    def _L0_attn_setup():
        import jax, jax.numpy as jnp
        import numpy as np
        import math
        B, T, C = (2, 256, 128)
        H, L = (16, 64)
        DH = C // H
        DHE = DH // 2
        THETA = 10000.0

        def _rope_cache(t, dim):
            inv_freq = 1.0 / THETA ** (jnp.arange(0, dim, 2, dtype=jnp.float32) / dim)
            freqs = jnp.arange(t, dtype=jnp.float32)[:, None] * inv_freq[None, :]
            emb = jnp.concatenate((freqs, freqs), axis=-1)
            return (jnp.cos(emb), jnp.sin(emb))

        def _apply_rope(x, cos, sin):
            x1 = x[..., 0::2]
            x2 = x[..., 1::2]
            rot = jnp.stack((-x2, x1), axis=-1).reshape(x.shape)
            return x * cos[None, None] + rot * sin[None, None]
        key = jax.random.key(seed)
        ks = jax.random.split(key, 10)
        s = 0.02
        return {'x': jax.random.normal(ks[0], (B, T, C), jnp.float32), 'Wq_down': jax.random.normal(ks[1], (C, H * L), jnp.float32) * s, 'Wk_down': jax.random.normal(ks[2], (C, H * L), jnp.float32) * s, 'Wv_down': jax.random.normal(ks[3], (C, H * L), jnp.float32) * s, 'Wq_up_c': jax.random.normal(ks[4], (L, DHE), jnp.float32) * s, 'Wq_up_e': jax.random.normal(ks[5], (L, DHE), jnp.float32) * s, 'Wk_up_c': jax.random.normal(ks[6], (L, DHE), jnp.float32) * s, 'Wk_up_e': jax.random.normal(ks[7], (L, DHE), jnp.float32) * s, 'Wv_up': jax.random.normal(ks[8], (L, DH), jnp.float32) * s, 'Wc': jax.random.normal(ks[9], (C, C), jnp.float32) * s}
    _L0_attn_in = _L0_attn_setup()

    def _L0_ffn_setup():
        import jax, jax.numpy as jnp
        import numpy as np
        HIDDEN = 128
        INTER = 512
        NUM_EXPERTS = 8
        TOP_K = 2
        EPS = 1e-05

        def _layer_norm(x, g, b):
            m = jnp.mean(x, axis=-1, keepdims=True)
            v = jnp.mean(jnp.square(x - m), axis=-1, keepdims=True)
            return (x - m) * jax.lax.rsqrt(v + EPS) * g + b
        key = jax.random.key(seed)
        ks = jax.random.split(key, 8)
        s = 0.02
        return {'x': jax.random.normal(ks[0], (4, 256, HIDDEN), dtype=jnp.float32), 'ln1_g': jnp.ones((HIDDEN,), jnp.float32), 'ln1_b': jnp.zeros((HIDDEN,), jnp.float32), 'attn_w': jax.random.normal(ks[1], (HIDDEN, HIDDEN), jnp.float32) * s, 'ln2_g': jnp.ones((HIDDEN,), jnp.float32), 'ln2_b': jnp.zeros((HIDDEN,), jnp.float32), 'gate_w': jax.random.normal(ks[2], (NUM_EXPERTS, HIDDEN), jnp.float32) * s, 'gate_proj': jax.random.normal(ks[3], (NUM_EXPERTS, INTER, HIDDEN), jnp.float32) * s, 'up_proj': jax.random.normal(ks[4], (NUM_EXPERTS, INTER, HIDDEN), jnp.float32) * s, 'down_proj': jax.random.normal(ks[5], (NUM_EXPERTS, HIDDEN, INTER), jnp.float32) * s}
    _L0_ffn_in = _L0_ffn_setup()
    _L0_c = _w((lambda *s: np.random.randn(*s).astype(np.float32) * 0.05)(16, 128))
    _L0_wmod = _w((lambda *s: np.random.randn(*s).astype(np.float32) * 0.05)(128, 6 * 128) * 128 ** (-0.5))

    def _L1_attn_setup():
        import jax, jax.numpy as jnp
        import numpy as np
        EPS = 1e-06
        NEG = -10000.0

        def compute_alibi_slopes(n_head):
            start = 2.0 ** (-8.0 / n_head)
            return jnp.asarray([start ** (i + 1) for i in range(n_head)], dtype=jnp.float32)

        def rational_softmax(scores, eps=EPS):
            num = 0.5 * (1.0 + scores * jax.lax.rsqrt(1.0 + scores * scores))
            return num / (jnp.sum(num, axis=-1, keepdims=True) + eps)
        key = jax.random.key(seed)
        k1, k2, k3 = jax.random.split(key, 3)
        B, T, C, H = (2, 256, 128, 16)
        x = jax.random.normal(k1, (B, T, C), dtype=jnp.float32)
        w_qkv = jax.random.normal(k2, (3 * C, C), dtype=jnp.float32) * C ** (-0.5)
        w_out = jax.random.normal(k3, (C, C), dtype=jnp.float32) * C ** (-0.5)
        alibi_slopes = compute_alibi_slopes(H)
        return {'x': x, 'w_qkv': w_qkv, 'w_out': w_out, 'alibi_slopes': alibi_slopes}
    _L1_attn_in = _L1_attn_setup()

    def _L1_ffn_setup():
        import jax, jax.numpy as jnp
        import numpy as np
        B, C, D, O = (4, 512, 128, 128)
        PROJ = 32
        RANKS = [1, 2, 4, 8]
        E = len(RANKS)
        CLAMP_MAX = float(np.log(1.0 / 0.01))

        def _l2norm(v, axis):
            return v / jnp.maximum(jnp.linalg.norm(v, axis=axis, keepdims=True), 1e-12)
        key = jax.random.key(seed)
        ks = jax.random.split(key, 16)
        inp = {'x': jax.random.normal(ks[0], (B, C, D), dtype=jnp.float32), 'W': jax.random.normal(ks[1], (O, D), dtype=jnp.float32) / np.sqrt(D), 'Wp': jax.random.normal(ks[2], (PROJ, D), dtype=jnp.float32) / np.sqrt(D), 'bp': jnp.zeros((PROJ,), dtype=jnp.float32), 'sim': jax.random.normal(ks[3], (PROJ, E), dtype=jnp.float32) * 0.01, 'temp': jnp.full((1,), np.log(1.0 / 0.5), dtype=jnp.float32)}
        for i, r in enumerate(RANKS):
            inp[f'Wd{i}'] = jax.random.normal(ks[4 + 2 * i], (r, D), dtype=jnp.float32) / r
            inp[f'Wu{i}'] = jax.random.normal(ks[5 + 2 * i], (O, r), dtype=jnp.float32) * 0.01
        return inp
    _L1_ffn_in = _L1_ffn_setup()
    _L1_c = _w((lambda *s: np.random.randn(*s).astype(np.float32) * 0.05)(16, 128))
    _L1_wmod = _w((lambda *s: np.random.randn(*s).astype(np.float32) * 0.05)(128, 6 * 128) * 128 ** (-0.5))
    _d = {'L0_attn_x': _L0_attn_in['x'], 'L0_attn_Wq_down': _L0_attn_in['Wq_down'], 'L0_attn_Wk_down': _L0_attn_in['Wk_down'], 'L0_attn_Wv_down': _L0_attn_in['Wv_down'], 'L0_attn_Wq_up_c': _L0_attn_in['Wq_up_c'], 'L0_attn_Wq_up_e': _L0_attn_in['Wq_up_e'], 'L0_attn_Wk_up_c': _L0_attn_in['Wk_up_c'], 'L0_attn_Wk_up_e': _L0_attn_in['Wk_up_e'], 'L0_attn_Wv_up': _L0_attn_in['Wv_up'], 'L0_attn_Wc': _L0_attn_in['Wc'], 'L0_ffn_ln1_g': _L0_ffn_in['ln1_g'], 'L0_ffn_ln1_b': _L0_ffn_in['ln1_b'], 'L0_ffn_attn_w': _L0_ffn_in['attn_w'], 'L0_ffn_ln2_g': _L0_ffn_in['ln2_g'], 'L0_ffn_ln2_b': _L0_ffn_in['ln2_b'], 'L0_ffn_gate_w': _L0_ffn_in['gate_w'], 'L0_ffn_gate_proj': _L0_ffn_in['gate_proj'], 'L0_ffn_up_proj': _L0_ffn_in['up_proj'], 'L0_ffn_down_proj': _L0_ffn_in['down_proj'], 'L0_c': _L0_c, 'L0_wmod': _L0_wmod, 'L1_attn_w_qkv': _L1_attn_in['w_qkv'], 'L1_attn_w_out': _L1_attn_in['w_out'], 'L1_attn_alibi_slopes': _L1_attn_in['alibi_slopes'], 'L1_ffn_W': _L1_ffn_in['W'], 'L1_ffn_Wp': _L1_ffn_in['Wp'], 'L1_ffn_bp': _L1_ffn_in['bp'], 'L1_ffn_sim': _L1_ffn_in['sim'], 'L1_ffn_temp': _L1_ffn_in['temp'], 'L1_ffn_Wd0': _L1_ffn_in['Wd0'], 'L1_ffn_Wu0': _L1_ffn_in['Wu0'], 'L1_ffn_Wd1': _L1_ffn_in['Wd1'], 'L1_ffn_Wu1': _L1_ffn_in['Wu1'], 'L1_ffn_Wd2': _L1_ffn_in['Wd2'], 'L1_ffn_Wu2': _L1_ffn_in['Wu2'], 'L1_ffn_Wd3': _L1_ffn_in['Wd3'], 'L1_ffn_Wu3': _L1_ffn_in['Wu3'], 'L1_c': _L1_c, 'L1_wmod': _L1_wmod}
    _x0 = _d['L0_attn_x']
    _d['L0_attn_x'] = jax.random.normal(jax.random.fold_in(jax.random.key(seed), 1), (16, 256, 128), dtype=_x0.dtype)
    del _x0
    return _d

def reference(L0_attn_x, L0_attn_Wq_down, L0_attn_Wk_down, L0_attn_Wv_down, L0_attn_Wq_up_c, L0_attn_Wq_up_e, L0_attn_Wk_up_c, L0_attn_Wk_up_e, L0_attn_Wv_up, L0_attn_Wc, L0_ffn_ln1_g, L0_ffn_ln1_b, L0_ffn_attn_w, L0_ffn_ln2_g, L0_ffn_ln2_b, L0_ffn_gate_w, L0_ffn_gate_proj, L0_ffn_up_proj, L0_ffn_down_proj, L0_c, L0_wmod, L1_attn_w_qkv, L1_attn_w_out, L1_attn_alibi_slopes, L1_ffn_W, L1_ffn_Wp, L1_ffn_bp, L1_ffn_sim, L1_ffn_temp, L1_ffn_Wd0, L1_ffn_Wu0, L1_ffn_Wd1, L1_ffn_Wu1, L1_ffn_Wd2, L1_ffn_Wu2, L1_ffn_Wd3, L1_ffn_Wu3, L1_c, L1_wmod):

    def _L0_attn_ref(x, Wq_down, Wk_down, Wv_down, Wq_up_c, Wq_up_e, Wk_up_c, Wk_up_e, Wv_up, Wc):
        import jax, jax.numpy as jnp
        import numpy as np
        import math
        B, T, C = (2, 256, 128)
        H, L = (16, 64)
        DH = C // H
        DHE = DH // 2
        THETA = 10000.0

        def _rope_cache(t, dim):
            inv_freq = 1.0 / THETA ** (jnp.arange(0, dim, 2, dtype=jnp.float32) / dim)
            freqs = jnp.arange(t, dtype=jnp.float32)[:, None] * inv_freq[None, :]
            emb = jnp.concatenate((freqs, freqs), axis=-1)
            return (jnp.cos(emb), jnp.sin(emb))

        def _apply_rope(x, cos, sin):
            x1 = x[..., 0::2]
            x2 = x[..., 1::2]
            rot = jnp.stack((-x2, x1), axis=-1).reshape(x.shape)
            return x * cos[None, None] + rot * sin[None, None]
        b, t, c = x.shape
        q_lat = (x @ Wq_down).reshape(b, t, H, L)
        k_lat = (x @ Wk_down).reshape(b, t, H, L)
        v_lat = (x @ Wv_down).reshape(b, t, H, L)
        q_c = jnp.einsum('bthl,ld->bhtd', q_lat, Wq_up_c)
        q_e = jnp.einsum('bthl,ld->bhtd', q_lat, Wq_up_e)
        k_c = jnp.einsum('bthl,ld->bhtd', k_lat, Wk_up_c)
        k_e = jnp.einsum('bthl,ld->bhtd', k_lat, Wk_up_e)
        v = jnp.einsum('bthl,ld->bhtd', v_lat, Wv_up)
        cos, sin = _rope_cache(t, DHE)
        q = jnp.concatenate([q_c, _apply_rope(q_e, cos, sin)], axis=-1)
        k = jnp.concatenate([k_c, _apply_rope(k_e, cos, sin)], axis=-1)
        scale = 1.0 / math.sqrt(DH)
        scores = jnp.einsum('bhqd,bhkd->bhqk', q, k) * scale
        causal = jnp.tril(jnp.ones((t, t), dtype=bool))
        scores = jnp.where(causal[None, None], scores, -jnp.inf)
        att = jax.nn.softmax(scores, axis=-1)
        y = jnp.einsum('bhqk,bhkd->bhqd', att, v)
        y = y.transpose(0, 2, 1, 3).reshape(b, t, c)
        return y @ Wc

    def _L0_ffn_ref(x, ln1_g, ln1_b, attn_w, ln2_g, ln2_b, gate_w, gate_proj, up_proj, down_proj):
        import jax, jax.numpy as jnp
        import numpy as np
        HIDDEN = 128
        INTER = 512
        NUM_EXPERTS = 8
        TOP_K = 2
        EPS = 1e-05

        def _layer_norm(x, g, b):
            m = jnp.mean(x, axis=-1, keepdims=True)
            v = jnp.mean(jnp.square(x - m), axis=-1, keepdims=True)
            return (x - m) * jax.lax.rsqrt(v + EPS) * g + b
        B, S, H = x.shape
        h = x + jnp.einsum('bsh,oh->bso', _layer_norm(x, ln1_g, ln1_b), attn_w)
        t = _layer_norm(h, ln2_g, ln2_b).reshape(-1, H)
        T = t.shape[0]
        logits = jnp.einsum('th,eh->te', t, gate_w)
        top_vals, top_idx = jax.lax.top_k(logits, TOP_K)
        rw = jax.nn.softmax(top_vals, axis=-1)
        comb = jnp.zeros((T, NUM_EXPERTS), dtype=t.dtype)
        comb = comb.at[jnp.arange(T)[:, None], top_idx].add(rw)
        out = jnp.zeros_like(t)
        for e in range(NUM_EXPERTS):
            g = jnp.einsum('th,ih->ti', t, gate_proj[e])
            u = jnp.einsum('th,ih->ti', t, up_proj[e])
            oe = jnp.einsum('ti,hi->th', jax.nn.silu(g) * u, down_proj[e])
            out = out + comb[:, e:e + 1] * oe
        return h + out.reshape(B, S, H)

    def _L1_attn_ref(x, w_qkv, w_out, alibi_slopes):
        import jax, jax.numpy as jnp
        import numpy as np
        EPS = 1e-06
        NEG = -10000.0

        def compute_alibi_slopes(n_head):
            start = 2.0 ** (-8.0 / n_head)
            return jnp.asarray([start ** (i + 1) for i in range(n_head)], dtype=jnp.float32)

        def rational_softmax(scores, eps=EPS):
            num = 0.5 * (1.0 + scores * jax.lax.rsqrt(1.0 + scores * scores))
            return num / (jnp.sum(num, axis=-1, keepdims=True) + eps)
        B, T, C = x.shape
        H = alibi_slopes.shape[0]
        D = C // H
        scale = 1.0 / jnp.sqrt(jnp.float32(D))
        qkv = (x @ w_qkv.T).reshape(B, T, 3, H, D)
        qkv = jnp.transpose(qkv, (2, 0, 3, 1, 4))
        q, k, v = (qkv[0], qkv[1], qkv[2])
        scores = jnp.einsum('bhtd,bhsd->bhts', q, k) * scale
        pos = jnp.arange(T)
        rel = pos[:, None] - pos[None, :]
        alibi = -jnp.abs(rel).astype(jnp.float32) * alibi_slopes[None, :, None, None]
        scores = scores + alibi
        causal = rel < 0
        scores = jnp.where(causal[None, None], NEG, scores)
        probs = rational_softmax(scores, EPS)
        out = jnp.einsum('bhts,bhsd->bhtd', probs, v)
        out = jnp.transpose(out, (0, 2, 1, 3)).reshape(B, T, C)
        return out @ w_out.T

    def _L1_ffn_ref(x, W, Wp, bp, sim, temp, Wd0, Wu0, Wd1, Wu1, Wd2, Wu2, Wd3, Wu3):
        import jax, jax.numpy as jnp
        import numpy as np
        B, C, D, O = (4, 512, 128, 128)
        PROJ = 32
        RANKS = [1, 2, 4, 8]
        E = len(RANKS)
        CLAMP_MAX = float(np.log(1.0 / 0.01))

        def _l2norm(v, axis):
            return v / jnp.maximum(jnp.linalg.norm(v, axis=axis, keepdims=True), 1e-12)
        base = jnp.einsum('bcd,od->bco', x, W)
        xf = x.reshape(-1, x.shape[-1])
        proj = _l2norm(xf @ Wp.T + bp, axis=1)
        simn = _l2norm(sim, axis=0)
        scale = jnp.exp(jnp.minimum(temp, CLAMP_MAX))
        logits = proj @ simn * scale
        lw = jax.nn.softmax(logits, axis=1)
        top1 = jnp.argmax(lw, axis=1)
        ret = jnp.where(jnp.arange(E)[None, :] == top1[:, None], lw, 0.0)
        ret = ret.reshape(x.shape[0], x.shape[1], E)
        downs = (Wd0, Wd1, Wd2, Wd3)
        ups = (Wu0, Wu1, Wu2, Wu3)
        l = jnp.stack([jnp.einsum('bcr,or->bco', jnp.einsum('bcd,rd->bcr', x, d), u) for d, u in zip(downs, ups)], axis=2)
        res = jnp.sum(ret[..., None] * l, axis=2)
        return base + res
    x = L0_attn_x
    mod = (_silu(L0_c) @ L0_wmod).reshape(L0_c.shape[0], 6, 1, -1)
    sa, ca, ga, sb, cb, gb = (mod[:, 0], mod[:, 1], mod[:, 2], mod[:, 3], mod[:, 4], mod[:, 5])
    ga = (2 * (ga >= 0) - 1) * jnp.maximum(jnp.abs(ga), 0.25)
    gb = (2 * (gb >= 0) - 1) * jnp.maximum(jnp.abs(gb), 0.25)
    h = _layernorm(x, axis=-1) * (1 + ca) + sa
    x = x + ga * _L0_attn_ref(h, L0_attn_Wq_down, L0_attn_Wk_down, L0_attn_Wv_down, L0_attn_Wq_up_c, L0_attn_Wq_up_e, L0_attn_Wk_up_c, L0_attn_Wk_up_e, L0_attn_Wv_up, L0_attn_Wc)
    h = _layernorm(x, axis=-1) * (1 + cb) + sb
    x = x + gb * _L0_ffn_ref(h, L0_ffn_ln1_g, L0_ffn_ln1_b, L0_ffn_attn_w, L0_ffn_ln2_g, L0_ffn_ln2_b, L0_ffn_gate_w, L0_ffn_gate_proj, L0_ffn_up_proj, L0_ffn_down_proj)
    mod = (_silu(L1_c) @ L1_wmod).reshape(L1_c.shape[0], 6, 1, -1)
    sa, ca, ga, sb, cb, gb = (mod[:, 0], mod[:, 1], mod[:, 2], mod[:, 3], mod[:, 4], mod[:, 5])
    ga = (2 * (ga >= 0) - 1) * jnp.maximum(jnp.abs(ga), 0.25)
    gb = (2 * (gb >= 0) - 1) * jnp.maximum(jnp.abs(gb), 0.25)
    h = _layernorm(x, axis=-1) * (1 + ca) + sa
    x = x + ga * _L1_attn_ref(h, L1_attn_w_qkv, L1_attn_w_out, L1_attn_alibi_slopes)
    h = _layernorm(x, axis=-1) * (1 + cb) + sb
    x = x + gb * _L1_ffn_ref(h, L1_ffn_W, L1_ffn_Wp, L1_ffn_bp, L1_ffn_sim, L1_ffn_temp, L1_ffn_Wd0, L1_ffn_Wu0, L1_ffn_Wd1, L1_ffn_Wu1, L1_ffn_Wd2, L1_ffn_Wu2, L1_ffn_Wd3, L1_ffn_Wu3)
    return x

_drawn_inputs = setup_inputs


def setup_inputs(seed=0):
    import zlib

    import numpy as np

    out = dict(_drawn_inputs(seed))
    spreads = {'L0_ffn_ln1_g': (1.0, 0.6),
     'L0_ffn_ln1_b': (0.0, 0.8),
     'L0_ffn_ln2_g': (1.0, 0.6),
     'L0_ffn_ln2_b': (0.0, 0.8),
     'L1_ffn_bp': (0.0, 0.8)}
    factors = {'L0_attn_Wq_down': 8.0,
     'L0_attn_Wk_down': 8.0,
     'L0_attn_Wv_down': 8.0,
     'L0_attn_Wq_up_c': 8.0,
     'L0_attn_Wq_up_e': 8.0,
     'L0_attn_Wk_up_c': 8.0,
     'L0_attn_Wk_up_e': 8.0,
     'L0_attn_Wv_up': 8.0,
     'L0_attn_Wc': 8.0,
     'L0_ffn_gate_w': 8.0,
     'L0_ffn_gate_proj': 8.0,
     'L0_ffn_up_proj': 8.0,
     'L0_ffn_down_proj': 8.0,
     'L1_ffn_Wp': 8.0,
     'L1_ffn_sim': 8.0,
     'L1_ffn_Wd0': 8.0,
     'L1_ffn_Wu0': 8.0,
     'L1_ffn_Wd1': 8.0,
     'L1_ffn_Wu1': 8.0,
     'L1_ffn_Wd2': 8.0,
     'L1_ffn_Wu2': 8.0,
     'L1_ffn_Wd3': 8.0,
     'L1_ffn_Wu3': 8.0,
     'L1_attn_alibi_slopes': 3.767}
    for name, (base, spread) in spreads.items():
        noise = np.random.default_rng([zlib.crc32(name.encode()), seed]).standard_normal(out[name].shape)
        drawn = base * np.exp(spread * noise) if base else spread * noise
        out[name] = jnp.asarray(drawn.astype(out[name].dtype))
    for name, factor in factors.items():
        out[name] = (out[name] * factor).astype(out[name].dtype)
    return out
```

```python
import math
from contextlib import ExitStack

import numpy as np

import concourse.bass as bass
from concourse import mybir

F32 = mybir.dt.float32
F32R = mybir.dt.float32r
BF16 = mybir.dt.bfloat16
ALU = mybir.AluOpType
ACT = mybir.ActivationFunctionType
AX = mybir.AxisListType

P = 128
B, T = 16, 256
NT = T // P
H, D = 16, 8
DE = D // 2
L = 64
NPAIR = H // 2
ROWS = 64
SLOTS = 6
ALIBI = SLOTS * D
NE, NI = 8, 512
CH = NI // P
NCH = NE * CH
NQ = 16
NR = 4
RANKS = [1, 2, 4, 8]
RTOT = sum(RANKS)
PROJ = 32
SCALE = 1.0 / math.sqrt(D)
VW = 32
MASKED = -1e30
ROWMODS = 6
EPS_LN = 1e-5
EPS_RATIONAL = 1e-6
CLAMP_MAX = float(np.log(1.0 / 0.01))


class Signal:

    def __init__(self, ctx, nc, name, per, ahead):
        self.sem, self.per, self.ahead = ctx.enter_context(nc.semaphore(name)), per, ahead

    def __call__(self, i, n):
        return self.sem, i * self.per + (n + self.per * self.ahead)

    def before(self, i, n):
        assert self.ahead
        return self.sem, i * self.per + n


class Chain:

    def __init__(self, eng, steps, i):
        self.eng, self.steps, self.i, self.n = eng, steps, i, 0

    def __call__(self, ins):
        self.n += 1
        ins.then_inc(self.steps.sem, 1)
        self.eng.wait_ge(*self.steps(self.i, self.n))

    def done(self):
        assert self.n == self.steps.per, (self.n, self.steps.per)


def build(nc, a, out):
    with ExitStack() as ctx:
        def sb(name, shape, dt=F32):
            return ctx.enter_context(nc.sbuf_tensor(name, shape, dt))

        def sem(name):
            return ctx.enter_context(nc.semaphore(name))

        def signal(name, per=1, ahead=False):
            return Signal(ctx, nc, name, per, ahead)

        identf = sb("identf", [P, P])
        identb = sb("identb", [P, P], BF16)
        maskb = sb("maskb", [P, 2, P], BF16)
        selb = sb("selb", [P, H, P], BF16)
        rope = sb("rope", [P, 2, NT, DE])
        before = sb("before", [P, NE * NE])
        before4 = sb("before4", [P, NR * NR])
        position = sb("position", [P, NT])
        w_qkv0 = sb("w_qkv0", [P, 512])
        w_qkv1 = sb("w_qkv1", [P, 384])
        w_o = [sb("w_o0", [P, P]), sb("w_o1", [P, P])]
        w_mix = sb("w_mix", [P, P])
        w_gate = sb("w_gate", [P, NE])
        gu_hi = sb("gu_hi", [P, 2, NCH, P], F32R)
        gu_lo = sb("gu_lo", [P, 2, NCH, P], F32R)
        w_down = sb("w_down", [P, NCH, P])
        lncol = sb("lncol", [P, 4])
        w_ffn1 = sb("w_ffn1", [P, P + PROJ + RTOT])
        w_up1 = sb("w_up1", [RTOT, P])
        bp_row = sb("bp_row", [P, PROJ])
        simn = sb("simn", [PROJ, NR])
        modcols = sb("modcols", [P, B, 2, 6])
        minus_half = sb("minus_half", [P, NT])

        NU = 12
        probs = sb("probs", [P, NU, 512])
        wd3 = probs[:, 0:6, :].rearrange("p u (g c) -> p (u g) c", c=P)\
            .rearrange("p (n g) c -> p n g c", n=3)
        stage = probs[:, 6:8, :].rearrange("p u (g c) -> p (u g) c", c=P)\
            .rearrange("p (k n g) c -> p k n g c", k=2, n=2)
        modrow = probs[0:B, 8:11, :].rearrange("b u (g c) -> b (u g) c", c=P)\
            .rearrange("b (l m) c -> b l m c", l=2)
        gate_s = probs[0:B, 11, :].rearrange("b (l m c) -> b l m c", l=2, c=P)
        u2 = sb("u2", [P, 3, 2, 12])
        c_t = sb("c_t", [P, 2, B])
        silu_c = sb("silu_c", [P, 2, B])
        wmod = sb("wmod", [P, 2, 6 * P])
        gate_m = sb("gate_m", [B, 2, 2, P])
        rowmods = sb("rowmods", [B, ROWMODS, P])
        slope = sb("slope", [P, H])
        slope_r = sb("slope_r", [P, H])
        slope_p = sb("slope_p", [P, 3, H], BF16)
        simt = sb("simt", [NR, PROJ])
        simsq = sb("simsq", [NR, PROJ])
        simst = sb("simst", [NR, 4])
        tempc = sb("tempc", [NR, 1])

        x_in = sb("x_in", [P, NT, P])
        x_mid = [sb("x_a", [P, NT, P]), sb("x_c", [P, NT, P])]
        x_b = sb("x_b", [P, NT, P])
        x_out = sb("x_out", [P, NT, P])
        rows_a = sb("rows_a", [P, 1, P])
        rows_b = sb("rows_b", [P, 3, P])
        rows_c = sb("rows_c", [P, 2, P])
        cols_now = sb("cols_now", [P, 2, 6])
        stats = sb("stats", [P, NT, 6])
        meanvar = sb("meanvar", [P, NT, 2])
        vareps = sb("vareps", [P, NT])
        rstd = sb("rstd", [P, NT])
        xn = sb("xn", [P, NT, P])
        h_t = sb("h_t", [P, T])
        tmp = sb("tmp", [P, NT, P])
        raw = sb("raw", [P, NT, 512])
        rot = sb("rot", [P, NT, 2 * H, DE])
        resid = sb("resid", [P, NT, 2 * H, D])
        v_aug = sb("v_aug", [P, NT, H, VW])
        stack = [sb(f"stack{n}", [P, NT, 2 * H, ROWS], BF16) for n in range(2)]
        q_t = sb("q_t", [P, NPAIR, 2, T], BF16)
        k_t = sb("k_t", [P, NPAIR, T], BF16)
        negmax = sb("negmax", [P, NT, H])
        negmax_r = sb("negmax_r", [P, NT, H])
        max_stack = sb("max_stack", [P, NT, P], BF16)
        max_t = sb("max_t", [P, T], BF16)
        ratio = sb("ratio", [P, 3, 512])
        y_t = sb("y_t", [P, 4, T])
        den = sb("den", [P, NT, H])
        y_n = sb("y_n", [P, NT, P])
        y_nt = sb("y_nt", [P, T])
        h_ffn = sb("h_ffn", [P, NT, P])
        h2 = sb("h2", [P, NT, P])
        tt = sb("tt", [P, T])
        tt_hi = sb("tt_hi", [P, T], F32R)
        tt_lo = sb("tt_lo", [P, T], F32R)
        logit = sb("logit", [P, NT, NE])
        cmp_a = sb("cmp_a", [P, NT, NE * NE])
        cmp_b = sb("cmp_b", [P, NT, NE * NE])
        rank = sb("rank", [P, NT, NE])
        first = sb("first", [P, NT, NE])
        second = sb("second", [P, NT, NE])
        gap = sb("gap", [P, NT])
        tgap = sb("tgap", [P, NT])
        comb = sb("comb", [P, NT, NE])
        silu_g = sb("silu_g", [P, 2, T])
        hidden = sb("hidden", [P, 2, T])
        acc = sb("acc", [P, NT, P])
        pj = sb("pj", [P, NT, PROJ])
        pjsq = sb("pjsq", [P, NT, PROJ])
        pj_ss = sb("pj_ss", [P, NT])
        pj_inv = sb("pj_inv", [P, NT])
        pj_t = sb("pj_t", [PROJ, T])
        lg4 = sb("lg4", [P, NT, NR])
        ex4 = sb("ex4", [P, NT, NR])
        st4 = sb("st4", [P, 3, NT])
        ret = sb("ret", [P, NT, NR])
        dr = sb("dr", [P, NT, RTOT])
        dr_t = sb("dr_t", [RTOT, T])

        bank = [ctx.enter_context(nc.psum_tensor(f"bank{n}", [P, 512], F32)) for n in range(8)]
        SCORE = bank[0:3]
        BPV, BMISC = bank[3], bank[4]
        GU = bank[5:7]
        BOUT = bank[7]

        loads = {n: sem("ld_" + n) for n in ("const", "mod", "attn", "gu0", "gu1", "ffn", "small")}
        prep = {n: sem("prep_" + n) for n in (
            "silu", "temp", "exptemp", "u2", "simss", "siminv", "modcols_pe", "modcols", "modrows_pe", "rows",
            "weff_pe", "wqkv0", "wqkv1", "cleared", "stack1", "hi", "lo", "simt", "simn_pe",
            "simn", "dve", "pool")}
        scratch_written = sem("scratch_written")

        passed = {e: sem("passed_" + e) for e in ("pool", "dve")}

        x_loaded = signal("x_loaded", 16)
        rows_a_loaded = signal("rows_a_loaded", 16)
        rows_b_loaded = signal("rows_b_loaded", 16)
        rows_c_loaded = signal("rows_c_loaded", 16)
        cols_ready = signal("cols_ready")
        x_stored = signal("x_stored", 16, ahead=True)
        SITES = ("a", "b", "mix", "moe", "c", "d")
        var_ready = {s: signal("var_" + s) for s in SITES}
        rstd_ready = {s: signal("rstd_" + s) for s in SITES}
        xn_ready = {s: signal("xn_" + s) for s in SITES}
        xt_ready = {s: signal("xt_" + s) for s in SITES if s != "b"}
        h_ready = {s: signal("h_" + s, 1, s == "d") for s in SITES if s != "b"}
        pool_self = {s: signal("pself_" + s) for s in SITES}
        dve_self = {p: signal("dself_" + p, n) for p, n in
                    (("a", 11), ("b", 20), ("c", 9), ("d", 15))}

        def pair(name, per=1):
            return [signal(f"{name}{n}", per) for n in range(2)]

        qkv_done = pair("qkv_done", NT)
        qkv_copied = pair("qkv_copied", NT)
        parts_ready = pair("parts_ready")
        thirds_ready = pair("thirds_ready")
        placed = pair("placed")
        spread_done = pair("spread_done", 4)
        k_spread = pair("k_spread", NT)
        q_spread = pair("q_spread", NT)
        maxscore_done = signal("maxscore_done", NU)
        max_taken = signal("max_taken", NU)
        max_stacked = signal("max_stacked")
        max_turned = signal("max_turned")
        max_ready = signal("max_ready")
        score_done = pair("score_done", NU)
        squared = signal("squared", NU)
        rooted = signal("rooted", NU)
        ratio_done = signal("ratio_done", NU)
        shifted = signal("shifted", NU)
        probs_ready = pair("probs_ready", NU)
        pv_done = pair("pv_done", 2)
        pv_copied = pair("pv_copied", 2)
        y_back = pair("y_back", NT)
        y_ready = pair("y_ready")
        yt_done = pair("yt_done")
        yt_copied = pair("yt_copied")
        attn_out = pair("attn_out")
        x_mid_ready = [signal("x_a_ready", 1, ahead=True), signal("x_c_ready")]
        mix_done = signal("mix_done")
        parts_moe = signal("parts_moe")
        logits_done = signal("logits_done")
        gap_ready = signal("gap_ready")
        tanh_ready = signal("tanh_ready")
        gu_done = signal("gu_done", NCH)
        silu_done = signal("silu_done", NCH)
        hidden_ready = signal("hidden_ready", NCH)
        expert_done = signal("expert_done", NE)
        expert_added = signal("expert_added", NE)
        x_b_ready = signal("x_b_ready", 1, ahead=True)
        ffn1_done = signal("ffn1_done")
        pj_ready = signal("pj_ready")
        pjss_ready = signal("pjss_ready")
        pjinv_ready = signal("pjinv_ready")
        pjt_done = signal("pjt_done")
        pjt_ready = signal("pjt_ready")
        lg4_done = signal("lg4_done")
        lg4_shifted = signal("lg4_shifted")
        exp4_ready = signal("exp4_ready")
        dr_ready = signal("dr_ready")
        drt_done = signal("drt_done")
        drt_ready = signal("drt_ready")
        ffn1_out = signal("ffn1_out")
        x_out_ready = signal("x_out_ready", 1, ahead=True)

        scratch = a["scratch"]
        block = ctx.enter_context(nc.Block())

        def load_sequence(sp, i):
            sp.wait_ge(*x_mid_ready[0].before(i, 1))
            sp.dma_start(x_in[:, :, :], a["L0_attn_x"][bass.ds(i, 1)]
                         .rearrange("o (n p) c -> p (o n) c", p=P)).then_inc(x_loaded.sem, 16)
            for dst, lo, n, sig, user in ((rows_a, 0, 1, rows_a_loaded, None),
                                          (rows_b, 1, 3, rows_b_loaded, x_b_ready),
                                          (rows_c, 4, 2, rows_c_loaded, x_out_ready)):
                if user is not None:
                    sp.wait_ge(*user.before(i, 1))
                sp.dma_start(dst[:, :, :].rearrange("p n c -> p (n c)"),
                             scratch[bass.ds(i, 1), lo:lo + n, :]
                             .rearrange("o n c -> o (n c)").to_broadcast([P, n * P])).then_inc(sig.sem, 16)


        @block.sync
        def _(sp):
            for name, dst, src in (
                ("const", identf[:, :], a["identf"]), ("const", identb[:, :], a["identb"].bitcast(BF16)),
                ("mod", c_t[:, 0, :], a["L0_c"]), ("mod", c_t[:, 1, :], a["L1_c"]),
                ("mod", wmod[:, 0, :], a["L0_wmod"]), ("mod", wmod[:, 1, :], a["L1_wmod"]),
                ("attn", u2[:, :, :, :], a["u2"]), ("attn", wd3[:, :, :, :], a["wd3"]),
                ("const", maskb[:, :, :], a["maskb"].bitcast(BF16)), ("const", selb[:, :, :], a["selb"].bitcast(BF16)),
                ("const", rope[:, :, :, :], a["rope"]),
                ("small", slope[:, :], a["L1_attn_alibi_slopes"].partition_broadcast(P)),
                ("small", position[:, :], a["position"]), ("small", simt[:, :], a["L1_ffn_sim"]),
                ("small", tempc[:, :], a["L1_ffn_temp"].partition_broadcast(NR)),
                ("small", w_qkv1[:, :], a["L1_attn_w_qkv"]),
                ("ffn", w_o[0][:, :], a["L0_attn_Wc"]), ("ffn", w_o[1][:, :], a["L1_attn_w_out"]),
                ("ffn", w_mix[:, :], a["L0_ffn_attn_w"]), ("ffn", w_gate[:, :], a["L0_ffn_gate_w"]),
                ("ffn", lncol[:, :], a["lncol"]), ("ffn", before[:, :], a["before"]),
                ("ffn", before4[:, :], a["before4"]), ("ffn", w_ffn1[:, :], a["w_ffn1"]),
                ("ffn", w_up1[:, :], a["w_up1"]), ("ffn", bp_row[:, :], a["L1_ffn_bp"].partition_broadcast(P)),
                ("ffn", w_down[:, :, :], a["L0_ffn_down_proj"]),
            ):
                sp.dma_start(dst, src).then_inc(loads[name], 16)
            sp.sem_inc(x_stored.sem, 16)
            sp.wait_ge(prep["rows"], 1)
            sp.dma_start(scratch, rowmods[:, :, :]).then_inc(scratch_written, 16)
            sp.wait_ge(scratch_written, 16)
            with sp.Fori(0, B) as i:
                load_sequence(sp, i)
                sp.wait_ge(*x_out_ready(i, 1))
                sp.dma_start(out[bass.ds(i, 1)].rearrange("o (n p) c -> p (o n) c", p=P),
                             x_out[:, :, :]).then_inc(x_stored.sem, 16)
            sp.wait_ge(*x_stored(B - 1, 16))

        def pool_cols(pool, i):
            pool.wait_ge(*h_ready["d"].before(i, 1))
            pool.sem_inc(passed["pool"], 1)
            pool.tensor_copy(cols_now[:, :, :], modcols[:, bass.ds(i, 1), :, :]
                             .rearrange("p o l m -> p (o l) m")).then_inc(cols_ready.sem, 1)

        def pool_rstd(pool, i, s):
            pool.wait_ge(*var_ready[s](i, 1))
            pool.sem_inc(passed["pool"], 1)
            pool.tensor_scalar(vareps[:, :], meanvar[:, :, 1], EPS_LN, None, ALU.add)\
                .then_inc(pool_self[s].sem, 1)
            pool.wait_ge(*pool_self[s](i, 1))
            pool.tensor_tensor(rstd[:, :], vareps[:, :], minus_half[:, :], ALU.pow)\
                .then_inc(rstd_ready[s].sem, 1)

        def pool_place(pool, i, n):
            st = stack[n]
            pool.wait_ge(*parts_ready[n](i, 1))
            pool.sem_inc(passed["pool"], 1)
            last = None
            for qk, slot, part in ((0, 2, 0), (0, 4, 0), (0, 3, 1), (1, 3, 0), (1, 5, 0), (1, 2, 1)):
                last = pool.tensor_copy(st[:, :, qk * H:(qk + 1) * H, slot * D:(slot + 1) * D],
                                        st[:, :, qk * H:(qk + 1) * H, part * D:(part + 1) * D])
            last.then_inc(placed[n].sem, 1)

        def pool_shift(pool, i):
            for u in range(NU):
                g, r = divmod(u, 3)
                pool.wait_ge(*ratio_done(i, u + 1))
                pool.sem_inc(passed["pool"], 1)
                pool.tensor_scalar(probs[:, u, :], probs[:, u, :], 1.0, None, ALU.add)\
                    .then_inc(shifted.sem, 1)
                pool.wait_ge(*shifted(i, u + 1))
                pool.sem_inc(passed["pool"], 1)
                if r < 2:
                    v = probs[:, u, :].rearrange("p (h q) -> p h q", h=2)[:, :, 0:P]
                    pat = [[0, 2], [1, P]]
                else:
                    v = probs[:, u, :].rearrange("p (h q) -> p h q", h=4)
                    pat = [[0, 4], [1, P]]
                pool.affine_select(out=v, in_=v, compare_op=ALU.is_ge, fill=0.0, base=0,
                                   pattern=pat, channel_multiplier=-1).then_inc(probs_ready[1].sem, 1)


        @block.gpsimd
        def _(pool):
            steps = [0]

            def step(ins):
                steps[0] += 1
                ins.then_inc(prep["pool"], 1)
                pool.wait_ge(prep["pool"], steps[0])

            step(pool.memset(minus_half[:, :], -0.5))
            for n in range(2):
                pool.memset(stack[n][:, :, :, :], 0.0)
            pool.memset(max_stack[:, :, :], 0.0)
            pool.memset(q_t[:, :, :, :], 0.0)
            step(pool.memset(v_aug[:, :, :, :], 0.0))
            pool.memset(v_aug[:, :, :, D:D + 1], 1.0).then_inc(prep["cleared"], 1)
            pool.wait_ge(prep["simss"], 1)
            pool.tensor_tensor(simst[:, 3:4], simst[:, 0:1], minus_half[0:NR, 0:1], ALU.pow)\
                .then_inc(prep["siminv"], 1)
            pool.wait_ge(prep["modcols"], 1)
            with pool.Fori(0, B) as i:
                pool_cols(pool, i)
                pool_rstd(pool, i, "a")
                pool_place(pool, i, 0)
                pool_rstd(pool, i, "b")
                pool_rstd(pool, i, "mix")
                pool_rstd(pool, i, "moe")
                pool_rstd(pool, i, "c")
                pool_place(pool, i, 1)
                pool_shift(pool, i)
                pool_rstd(pool, i, "d")
                pool.wait_ge(*pjss_ready(i, 1))
                pool.tensor_tensor(pj_inv[:, :], pj_ss[:, :], minus_half[:, :], ALU.pow)\
                    .then_inc(pjinv_ready.sem, 1)

        def act_turned(act, i, s, src, scale, bias, dst):
            act.wait_ge(*xt_ready[s](i, 1))
            act.activation(dst, src, ACT.Identity, scale=scale, bias=bias).then_inc(h_ready[s].sem, 1)

        def act_attention(act, i, n):
            s = "ac"[n]
            if n == 0:
                act.wait_ge(*cols_ready(i, 1))
            act_turned(act, i, s, BMISC[:, 0:T], cols_now[:, n, 1:2], cols_now[:, n, 0:1], h_t[:, :])
            for t in range(NT):
                act.wait_ge(*qkv_done[n](i, t + 1))
                src = SCORE[t]
                if n == 0:
                    act.activation(raw[:, t, 0:256], src[:, 0:256], ACT.Copy)
                    act.activation(raw[:, t, 384:512], src[:, 384:512], ACT.Copy)
                else:
                    act.activation(raw[:, t, 0:256], src[:, 0:256], ACT.Copy)
                act.activation(v_aug[:, t, :, 0:D], src[:, 256:384].rearrange("p (h d) -> p h d", h=H),
                               ACT.Copy).then_inc(qkv_copied[n].sem, 1)
            for t in range(NT):
                act.wait_ge(*spread_done[n](i, 2 * t + 1))
                act.activation(k_t[:, :, t * P:(t + 1) * P],
                               SCORE[(2 + 2 * t) % 3][:, :].bitcast(BF16).rearrange("p (g q) -> p g q", g=NPAIR),
                               ACT.Copy).then_inc(k_spread[n].sem, 1)
            if n == 0:
                act.wait_ge(*max_turned(i, 1))
                act.activation(max_t[:, :], BMISC[:, 0:P].bitcast(BF16), ACT.Copy).then_inc(max_ready.sem, 1)
            for u in range(NU):
                act.wait_ge(*score_done[n](i, u + 1))
                if n == 0:
                    act.activation(probs[:, u, :], SCORE[u % 3][:, :], ACT.Exp, scale=SCALE)\
                        .then_inc(probs_ready[0].sem, 1)
                else:
                    if u >= 3:
                        act.wait_ge(*ratio_done(i, u - 2))
                    act.activation(ratio[:, u % 3, :], SCORE[u % 3][:, :], ACT.Square).then_inc(squared.sem, 1)
                    act.wait_ge(*squared(i, u + 1))
                    act.activation(ratio[:, u % 3, :], ratio[:, u % 3, :], ACT.Abs_reciprocal_sqrt, bias=1.0)\
                        .then_inc(rooted.sem, 1)
            act.wait_ge(*yt_done[n](i, 1))
            act.activation(y_nt[:, :], BMISC[:, 0:T], ACT.Copy).then_inc(yt_copied[n].sem, 1)

        def act_moe(act, i):
            act_turned(act, i, "mix", BOUT[:, 0:T], lncol[:, 0:1], lncol[:, 1:2], h_t[:, :])
            act_turned(act, i, "moe", BOUT[:, 0:T], lncol[:, 2:3], lncol[:, 3:4], tt[:, :])
            act.wait_ge(*gap_ready(i, 1))
            act.activation(tgap[:, :], gap[:, :], ACT.Tanh, scale=0.5).then_inc(tanh_ready.sem, 1)
            for c in range(NCH):
                act.wait_ge(*gu_done(i, c + 1))
                if c >= 2:
                    act.wait_ge(*hidden_ready(i, c - 1))
                act.activation(silu_g[:, c % 2, :], GU[c % 2][:, 0:T], ACT.Silu).then_inc(silu_done.sem, 1)

        def act_ffn1(act, i):
            act_turned(act, i, "d", BMISC[:, 0:T], cols_now[:, 1, 4:5], cols_now[:, 1, 3:4], h_t[:, :])
            act.wait_ge(*pjt_done(i, 1))
            act.activation(pj_t[:, :], BMISC[0:PROJ, 0:T], ACT.Copy).then_inc(pjt_ready.sem, 1)
            act.wait_ge(*lg4_shifted(i, 1))
            act.activation(ex4[:, :, :], lg4[:, :, :], ACT.Exp).then_inc(exp4_ready.sem, 1)
            act.wait_ge(*drt_done(i, 1))
            act.activation(dr_t[:, :], BMISC[0:RTOT, 0:T], ACT.Copy).then_inc(drt_ready.sem, 1)


        @block.scalar
        def _(act):
            act.sem_inc(h_ready["d"].sem, 1)
            piece = NCH // NQ
            for k in range(2):
                act.dma_start(stage[:, k, :, :, :], a["gu"][:, :, k * piece:(k + 1) * piece, :])\
                   .then_inc(loads[f"gu{k}"], 16)
            act.wait_ge(loads["mod"], 64)
            act.activation(silu_c[:, :, :], c_t[:, :, :], ACT.Silu).then_inc(prep["silu"], 1)
            act.wait_ge(prep["temp"], 1)
            act.activation(simst[:, 2:3], simst[:, 1:2], ACT.Exp).then_inc(prep["exptemp"], 1)
            for k in range(NQ):
                act.wait_ge(loads[f"gu{k % 2}"], 16 * (k // 2 + 1))
                act.activation(gu_hi[:, :, k * piece:(k + 1) * piece, :], stage[:, k % 2, :, :, :], ACT.Copy)\
                    .then_inc(prep["hi"], 1)
                if k + 2 < NQ:
                    act.wait_ge(prep["hi"], k + 1)
                    act.wait_ge(prep["lo"], k + 1)
                    act.dma_start(stage[:, k % 2, :, :, :], a["gu"][:, :, (k + 2) * piece:(k + 3) * piece, :])\
                       .then_inc(loads[f"gu{k % 2}"], 16)
            act.wait_ge(loads["ffn"], 11 * 16)
            with act.Fori(0, B) as i:
                act_attention(act, i, 0)
                act_moe(act, i)
                act_attention(act, i, 1)
                act_ffn1(act, i)

        def pe_turn(pe, i, s, dst):
            pe.wait_ge(*xn_ready[s](i, 1))
            for t in range(NT):
                last = pe.transpose(dst[:, t * P:(t + 1) * P], xn[:, t, :], identf[:, :])
            last.then_inc(xt_ready[s].sem, 1)

        def pe_attention(pe, i, n):
            s = "ac"[n]
            w = (w_qkv0, w_qkv1)[n]
            wide = (512, 384)[n]
            pe_turn(pe, i, s, BMISC)
            pe.wait_ge(*h_ready[s](i, 1))
            for t in range(NT):
                pe.matmul(SCORE[t][:, 0:wide], h_t[:, t * P:(t + 1) * P], w[:, :], start=True, stop=True)\
                    .then_inc(qkv_done[n].sem, 1)
            pe.wait_ge(*parts_ready[n](i, 1))
            pe.wait_ge(*thirds_ready[n](i, 1))
            pe.wait_ge(*placed[n](i, 1))
            for k in range(4):
                t, q = divmod(k, 2)
                if k == 3:
                    pe.wait_ge(*k_spread[n](i, 1))
                dst = SCORE[(2 + k) % 3][:, :].bitcast(BF16)
                for g in range(NPAIR):
                    row = (1 - q) * H + 2 * g
                    last = pe.transpose(dst[:, g * P:(g + 1) * P],
                                        stack[n][:, t, row:row + 2, :].rearrange("p h r -> p (h r)"),
                                        identb[:, :])
                last.then_inc(spread_done[n].sem, 1)
            pe.wait_ge(*k_spread[n](i, NT))
            pe.wait_ge(*q_spread[n](i, NT))
            if n == 0:
                pe_maxima(pe, i)
            for u in range(NU):
                g, r = divmod(u, 3)
                dst = SCORE[u % 3]
                if u >= 3:
                    pe.wait_ge(*((probs_ready[0] if n == 0 else ratio_done)(i, u - 2)))
                if r < 2:
                    p = 2 * g + r
                    q3 = dst[:, :].rearrange("p (h q) -> p h q", h=2)
                    if n == 0:
                        pe.matmul(q3[:, :, 0:P], identb[:, :], maskb[:, 1:2, :].to_broadcast([P, 2, P]),
                                  start=True, stop=False, skip_group_check=True)
                    last = pe.matmul(dst[:, :], k_t[:, p, 0:P], q_t[:, p, :, :].rearrange("p h q -> p (h q)"),
                                     start=n == 1, stop=n == 1, skip_group_check=True)
                    if n == 0:
                        for j in range(2):
                            last = pe.matmul(q3[:, j, :], selb[:, 2 * p + j, :], max_t[:, :], start=False,
                                             stop=j == 1, skip_group_check=True)
                else:
                    q4 = dst[:, :].rearrange("p (h q) -> p h q", h=4)
                    if n == 0:
                        pe.matmul(q4, identb[:, :], maskb[:, 1:2, :].to_broadcast([P, 4, P]),
                                  start=True, stop=False, skip_group_check=True)
                    for j in range(2):
                        last = pe.matmul(q4[:, 2 * j:2 * j + 2, :], k_t[:, 2 * g + j, P:T],
                                         q_t[:, 2 * g + j, :, P:T], start=n == 1, stop=n == 1,
                                         skip_group_check=True)
                    if n == 0:
                        for j in range(4):
                            last = pe.matmul(q4[:, j, :], selb[:, 4 * g + j, :], max_t[:, P:T], start=False,
                                             stop=j == 3, skip_group_check=True)
                last.then_inc(score_done[n].sem, 1)
                if r == 2 and g >= 1:
                    pe_values(pe, i, n, g - 1)
            pe_values(pe, i, n, 3)
            for t in range(NT):
                pe.wait_ge(*pv_copied[n](i, 2))
                for g in range(4):
                    last = pe.transpose(SCORE[t][:, g * P:(g + 1) * P], y_t[:, g, t * P:(t + 1) * P], identf[:, :])
                last.then_inc(y_back[n].sem, 1)
            pe.wait_ge(*y_ready[n](i, 1))
            for t in range(NT):
                last = pe.transpose(BMISC[:, t * P:(t + 1) * P], y_n[:, t, :], identf[:, :])
            last.then_inc(yt_done[n].sem, 1)
            pe.wait_ge(*yt_copied[n](i, 1))
            for t in range(NT):
                last = pe.matmul(BPV[:, t * P:(t + 1) * P], y_nt[:, t * P:(t + 1) * P], w_o[n][:, :],
                                 start=True, stop=True)
            last.then_inc(attn_out[n].sem, 1)

        def pe_maxima(pe, i):
            for u in range(NU):
                dst = SCORE[u % 3]
                if u >= 3:
                    pe.wait_ge(*max_taken(i, u - 2))
                if u < 8:
                    k3 = dst[:, :].rearrange("p (h k) -> p h k", h=2)
                    pe.matmul(k3[:, :, P:T], identb[:, :], maskb[:, 0:1, :].to_broadcast([P, 2, P]),
                              start=True, stop=False, skip_group_check=True)
                    for j in range(2):
                        last = pe.matmul(k3[:, j, :], q_t[:, u, j, P:T], k_t[:, u, :], start=False,
                                         stop=j == 1, skip_group_check=True)
                else:
                    k4 = dst[:, :].rearrange("p (h k) -> p h k", h=4)
                    pe.matmul(k4, identb[:, :], maskb[:, 0:1, :].to_broadcast([P, 4, P]),
                              start=True, stop=False, skip_group_check=True)
                    for j in range(4):
                        g = 2 * (u - 8) + j // 2
                        last = pe.matmul(k4[:, j, :], q_t[:, g, j % 2, 0:P], k_t[:, g, 0:P], start=False,
                                         stop=j == 3, skip_group_check=True)
                last.then_inc(maxscore_done.sem, 1)
            pe.wait_ge(*max_stacked(i, 1))
            for t in range(NT):
                last = pe.transpose(BMISC[:, t * 64:(t + 1) * 64].bitcast(BF16), max_stack[:, t, :], identb[:, :])
            last.then_inc(max_turned.sem, 1)
            pe.wait_ge(*max_ready(i, 1))

        def pe_values(pe, i, n, g):
            pe.wait_ge(*probs_ready[n](i, 3 * g + 3))
            half = (BPV, BMISC)[g // 2][:, (g % 2) * T:(g % 2 + 1) * T]
            for j in range(4):
                pe.matmul(half[VW * j:VW * (j + 1), :], v_aug[:, 0, 4 * g + j, :],
                          probs[:, 3 * g + j // 2, (j % 2) * T:(j % 2 + 1) * T],
                          start=True, stop=False, skip_group_check=True)
                last = pe.matmul(half[VW * j:VW * (j + 1), P:T], v_aug[:, 1, 4 * g + j, :],
                                 probs[:, 3 * g + 2, j * P:(j + 1) * P],
                                 start=False, stop=True, skip_group_check=True)
            if g % 2:
                last.then_inc(pv_done[n].sem, 1)

        def pe_moe(pe, i):
            pe_turn(pe, i, "mix", BOUT)
            pe.wait_ge(*h_ready["mix"](i, 1))
            for t in range(NT):
                last = pe.matmul(GU[0][:, t * P:(t + 1) * P], h_t[:, t * P:(t + 1) * P], w_mix[:, :],
                                 start=True, stop=True)
            last.then_inc(mix_done.sem, 1)
            pe_turn(pe, i, "moe", BOUT)
            pe.wait_ge(*h_ready["moe"](i, 1))
            for t in range(NT):
                last = pe.matmul(GU[1][:, t * NE:(t + 1) * NE], tt[:, t * P:(t + 1) * P], w_gate[:, :],
                                 start=True, stop=True)
            last.then_inc(logits_done.sem, 1)
            pe.wait_ge(*parts_moe(i, 1))
            for c in range(NCH):
                if c == 1:
                    pe.wait_ge(*gap_ready(i, 1))
                if c >= 2:
                    pe.wait_ge(*hidden_ready(i, c - 1))
                for n in range(2):
                    dst = GU[c % 2][:, n * T:(n + 1) * T]
                    pe.matmul(dst, gu_hi[:, n, c, :], tt_hi[:, :], start=True, stop=False, skip_group_check=True)
                    pe.matmul(dst, gu_hi[:, n, c, :], tt_lo[:, :], start=False, stop=False, skip_group_check=True)
                    last = pe.matmul(dst, gu_lo[:, n, c, :], tt_hi[:, :], start=False, stop=True,
                                     skip_group_check=True)
                last.then_inc(gu_done.sem, 1)
                if c >= 1:
                    pe_down(pe, i, c - 1)
            pe_down(pe, i, NCH - 1)

        def pe_down(pe, i, c):
            e, k = divmod(c, CH)
            pe.wait_ge(*hidden_ready(i, c + 1))
            if k == 0 and e >= 1:
                pe.wait_ge(*expert_added(i, e))
            for t in range(NT):
                last = pe.matmul(BOUT[:, t * P:(t + 1) * P], hidden[:, c % 2, t * P:(t + 1) * P],
                                 w_down[:, c, :], start=k == 0 and t == 0, stop=k == CH - 1 and t == 1,
                                 skip_group_check=True)
            if k == CH - 1:
                last.then_inc(expert_done.sem, 1)

        def pe_ffn1(pe, i):
            pe_turn(pe, i, "d", BMISC)
            pe.wait_ge(*h_ready["d"](i, 1))
            for t in range(NT):
                last = pe.matmul(BPV[:, t * T:t * T + P + PROJ + RTOT], h_t[:, t * P:(t + 1) * P], w_ffn1[:, :],
                                 start=t == 0, stop=False, skip_group_check=True)
            last.then_inc(ffn1_done.sem, 1)
            pe.wait_ge(*pj_ready(i, 1))
            for t in range(NT):
                last = pe.transpose(BMISC[0:PROJ, t * P:(t + 1) * P], pj[:, t, :], identf[:, :])
            last.then_inc(pjt_done.sem, 1)
            pe.wait_ge(*pjt_ready(i, 1))
            for t in range(NT):
                last = pe.matmul(BMISC[:, T + t * NR:T + (t + 1) * NR], pj_t[:, t * P:(t + 1) * P], simn[:, :],
                                 start=True, stop=True)
            last.then_inc(lg4_done.sem, 1)
            pe.wait_ge(*dr_ready(i, 1))
            for t in range(NT):
                last = pe.transpose(BMISC[0:RTOT, t * P:(t + 1) * P], dr[:, t, :], identf[:, :])
            last.then_inc(drt_done.sem, 1)
            pe.wait_ge(*drt_ready(i, 1))
            for t in range(NT):
                last = pe.matmul(BPV[:, t * T:t * T + P], dr_t[:, t * P:(t + 1) * P], w_up1[:, :],
                                 start=False, stop=t == 1, skip_group_check=True)
            last.then_inc(ffn1_out.sem, 1)


        @block.tensor
        def _(pe):
            pe.wait_ge(prep["silu"], 1)
            for l in range(2):
                for m in range(6):
                    last = pe.matmul(bank[0][:, (l * 6 + m) * B:(l * 6 + m + 1) * B],
                                     wmod[:, l, m * P:(m + 1) * P], silu_c[:, l, :], start=True, stop=True)
            last.then_inc(prep["modcols_pe"], 1)
            for l in range(2):
                pe.matmul(bank[1 + 2 * l][0:B, 0:512], silu_c[:, l, :], wmod[:, l, 0:512], start=True, stop=True)
                last = pe.matmul(bank[2 + 2 * l][0:B, 0:256], silu_c[:, l, :], wmod[:, l, 512:768],
                                 start=True, stop=True)
            last.then_inc(prep["modrows_pe"], 1)
            pe.wait_ge(loads["attn"], 32)
            pe.wait_ge(prep["u2"], 1)
            for n in range(3):
                for g in range(NPAIR):
                    last = pe.matmul(bank[5 + n][:, g * 24:(g + 1) * 24], wd3[:, n, g, :],
                                     u2[:, n, :, :].rearrange("p h d -> p (h d)"), start=True, stop=True)
            last.then_inc(prep["weff_pe"], 1)
            pe.wait_ge(loads["const"], 80)
            pe.wait_ge(prep["simt"], 1)
            pe.wait_ge(prep["modcols"], 1)
            pe.transpose(bank[0][0:PROJ, 0:NR], simt[:, :], identf[0:NR, 0:NR]).then_inc(prep["simn_pe"], 1)
            pe.wait_ge(loads["ffn"], 11 * 16)
            pe.wait_ge(prep["lo"], NQ)
            pe.wait_ge(prep["hi"], NQ)
            with pe.Fori(0, B) as i:
                pe_attention(pe, i, 0)
                pe_moe(pe, i)
                pe_attention(pe, i, 1)
                pe_ffn1(pe, i)

        def dve_norm(dve, i, s, src, chain):
            for t in range(NT):
                last = dve.bn_stats(stats[:, t, :], src[:, t, :])
            chain(last)
            dve.sem_inc(passed["dve"], 1)
            for t in range(NT):
                last = dve.bn_aggr(meanvar[:, t, :], stats[:, t, :])
            last.then_inc(var_ready[s].sem, 1)
            dve.wait_ge(*rstd_ready[s](i, 1))
            for t in range(NT):
                last = dve.tensor_scalar(xn[:, t, :], src[:, t, :], meanvar[:, t, 0:1], rstd[:, t:t + 1],
                                         ALU.subtract, ALU.mult)
            last.then_inc(xn_ready[s].sem, 1)

        def rank_of(dve, chain, values, n, earlier):
            ca, cb = cmp_a[:, :, 0:n * n], cmp_b[:, :, 0:n * n]
            other = values.unsqueeze(2).to_broadcast([P, NT, n, n])
            own = values.unsqueeze(3).to_broadcast([P, NT, n, n])
            grid = dict(e=n)
            dve.tensor_tensor(ca.rearrange("p t (e j) -> p t e j", **grid), other, own, ALU.is_gt)
            chain(dve.tensor_tensor(cb.rearrange("p t (e j) -> p t e j", **grid), other, own, ALU.is_ge))
            chain(dve.tensor_tensor(cb, cb, ca, ALU.subtract))
            chain(dve.tensor_tensor(cb, cb, earlier[:, :].unsqueeze(1).to_broadcast([P, NT, n * n]), ALU.mult))
            chain(dve.tensor_tensor(ca, ca, cb, ALU.add))
            chain(dve.tensor_reduce(rank[:, :, 0:n], ca.rearrange("p t (e j) -> p t e j", **grid), AX.X, ALU.add))

        def dve_attention(dve, i, n):
            chain = Chain(dve, dve_self["ac"[n]], i)
            src = (x_in, x_b)[n]
            if n == 0:
                dve.wait_ge(*x_loaded(i, 16))
            else:
                dve.wait_ge(*x_b_ready(i, 1))
            dve_norm(dve, i, "ac"[n], src, chain)
            dve.wait_ge(*qkv_copied[n](i, NT))
            qk = raw[:, :, 0:256].rearrange("p t (h d) -> p t h d", d=D)
            if n == 0:
                e = qk[:, :, :, DE:D]
                cos, sin = (rope[:, k, :, :].unsqueeze(2).to_broadcast([P, NT, 2 * H, DE]) for k in range(2))
                dve.tensor_tensor(rot[:, :, :, :], raw[:, :, 384:512].rearrange("p t (h d) -> p t h d", d=DE),
                                  sin, ALU.mult)
                chain(dve.tensor_tensor(e, e, cos, ALU.mult))
                chain(dve.tensor_tensor(e, e, rot[:, :, :, :], ALU.add))
            st = stack[n]
            p1, p2 = st[:, :, :, 0:D], st[:, :, :, D:2 * D]
            chain(dve.tensor_copy(p1, qk))
            chain(dve.tensor_tensor(resid[:, :, :, :], qk, p1, ALU.subtract))
            dve.tensor_copy(p2, resid[:, :, :, :]).then_inc(parts_ready[n].sem, 1)
            dve.wait_ge(*parts_ready[n](i, 1))
            chain(dve.tensor_tensor(resid[:, :, :, :], resid[:, :, :, :], p2, ALU.subtract))
            dve.tensor_copy(st[:, :, 0:H, 5 * D:6 * D], resid[:, :, 0:H, :])
            dve.tensor_copy(st[:, :, H:2 * H, 4 * D:5 * D], resid[:, :, H:2 * H, :])\
               .then_inc(thirds_ready[n].sem, 1)
            for t in range(NT):
                dve.wait_ge(*spread_done[n](i, 2 * t + 2))
                src_q = SCORE[(3 + 2 * t) % 3][:, :].bitcast(BF16).rearrange("p (g q) -> p g q", g=NPAIR)
                for j in range(2):
                    rows = slice(ROWS * j, ROWS * (j + 1))
                    last = dve.tensor_copy(q_t[rows, :, j, t * P:(t + 1) * P], src_q[rows, :, :])
                last.then_inc(q_spread[n].sem, 1)
            if n == 0:
                for u in range(NU):
                    dve.wait_ge(*maxscore_done(i, u + 1))
                    if u < 8:
                        dst, heads = negmax[:, 1, 2 * u:2 * u + 2], 2
                    else:
                        dst, heads = negmax[:, 0, 4 * (u - 8):4 * (u - 7)], 4
                    dve.tensor_reduce(dst, SCORE[u % 3][:, :].rearrange("p (h k) -> p h k", h=heads),
                                      AX.X, ALU.max, negate=True).then_inc(max_taken.sem, 1)
                dve.wait_ge(*max_taken(i, NU))
                chain(dve.tensor_copy(max_stack[:, :, 0:H], negmax[:, :, :]))
                chain(dve.tensor_tensor(negmax_r[:, :, :], negmax[:, :, :], max_stack[:, :, 0:H], ALU.subtract))
                dve.tensor_copy(max_stack[:, :, H:2 * H], negmax_r[:, :, :]).then_inc(max_stacked.sem, 1)
            else:
                for u in range(NU):
                    dve.wait_ge(*rooted(i, u + 1))
                    dve.tensor_tensor(probs[:, u, :], SCORE[u % 3][:, :], ratio[:, u % 3, :], ALU.mult)\
                       .then_inc(ratio_done.sem, 1)
            for k in range(2):
                dve.wait_ge(*pv_done[n](i, k + 1))
                dve.tensor_copy(y_t[:, 2 * k:2 * k + 2, :].rearrange("p g q -> p (g q)"),
                                (BPV, BMISC)[k][:, :]).then_inc(pv_copied[n].sem, 1)
            for t in range(NT):
                dve.wait_ge(*y_back[n](i, t + 1))
                by_head = SCORE[t][:, :].rearrange("p (h v) -> p h v", v=VW)
                if n == 0:
                    chain(dve.reciprocal(den[:, t, :], by_head[:, :, D]))
                else:
                    chain(dve.tensor_scalar(den[:, t, :], by_head[:, :, D], 2 * EPS_RATIONAL, None, ALU.add))
                    chain(dve.reciprocal(den[:, t, :], den[:, t, :]))
                last = dve.tensor_tensor(y_n[:, t, :].rearrange("p (h d) -> p h d", d=D), by_head[:, :, 0:D],
                                         den[:, t, :].unsqueeze(2).to_broadcast([P, H, D]), ALU.mult)
            last.then_inc(y_ready[n].sem, 1)
            gate = (rows_a, rows_c)[n]
            dve.wait_ge(*(rows_a_loaded, rows_c_loaded)[n](i, 16))
            dve.wait_ge(*attn_out[n](i, 1))
            chain(dve.tensor_tensor(tmp[:, :, :], BPV[:, 0:T].rearrange("p (t c) -> p t c", t=NT),
                                    gate[:, 0:1, :].to_broadcast([P, NT, P]), ALU.mult))
            dve.tensor_tensor(x_mid[n][:, :, :], tmp[:, :, :], src[:, :, :], ALU.add)\
               .then_inc(x_mid_ready[n].sem, 1)
            chain.done()

        def dve_moe(dve, i):
            chain = Chain(dve, dve_self["b"], i)
            dve.wait_ge(*x_mid_ready[0](i, 1))
            dve_norm(dve, i, "b", x_mid[0], chain)
            dve.wait_ge(*xn_ready["b"](i, 1))
            dve.wait_ge(*rows_b_loaded(i, 16))
            chain(dve.tensor_tensor(h_ffn[:, :, :], xn[:, :, :], rows_b[:, 2:3, :].to_broadcast([P, NT, P]), ALU.mult))
            chain(dve.tensor_tensor(h_ffn[:, :, :], h_ffn[:, :, :], rows_b[:, 1:2, :].to_broadcast([P, NT, P]),
                                    ALU.add))
            dve_norm(dve, i, "mix", h_ffn, chain)
            dve.wait_ge(*mix_done(i, 1))
            chain(dve.tensor_tensor(h2[:, :, :], GU[0][:, 0:T].rearrange("p (t c) -> p t c", t=NT),
                                    h_ffn[:, :, :], ALU.add))
            dve_norm(dve, i, "moe", h2, chain)
            dve.wait_ge(*h_ready["moe"](i, 1))
            chain(dve.tensor_copy(tt_hi[:, :], tt[:, :]))
            dve.tensor_tensor(tt_lo[:, :], tt[:, :], tt_hi[:, :].bitcast(F32), ALU.subtract)\
               .then_inc(parts_moe.sem, 1)
            dve.wait_ge(*logits_done(i, 1))
            chain(dve.tensor_copy(logit[:, :, :], GU[1][:, 0:NT * NE].rearrange("p (t e) -> p t e", t=NT)))
            rank_of(dve, chain, logit[:, :, :], NE, before)
            dve.tensor_scalar(first[:, :, :], rank[:, :, :], 0.0, None, ALU.is_equal)
            chain(dve.tensor_scalar(second[:, :, :], rank[:, :, :], 1.0, None, ALU.is_equal))
            dve.tensor_tensor(comb[:, :, :], first[:, :, :], second[:, :, :], ALU.add)
            chain(dve.tensor_tensor(first[:, :, :], first[:, :, :], second[:, :, :], ALU.subtract))
            chain(dve.tensor_tensor(second[:, :, :], first[:, :, :], logit[:, :, :], ALU.mult))
            dve.tensor_reduce(gap[:, :], second[:, :, :], AX.X, ALU.add).then_inc(gap_ready.sem, 1)
            dve.wait_ge(*tanh_ready(i, 1))
            chain(dve.tensor_tensor(first[:, :, :], first[:, :, :],
                                    tgap[:, :].unsqueeze(2).to_broadcast([P, NT, NE]), ALU.mult))
            chain(dve.tensor_tensor(comb[:, :, :], comb[:, :, :], first[:, :, :], ALU.add))
            chain(dve.tensor_scalar(comb[:, :, :], comb[:, :, :], 0.5, None, ALU.mult))
            for c in range(NCH):
                dve.wait_ge(*silu_done(i, c + 1))
                dve.tensor_tensor(hidden[:, c % 2, :], GU[c % 2][:, T:2 * T], silu_g[:, c % 2, :], ALU.mult)\
                   .then_inc(hidden_ready.sem, 1)
                if c % CH == 0 and c >= CH:
                    dve_expert(dve, i, c // CH - 1)
            dve_expert(dve, i, NE - 1)
            dve.wait_ge(*expert_added(i, NE))
            chain(dve.tensor_tensor(tmp[:, :, :], acc[:, :, :], rows_b[:, 0:1, :].to_broadcast([P, NT, P]), ALU.mult))
            dve.tensor_tensor(x_b[:, :, :], tmp[:, :, :], x_mid[0][:, :, :], ALU.add).then_inc(x_b_ready.sem, 1)
            chain.done()

        def dve_expert(dve, i, e):
            dve.wait_ge(*expert_done(i, e + 1))
            if e >= 1:
                dve.wait_ge(*expert_added(i, e))
            for t in range(NT):
                last = dve.scalar_tensor_tensor(out=acc[:, t, :], in0=BOUT[:, t * P:(t + 1) * P],
                                                scalar=comb[:, t, e:e + 1],
                                                in1=(h2 if e == 0 else acc)[:, t, :], op0=ALU.mult, op1=ALU.add)
            last.then_inc(expert_added.sem, 1)

        def dve_ffn1(dve, i):
            chain = Chain(dve, dve_self["d"], i)
            dve.wait_ge(*x_mid_ready[1](i, 1))
            dve_norm(dve, i, "d", x_mid[1], chain)
            dve.wait_ge(*ffn1_done(i, 1))
            both = BPV[:, :].rearrange("p (t c) -> p t c", t=NT)
            dve.tensor_tensor(pj[:, :, :], both[:, :, P:P + PROJ],
                              bp_row[:, :].unsqueeze(1).to_broadcast([P, NT, PROJ]), ALU.add)\
               .then_inc(pj_ready.sem, 1)
            dve.wait_ge(*pj_ready(i, 1))
            chain(dve.tensor_tensor(pjsq[:, :, :], pj[:, :, :], pj[:, :, :], ALU.mult))
            chain(dve.tensor_reduce(pj_ss[:, :], pjsq[:, :, :], AX.X, ALU.add))
            dve.tensor_scalar(pj_ss[:, :], pj_ss[:, :], 1e-24, None, ALU.max).then_inc(pjss_ready.sem, 1)
            dve.wait_ge(*pjinv_ready(i, 1))
            dve.wait_ge(*lg4_done(i, 1))
            chain(dve.tensor_tensor(lg4[:, :, :], BMISC[:, T:T + NT * NR].rearrange("p (t e) -> p t e", t=NT),
                                    pj_inv[:, :].unsqueeze(2).to_broadcast([P, NT, NR]), ALU.mult))
            chain(dve.tensor_reduce(st4[:, 0, :], lg4[:, :, :], AX.X, ALU.max))
            dve.tensor_tensor(lg4[:, :, :], lg4[:, :, :], st4[:, 0, :].unsqueeze(2).to_broadcast([P, NT, NR]),
                              ALU.subtract).then_inc(lg4_shifted.sem, 1)
            dve.wait_ge(*lg4_shifted(i, 1))
            rank_of(dve, chain, lg4[:, :, :], NR, before4)
            dve.tensor_scalar(ret[:, :, :], rank[:, :, 0:NR], 0.0, None, ALU.is_equal)
            dve.wait_ge(*exp4_ready(i, 1))
            chain(dve.tensor_reduce(st4[:, 1, :], ex4[:, :, :], AX.X, ALU.add))
            chain(dve.reciprocal(st4[:, 2, :], st4[:, 1, :]))
            chain(dve.tensor_tensor(ret[:, :, :], ret[:, :, :], ex4[:, :, :], ALU.mult))
            chain(dve.tensor_tensor(ret[:, :, :], ret[:, :, :],
                                    st4[:, 2, :].unsqueeze(2).to_broadcast([P, NT, NR]), ALU.mult))
            at = 0
            for k, r in enumerate(RANKS):
                last = dve.tensor_tensor(dr[:, :, at:at + r], both[:, :, P + PROJ + at:P + PROJ + at + r],
                                         ret[:, :, k:k + 1].to_broadcast([P, NT, r]), ALU.mult)
                at += r
            last.then_inc(dr_ready.sem, 1)
            dve.wait_ge(*ffn1_out(i, 1))
            chain(dve.tensor_tensor(tmp[:, :, :], both[:, :, 0:P], rows_c[:, 1:2, :].to_broadcast([P, NT, P]),
                                    ALU.mult))
            dve.wait_ge(*x_stored.before(i, 16))
            dve.tensor_tensor(x_out[:, :, :], tmp[:, :, :], x_mid[1][:, :, :], ALU.add)\
               .then_inc(x_out_ready.sem, 1)
            chain.done()

        @block.vector
        def _(dve):
            steps = [0]

            def step(ins):
                steps[0] += 1
                ins.then_inc(prep["dve"], 1)
                dve.wait_ge(prep["dve"], steps[0])

            for user in (x_mid_ready[0], x_b_ready, x_out_ready):
                dve.sem_inc(user.sem, 1)
            dve.wait_ge(loads["small"], 80)
            dve.tensor_scalar(simst[:, 1:2], tempc[:, :], CLAMP_MAX, None, ALU.min).then_inc(prep["temp"], 1)
            step(dve.tensor_tensor(simsq[:, :], simt[:, :], simt[:, :], ALU.mult))
            step(dve.tensor_reduce(simst[:, 0:1], simsq[:, :], AX.X, ALU.add))
            dve.tensor_scalar(simst[:, 0:1], simst[:, 0:1], 1e-24, None, ALU.max).then_inc(prep["simss"], 1)
            dve.wait_ge(loads["attn"], 32)
            uq = u2[:, 0:2, :, :].rearrange("p n h d -> p (n h) d")
            dve.tensor_scalar(uq[:, :, 8:12:2], uq[:, :, 5:8:2], -1.0, None, ALU.mult)
            dve.tensor_copy(uq[:, :, 9:12:2], uq[:, :, 4:8:2]).then_inc(prep["u2"], 1)
            dve.wait_ge(prep["modcols_pe"], 1)
            cols = modcols[:, :, :, :].rearrange("p b l m -> p (l m) b")
            step(dve.tensor_copy(cols, bank[0][:, 0:12 * B].rearrange("p (m b) -> p m b", b=B)))
            ones = modcols[:, :, :, :].rearrange("p b l m -> p (b l) m")[:, :, 1:5:3]
            dve.tensor_scalar(ones, ones, 1.0, None, ALU.add).then_inc(prep["modcols"], 1)
            dve.wait_ge(prep["modrows_pe"], 1)
            for l in range(2):
                dve.tensor_copy(modrow[:, l, 0:4, :].rearrange("b m c -> b (m c)"), bank[1 + 2 * l][0:B, :])
                last = dve.tensor_copy(modrow[:, l, 4:6, :].rearrange("b m c -> b (m c)"),
                                       bank[2 + 2 * l][0:B, 0:256])
            step(last)
            gates = modrow[:, :, 2:6:3, :]
            step(dve.tensor_scalar(gate_s[:, :, :, :], gates, 0.0, 2.0, ALU.is_ge, ALU.mult))
            dve.tensor_scalar(gate_s[:, :, :, :], gate_s[:, :, :, :], -1.0, None, ALU.add)
            for l in range(2):
                last = dve.scalar_tensor_tensor(out=gate_m[:, l, :, :], in0=gates[:, l, :, :], scalar=-1.0,
                                                in1=gates[:, l, :, :], op0=ALU.mult, op1=ALU.max)
            step(last)
            step(dve.tensor_scalar(gate_m[:, :, :, :], gate_m[:, :, :, :], 0.25, None, ALU.max))
            for l in range(2):
                dve.tensor_tensor(rowmods[:, 4 * l:4 * l + 2, :], gate_s[:, l, :, :], gate_m[:, l, :, :], ALU.mult)
            dve.tensor_copy(rowmods[:, 2, :], modrow[:, 0, 3, :])
            dve.tensor_scalar(rowmods[:, 3, :], modrow[:, 0, 4, :], 1.0, None, ALU.add).then_inc(prep["rows"], 1)
            dve.wait_ge(prep["weff_pe"], 1)
            for n in range(3):
                src = bank[5 + n][:, 0:192].rearrange("p (h d) -> p h d", d=12)
                last = dve.tensor_copy(w_qkv0[:, n * P:(n + 1) * P].rearrange("p (h d) -> p h d", d=D),
                                       src[:, :, 0:D])
                if n < 2:
                    last = dve.tensor_copy(w_qkv0[:, 384 + 64 * n:448 + 64 * n]
                                           .rearrange("p (h d) -> p h d", d=DE), src[:, :, D:12])
            last.then_inc(prep["wqkv0"], 1)
            dve.tensor_scalar(w_qkv1[:, 0:P], w_qkv1[:, 0:P], SCALE, None, ALU.mult).then_inc(prep["wqkv1"], 1)
            for k in range(3):
                step(dve.tensor_copy(slope_p[:, k, :], (slope if k == 0 else slope_r)[:, :]))
                if k < 2:
                    step(dve.tensor_tensor(slope_r[:, :], (slope if k == 0 else slope_r)[:, :],
                                           slope_p[:, k, :], ALU.subtract))
            dve.wait_ge(prep["cleared"], 1)
            parts = slope_p[:, :, :].rearrange("p k h -> p h k")
            for t in range(NT):
                q, k = stack[1][:, t, 0:H, :], stack[1][:, t, H:2 * H, :]
                pos = position[:, t:t + 1].unsqueeze(2).to_broadcast([P, H, 3])
                dve.tensor_scalar(q[:, :, ALIBI:ALIBI + 3], pos, -1.0, None, ALU.mult)
                dve.tensor_copy(q[:, :, ALIBI + 3:ALIBI + 6], parts)
                dve.tensor_copy(k[:, :, ALIBI:ALIBI + 3], parts)
                last = dve.tensor_copy(k[:, :, ALIBI + 3:ALIBI + 6], pos)
            last.then_inc(prep["stack1"], 1)
            dve.wait_ge(prep["siminv"], 1)
            dve.wait_ge(prep["exptemp"], 1)
            dve.tensor_scalar(simt[:, :], simt[:, :], simst[:, 3:4], simst[:, 2:3], ALU.mult, ALU.mult)\
                .then_inc(prep["simt"], 1)
            dve.wait_ge(prep["simn_pe"], 1)
            dve.tensor_copy(simn[:, :], bank[0][0:PROJ, 0:NR]).then_inc(prep["simn"], 1)
            piece = NCH // NQ
            for k in range(NQ):
                dve.wait_ge(prep["hi"], k + 1)
                rows = slice(k * piece, (k + 1) * piece)
                for n in range(2):
                    last = dve.tensor_tensor(gu_lo[:, n, rows, :], stage[:, k % 2, n, :, :],
                                             gu_hi[:, n, rows, :].bitcast(F32), ALU.subtract)
                last.then_inc(prep["lo"], 1)
            dve.wait_ge(loads["const"], 80)
            dve.wait_ge(loads["ffn"], 11 * 16)
            with dve.Fori(0, B) as i:
                dve_attention(dve, i, 0)
                dve_moe(dve, i)
                dve_attention(dve, i, 1)
                dve_ffn1(dve, i)


def constants():
    def bf(x):
        return (np.ascontiguousarray(x, np.float32).view(np.uint32) >> 16).astype(np.uint16)

    r = np.arange(P)
    mask = np.zeros((P, 2, P), np.float32)
    mask[:, 0] = np.where(r[None, :] > r[:, None], MASKED, 0)
    mask[:, 1] = np.where(r[:, None] > r[None, :], MASKED, 0)
    sel = np.zeros((P, H, P), np.float32)
    for h in range(H):
        sel[[h, H + h], h] = 1
    inv = (1.0 / np.float32(10000.0) ** (np.arange(0, DE, 2, dtype=np.float32) / np.float32(DE))).astype(np.float32)
    f = np.arange(T, dtype=np.float32)[:, None] * inv[None, :]
    f = np.concatenate([f, f], -1).astype(np.float32)
    rope = np.stack([np.cos(f), np.sin(f)]).astype(np.float32).reshape(2, NT, P, DE).transpose(2, 0, 1, 3)
    tri = [np.broadcast_to((np.arange(n)[None, :] < np.arange(n)[:, None]).astype(np.float32).reshape(1, -1),
                           (P, n * n)) for n in (NE, NR)]
    return {"identf": np.eye(P, dtype=np.float32), "identb": bf(np.eye(P)), "maskb": bf(mask),
            "selb": bf(sel), "rope": rope, "before": tri[0], "before4": tri[1],
            "position": (np.arange(T, dtype=np.float32) - P).reshape(NT, P).T}


def kernel(**inputs):
    import concourse.bacc as bacc
    from concourse.bass_utils import run_bass_kernel_spmd

    w = {k: np.asarray(v) for k, v in inputs.items()}
    arrays = dict(constants())
    for l in range(2):
        arrays[f"L{l}_c"] = w[f"L{l}_c"].T
        arrays[f"L{l}_wmod"] = w[f"L{l}_wmod"]
    u2 = np.zeros((P, 3, 2, 12), np.float32)
    for n, parts in enumerate((("Wq_up_c", "Wq_up_e"), ("Wk_up_c", "Wk_up_e"), ("Wv_up",))):
        up = np.concatenate([w["L0_attn_" + p] for p in parts], 1)
        for h in range(2):
            u2[L * h:L * (h + 1), n, h, 0:D] = up
    arrays["u2"] = u2
    arrays["wd3"] = np.stack([w[f"L0_attn_W{x}_down"].reshape(P, NPAIR, 2 * L).transpose(2, 1, 0)
                              for x in "qkv"], 1)
    arrays["L0_attn_Wc"] = w["L0_attn_Wc"]
    arrays["L0_attn_x"] = w["L0_attn_x"]
    for name in ("L1_attn_w_qkv", "L1_attn_w_out", "L0_ffn_attn_w", "L0_ffn_gate_w", "L1_ffn_sim"):
        arrays[name] = w[name].T
    arrays["L1_attn_alibi_slopes"] = w["L1_attn_alibi_slopes"]
    arrays["L1_ffn_temp"] = w["L1_ffn_temp"]
    arrays["L1_ffn_bp"] = w["L1_ffn_bp"]
    arrays["lncol"] = np.stack([w["L0_ffn_" + k] for k in ("ln1_g", "ln1_b", "ln2_g", "ln2_b")], 1)
    arrays["gu"] = np.stack([w[f"L0_ffn_{k}_proj"].reshape(NCH * P, P).T.reshape(P, NCH, P)
                             for k in ("gate", "up")], 1)
    arrays["L0_ffn_down_proj"] = w["L0_ffn_down_proj"].reshape(NE, P, CH, P).transpose(3, 0, 2, 1)        .reshape(P, NCH, P)
    arrays["w_ffn1"] = np.concatenate([w["L1_ffn_W"].T, w["L1_ffn_Wp"].T]
                                      + [w[f"L1_ffn_Wd{k}"].T for k in range(NR)], 1)
    arrays["w_up1"] = np.concatenate([w[f"L1_ffn_Wu{k}"].T for k in range(NR)], 0)

    nc = bacc.Bacc("TRN2", target_bir_lowering=False, num_devices=1)
    fed, aps = {}, {}
    for name, x in arrays.items():
        x = np.ascontiguousarray(x)
        fed["in_" + name] = x
        aps[name] = nc.dram_tensor("in_" + name, x.shape, mybir.dt.from_np(x.dtype), kind="ExternalInput").ap()
    aps["scratch"] = nc.dram_tensor("scratch", (B, ROWMODS, P), F32, kind="Internal").ap()
    out = nc.dram_tensor("out_0", (B, T, P), F32, kind="ExternalOutput").ap()
    build(nc, aps, out)
    return run_bass_kernel_spmd(nc, [fed], core_ids=[0]).results[0]["out_0"]
```

```python
import math
from contextlib import ExitStack

import numpy as np

import concourse.bass as bass
from concourse import mybir

F32 = mybir.dt.float32
F32R = mybir.dt.float32r
BF16 = mybir.dt.bfloat16
ALU = mybir.AluOpType
ACT = mybir.ActivationFunctionType
AX = mybir.AxisListType

P = 128
B, T = 16, 256
NT = T // P
H, D = 16, 8
DE = D // 2
L = 64
NPAIR = H // 2
ROWS = 64
SLOTS = 6
ALIBI = SLOTS * D
NE, NI = 8, 512
CH = NI // P
NCH = NE * CH
NQ = 16
NR = 4
RANKS = [1, 2, 4, 8]
RTOT = sum(RANKS)
PROJ = 32
SCALE = 1.0 / math.sqrt(D)
VW = 32
MASKED = -1e30
ROWMODS = 6
EPS_LN = 1e-5
EPS_RATIONAL = 1e-6
CLAMP_MAX = float(np.log(1.0 / 0.01))


class Signal:

    def __init__(self, ctx, nc, name, per, ahead):
        self.sem, self.per, self.ahead = ctx.enter_context(nc.semaphore(name)), per, ahead

    def __call__(self, i, n):
        base, plus = i
        return self.sem, base * self.per + (n + self.per * (self.ahead + plus))

    def before(self, i, n):
        base, plus = i
        assert self.ahead
        return self.sem, base * self.per + (n + self.per * (self.ahead + plus - 1))


class Chain:

    def __init__(self, eng, steps, i):
        self.eng, self.steps, self.i, self.n = eng, steps, i, 0

    def __call__(self, ins):
        self.n += 1
        ins.then_inc(self.steps.sem, 1)
        self.eng.wait_ge(*self.steps(self.i, self.n))

    def done(self):
        assert self.n == self.steps.per, (self.n, self.steps.per)


def interleave(*streams):
    due = [[next(steps), k, steps] for k, steps in enumerate(streams)]
    while due:
        nearest = min(due, key=lambda d: (d[0], d[1]))
        slot = next(nearest[2], None)
        if slot is None:
            due.remove(nearest)
        else:
            assert slot >= nearest[0], (slot, nearest[0])
            nearest[0] = slot


def chunk_at(c):
    at = 0.8 + 1.24 * c
    return at + 1.2 * (at > 12.9) + 1.2 * (at > 18.9)


def maximum_at(u):
    return 10 + 0.7 * u


def score_at(n, u):
    if n == 0:
        return 20 + 0.8 * u
    return (10, 11.5, 16, 17.5)[u // 3] + 0.5 * (u % 3)


def values_at(n, g):
    return score_at(0, 3 * g + 2) + 1.3 if n == 0 else (15.5, 17, 21, 22.3)[g]


ROOT_AT = (13.2, 19.4)
GATHER_AT = (30.6, 22.6)
TOWARDS_EXPERTS = 35
FFN1_AT = 26.6


def build(nc, a, out):
    with ExitStack() as ctx:
        def sb(name, shape, dt=F32):
            return ctx.enter_context(nc.sbuf_tensor(name, shape, dt))

        def sem(name):
            return ctx.enter_context(nc.semaphore(name))

        def signal(name, per=1, ahead=0):
            return Signal(ctx, nc, name, per, ahead)

        identf = sb("identf", [P, P])
        identb = sb("identb", [P, P], BF16)
        maskb = sb("maskb", [P, 2, P], BF16)
        selb = sb("selb", [P, H], BF16)
        rope = sb("rope", [P, 2, NT, DE])
        before = sb("before", [P, NE * NE])
        before4 = sb("before4", [P, NR * NR])
        position = sb("position", [P, NT])
        w_qkv0 = sb("w_qkv0", [P, 512])
        w_qkv1 = sb("w_qkv1", [P, 384])
        w_o = [sb("w_o0", [P, P]), sb("w_o1", [P, P])]
        w_mix = sb("w_mix", [P, P])
        w_gate = sb("w_gate", [P, NE])
        gu_hi = sb("gu_hi", [P, 2, NCH, P], F32R)
        gu_lo = sb("gu_lo", [P, 2, NCH, P], F32R)
        w_down = sb("w_down", [P, NCH, P])
        lncol = sb("lncol", [P, 4])
        w_ffn1 = sb("w_ffn1", [P, P + PROJ + RTOT])
        w_up1 = sb("w_up1", [RTOT, P])
        bp_row = sb("bp_row", [P, PROJ])
        simn = sb("simn", [PROJ, NR])
        modcols = sb("modcols", [P, B, 2, 6])
        minus_half = sb("minus_half", [P, NT])

        NU = 12
        RING = 6
        probs = [sb(f"probs{n}", [P, RING, 512]) for n in range(2)]
        ratio = sb("ratio", [P, RING, 512])

        wd3 = probs[0][:, :, :].rearrange("p u (g c) -> p (u g) c", c=P)\
            .rearrange("p (n g) c -> p n g c", n=3)
        stage = probs[1][:, 0:2, :].rearrange("p u (g c) -> p (u g) c", c=P)\
            .rearrange("p (k n g) c -> p k n g c", k=2, n=2)
        modrow = probs[1][0:B, 2:5, :].rearrange("b u (g c) -> b (u g) c", c=P)\
            .rearrange("b (l m) c -> b l m c", l=2)
        gate_s = probs[1][0:B, 5, :].rearrange("b (l m c) -> b l m c", l=2, c=P)
        wmod = ratio[:, 0:3, :].rearrange("p u (g c) -> p (u g) c", c=P)\
            .rearrange("p (l m) c -> p l (m c)", l=2)
        rowmods = ratio[0:B, 3:5, :].rearrange("b u (g c) -> b (u g) c", c=P)[:, 0:ROWMODS, :]
        gate_m = ratio[0:B, 5, :].rearrange("b (l m c) -> b l m c", l=2, c=P)
        u2 = sb("u2", [P, 3, 2, 12])
        c_t = sb("c_t", [P, 2, B])
        silu_c = sb("silu_c", [P, 2, B])
        slope = sb("slope", [P, H])
        slope_r = sb("slope_r", [P, H])
        slope_p = sb("slope_p", [P, 3, H], BF16)
        simt = sb("simt", [NR, PROJ])
        simsq = sb("simsq", [NR, PROJ])
        simst = sb("simst", [NR, 4])
        tempc = sb("tempc", [NR, 1])

        def two(name, shape, dt=F32):
            return [sb(f"{name}{n}", shape, dt) for n in range(2)]

        x_in = sb("x_in", [P, NT, P])
        x_mid = [sb("x_a", [P, NT, P]), sb("x_c", [P, NT, P])]
        x_keep = sb("x_keep", [P, NT, P])
        x_b = sb("x_b", [P, NT, P])
        x_out = sb("x_out", [P, NT, P])
        rows_a = sb("rows_a", [P, 1, P])
        rows_g = sb("rows_g", [P, 1, P])
        rows_b = sb("rows_b", [P, 2, P])
        rows_c = sb("rows_c", [P, 2, P])
        cols_now = two("cols_now", [P, 6])
        stats = two("stats", [P, NT, 6])
        meanvar = two("meanvar", [P, NT, 2])
        vareps = two("vareps", [P, NT])
        rstd = two("rstd", [P, NT])
        xn = two("xn", [P, NT, P])
        h_t = two("h_t", [P, T])
        y_n = [h_t[n][:, :].rearrange("p (t c) -> p t c", t=NT) for n in range(2)]
        raw = two("raw", [P, NT, 512])
        y_t = [raw[n][:, :, :].rearrange("p t (g c) -> p (t g) c", g=2) for n in range(2)]
        rot = sb("rot", [P, NT, 2 * H, DE])
        v_aug = two("v_aug", [P, NT, H, D + 1])
        stack = two("stack", [P, NT, 2 * H, ROWS], BF16)
        q_t = two("q_t", [P, NPAIR, 2, T], BF16)
        k_t = two("k_t", [P, NPAIR, T], BF16)
        negmax = sb("negmax", [P, NT, H])
        negmax_r = sb("negmax_r", [P, NT, H])
        max_stack = sb("max_stack", [P, NT, P], BF16)
        max_t = sb("max_t", [P, T], BF16)
        den = two("den", [P, NT, H])
        y_nt = two("y_nt", [P, T])
        h_ffn = y_nt[0][:, :].rearrange("p (t c) -> p t c", t=NT)
        h2 = sb("h2", [P, NT, P])
        tt = rot[:, :, :, :].rearrange("p t h d -> p (t h d)")
        tt_hi = sb("tt_hi", [P, T], F32R)
        tt_lo = sb("tt_lo", [P, T], F32R)
        logit = sb("logit", [P, NT, NE])
        cmp_a = sb("cmp_a", [P, NT, NE * NE])
        cmp_b = sb("cmp_b", [P, NT, NE * NE])
        rank = sb("rank", [P, NT, NE])
        first = sb("first", [P, NT, NE])
        second = sb("second", [P, NT, NE])
        gap = sb("gap", [P, NT])
        tgap = sb("tgap", [P, NT])
        comb = sb("comb", [P, NT, NE])
        tanh_g = sb("tanh_g", [P, 2, T])
        hidden = sb("hidden", [P, 2, T])
        acc = sb("acc", [P, NT, P])
        pj = sb("pj", [P, NT, PROJ])
        pjsq = sb("pjsq", [P, NT, PROJ])
        pj_ss = sb("pj_ss", [P, NT])
        pj_inv = sb("pj_inv", [P, NT])
        pj_t = sb("pj_t", [PROJ, T])
        lg4 = sb("lg4", [P, NT, NR])
        ex4 = sb("ex4", [P, NT, NR])
        cmp4_a = sb("cmp4_a", [P, NT, NR * NR])
        cmp4_b = sb("cmp4_b", [P, NT, NR * NR])
        rank4 = sb("rank4", [P, NT, NR])
        st4 = sb("st4", [P, 3, NT])
        ret = sb("ret", [P, NT, NR])
        dr = sb("dr", [P, NT, RTOT])
        dr_t = sb("dr_t", [RTOT, T])

        bank = [ctx.enter_context(nc.psum_tensor(f"bank{n}", [P, 512], F32)) for n in range(8)]
        SCORE = [bank[0:2], bank[2:4]]
        BV = bank[4]
        GU = bank[5:7]
        BOUT = bank[7]

        loads = {n: sem("ld_" + n) for n in ("const", "mod", "attn", "gu0", "gu1", "ffn", "small")}
        prep = {n: sem("prep_" + n) for n in (
            "silu", "temp", "exptemp", "u2", "simss", "siminv", "modcols_pe", "modcols", "modrows_pe", "rows",
            "weff_pe", "wqkv0", "wqkv1", "cleared", "stack1", "hi", "lo", "simt", "simn_pe",
            "simn", "dve", "pool")}
        scratch_written = sem("scratch_written")

        passed = {e: sem("passed_" + e) for e in ("pool", "dve")}

        x_loaded = signal("x_loaded", 16)
        rows_a_loaded = signal("rows_a_loaded", 16)
        rows_b_loaded = signal("rows_b_loaded", 16)
        rows_g_loaded = signal("rows_g_loaded", 16)
        rows_c_loaded = signal("rows_c_loaded", 16)
        x_stored = signal("x_stored", 16, ahead=1)
        SITES = {"a": 0, "b": 0, "mix": 0, "moe": 0, "c": 1, "d": 1}
        var_ready = {s: signal("var_" + s, 1, int(s == "mix")) for s in SITES}
        rstd_ready = {s: signal("rstd_" + s) for s in SITES}
        xn_ready = {s: signal("xn_" + s) for s in SITES}
        xt_ready = {s: signal("xt_" + s) for s in SITES if s != "b"}
        h_ready = {s: signal("h_" + s, 1, int(s in "ad")) for s in SITES if s != "b"}
        pool_self = {s: signal("pself_" + s) for s in SITES}
        dve_self = {p: signal("dself_" + p, n) for p, n in
                    (("a", 11), ("head", 6), ("k", 14), ("c", 9), ("d", 15))}

        def pair(name, per=1, ahead=(0, 0)):
            return [signal(f"{name}{n}", per, ahead[n]) for n in range(2)]

        cols_ready = pair("cols_ready")
        qkv_done = pair("qkv_done", NT)
        qkv_copied = pair("qkv_copied", NT)
        parts_ready = pair("parts_ready")
        stack_ready = pair("stack_ready")
        spread_done = pair("spread_done", 4)
        k_spread = pair("k_spread", NT)
        q_spread = pair("q_spread", NT)
        maxscore_done = signal("maxscore_done", NU)
        max_taken = signal("max_taken", NU)
        max_stacked = signal("max_stacked")
        max_turned = signal("max_turned")
        max_ready = signal("max_ready")
        score_done = pair("score_done", NU)
        squared = signal("squared", NU)
        rooted = signal("rooted", NU)
        ratio_done = signal("ratio_done", NU)
        lifted = signal("lifted", NU)
        probs_ready = pair("probs_ready", NU)
        pv_done = pair("pv_done", 2)
        pv_copied = pair("pv_copied", 2, (0, 2))
        y_back = pair("y_back", NT)
        y_ready = pair("y_ready")
        yt_done = pair("yt_done")
        yt_copied = pair("yt_copied")
        attn_out = pair("attn_out")
        x_mid_ready = [signal("x_a_ready", 1, ahead=1), signal("x_c_ready")]
        mix_done = signal("mix_done")
        parts_moe = signal("parts_moe")
        logits_done = signal("logits_done")
        gap_ready = signal("gap_ready")
        tanh_ready = signal("tanh_ready")
        gu_done = signal("gu_done", NCH)
        tanh_done = signal("tanh_done", NCH)
        product_done = signal("product_done", NCH)
        hidden_ready = signal("hidden_ready", NCH)
        expert_done = signal("expert_done", NE)
        expert_added = signal("expert_added", NE)
        x_b_ready = signal("x_b_ready", 1, ahead=1)
        ffn1_done = signal("ffn1_done")
        pj_ready = signal("pj_ready")
        pjss_ready = signal("pjss_ready")
        pjinv_ready = signal("pjinv_ready")
        pjt_done = signal("pjt_done")
        pjt_ready = signal("pjt_ready")
        lg4_done = signal("lg4_done")
        lg4_shifted = signal("lg4_shifted")
        exp4_ready = signal("exp4_ready")
        dr_ready = signal("dr_ready")
        drt_done = signal("drt_done")
        drt_ready = signal("drt_ready")
        ffn1_out = signal("ffn1_out")
        x_out_ready = signal("x_out_ready", 1, ahead=1)

        def rounds(eng, a, k, c):
            interleave(a(eng, (-2, 2)))
            interleave(k(eng, (-1, 1)), a(eng, (-1, 2)))
            with eng.Fori(0, B - 2) as r:
                interleave(k(eng, (r, 1)), a(eng, (r, 2)), c(eng, (r, 0)))
            interleave(k(eng, (B - 2, 1)), c(eng, (B - 2, 0)))
            interleave(c(eng, (B - 1, 0)))

        scratch = a["scratch"]
        block = ctx.enter_context(nc.Block())

        def load_x(sp, i):
            sp.wait_ge(*x_mid_ready[0].before(i, 1))
            sp.dma_start(x_in[:, :, :], a["L0_attn_x"][bass.ds(i[0] + i[1], 1)]
                         .rearrange("o (n p) c -> p (o n) c", p=P)).then_inc(x_loaded.sem, 16)

        def load_rows(sp, i, dst, lo, n, loaded, used):
            sp.wait_ge(*used.before(i, 1))
            sp.dma_start(dst[:, :, :].rearrange("p n c -> p (n c)"),
                         scratch[bass.ds(i[0] + i[1], 1), lo:lo + n, :]
                         .rearrange("o n c -> o (n c)").to_broadcast([P, n * P])).then_inc(loaded.sem, 16)

        def sp_round(sp, r, streams):
            if "C" in streams:
                load_rows(sp, (r, 0), rows_c, 4, 2, rows_c_loaded, x_out_ready)
            if "A" in streams:
                load_rows(sp, (r, 2), rows_a, 0, 1, rows_a_loaded, x_mid_ready[0])
                load_rows(sp, (r, 2), rows_b, 2, 2, rows_b_loaded, var_ready["mix"])
            if "K" in streams:
                load_rows(sp, (r, 1), rows_g, 1, 1, rows_g_loaded, x_b_ready)
            if "C" in streams:
                sp.wait_ge(*x_out_ready((r, 0), 1))
                sp.dma_start(out[bass.ds(r, 1)].rearrange("o (n p) c -> p (o n) c", p=P),
                             x_out[:, :, :]).then_inc(x_stored.sem, 16)
            if "x" in streams:
                load_x(sp, (r, 3))

        @block.sync
        def _(sp):
            for name, dst, src in (
                ("const", identf[:, :], a["identf"]), ("const", identb[:, :], a["identb"].bitcast(BF16)),
                ("mod", c_t[:, 0, :], a["L0_c"]), ("mod", c_t[:, 1, :], a["L1_c"]),
                ("mod", wmod[:, 0, :], a["L0_wmod"]), ("mod", wmod[:, 1, :], a["L1_wmod"]),
                ("attn", u2[:, :, :, :], a["u2"]), ("attn", wd3[:, :, :, :], a["wd3"]),
                ("const", maskb[:, :, :], a["maskb"].bitcast(BF16)), ("const", selb[:, :], a["selb"].bitcast(BF16)),
                ("const", rope[:, :, :, :], a["rope"]),
                ("small", slope[:, :], a["L1_attn_alibi_slopes"].partition_broadcast(P)),
                ("small", position[:, :], a["position"]), ("small", simt[:, :], a["L1_ffn_sim"]),
                ("small", tempc[:, :], a["L1_ffn_temp"].partition_broadcast(NR)),
                ("small", w_qkv1[:, :], a["L1_attn_w_qkv"]),
                ("ffn", w_o[0][:, :], a["L0_attn_Wc"]), ("ffn", w_o[1][:, :], a["L1_attn_w_out"]),
                ("ffn", w_mix[:, :], a["L0_ffn_attn_w"]), ("ffn", w_gate[:, :], a["L0_ffn_gate_w"]),
                ("ffn", lncol[:, :], a["lncol"]), ("ffn", before[:, :], a["before"]),
                ("ffn", before4[:, :], a["before4"]), ("ffn", w_ffn1[:, :], a["w_ffn1"]),
                ("ffn", w_up1[:, :], a["w_up1"]), ("ffn", bp_row[:, :], a["L1_ffn_bp"].partition_broadcast(P)),
                ("ffn", w_down[:, :, :], a["L0_ffn_down_proj"]),
            ):
                sp.dma_start(dst, src).then_inc(loads[name], 16)
            sp.sem_inc(x_stored.sem, 16)
            sp.wait_ge(prep["rows"], 1)
            sp.dma_start(scratch, rowmods[:, :, :]).then_inc(scratch_written, 16)
            sp.wait_ge(scratch_written, 16)
            load_x(sp, (-2, 2))
            sp_round(sp, -2, "Ax")
            sp_round(sp, -1, "AKx")
            with sp.Fori(0, B - 3) as r:
                sp_round(sp, r, "AKCx")
            sp_round(sp, B - 3, "AKC")
            sp_round(sp, B - 2, "KC")
            sp_round(sp, B - 1, "C")
            sp.wait_ge(*x_stored((B - 1, 0), 16))

        def pool_cols(pool, i, n):
            pool.wait_ge(*h_ready["ad"[n]].before(i, 1))
            pool.sem_inc(passed["pool"], 1)
            pool.tensor_copy(cols_now[n][:, :], modcols[:, bass.ds(i[0] + i[1], 1), n, :]
                             .rearrange("p o m -> p (o m)")).then_inc(cols_ready[n].sem, 1)

        def pool_rstd(pool, i, s):
            n = SITES[s]
            pool.wait_ge(*var_ready[s](i, 1))
            pool.sem_inc(passed["pool"], 1)
            pool.tensor_scalar(vareps[n][:, :], meanvar[n][:, :, 1], EPS_LN, None, ALU.add)\
                .then_inc(pool_self[s].sem, 1)
            pool.wait_ge(*pool_self[s](i, 1))
            pool.tensor_tensor(rstd[n][:, :], vareps[n][:, :], minus_half[:, :], ALU.pow)\
                .then_inc(rstd_ready[s].sem, 1)

        def pool_a(pool, i):
            yield 0.1
            pool_cols(pool, i, 0)
            yield 0.4
            pool_rstd(pool, i, "a")
            for k, s in enumerate(("b", "mix", "moe")):
                yield TOWARDS_EXPERTS + (0.1, 1.7, 4.6)[k]
                pool_rstd(pool, i, s)

        def pool_k(pool, i):
            yield 0

        def pool_c(pool, i):
            yield 0.1
            pool_cols(pool, i, 1)
            yield 0.4
            pool_rstd(pool, i, "c")
            for u in range(NU):
                yield ROOT_AT[u // RING] + 0.8 + 0.25 * (u % RING)
                pool.wait_ge(*lifted(i, u + 1))
                pool.sem_inc(passed["pool"], 1)
                heads, cols = (2, 256) if u % 3 < 2 else (4, 128)
                v = probs[1][:, u % RING, :].rearrange("p (h q) -> p h q", h=heads)[:, :, 0:P]
                pool.affine_select(out=v, in_=v, compare_op=ALU.is_ge, fill=0.0, base=0,
                                   pattern=[[0, heads], [1, P]], channel_multiplier=-1)\
                    .then_inc(probs_ready[1].sem, 1)
            yield FFN1_AT + 0.1
            pool_rstd(pool, i, "d")
            yield FFN1_AT + 2.4
            pool.wait_ge(*pjss_ready(i, 1))
            pool.tensor_tensor(pj_inv[:, :], pj_ss[:, :], minus_half[:, :], ALU.pow)\
                .then_inc(pjinv_ready.sem, 1)

        @block.gpsimd
        def _(pool):
            steps = [0]

            def step(ins):
                steps[0] += 1
                ins.then_inc(prep["pool"], 1)
                pool.wait_ge(prep["pool"], steps[0])

            step(pool.memset(minus_half[:, :], -0.5))
            for n in range(2):
                pool.memset(stack[n][:, :, :, :], 0.0)
            pool.memset(max_stack[:, :, :], 0.0)
            for n in range(2):
                pool.memset(q_t[n][:, :, :, :], 0.0)
                last = pool.memset(v_aug[n][:, :, :, :], 0.0)
            step(last)
            for n in range(2):
                last = pool.memset(v_aug[n][:, :, :, D:D + 1], 1.0)
            last.then_inc(prep["cleared"], 1)
            pool.wait_ge(prep["simss"], 1)
            pool.tensor_tensor(simst[:, 3:4], simst[:, 0:1], minus_half[0:NR, 0:1], ALU.pow)\
                .then_inc(prep["siminv"], 1)
            pool.wait_ge(prep["modcols"], 1)
            rounds(pool, pool_a, pool_k, pool_c)

        def act_turned(act, i, s, src, scale, bias, dst):
            act.wait_ge(*xt_ready[s](i, 1))
            act.activation(dst, src, ACT.Identity, scale=scale, bias=bias).then_inc(h_ready[s].sem, 1)

        def act_qkv(act, i, n):
            for t in range(NT):
                act.wait_ge(*qkv_done[n](i, t + 1))
                src = SCORE[n][t]
                act.activation(raw[n][:, t, 0:256], src[:, 0:256], ACT.Copy)
                if n == 0:
                    act.activation(raw[0][:, t, 384:512], src[:, 384:512], ACT.Copy)
                act.activation(v_aug[n][:, t, :, 0:D], src[:, 256:384].rearrange("p (h d) -> p h d", h=H),
                               ACT.Copy).then_inc(qkv_copied[n].sem, 1)

        def act_keys(act, i, n, t):
            act.wait_ge(*spread_done[n](i, 2 * t + 1))
            act.activation(k_t[n][:, :, t * P:(t + 1) * P],
                           SCORE[n][0][:, :].bitcast(BF16).rearrange("p (g q) -> p g q", g=NPAIR),
                           ACT.Copy).then_inc(k_spread[n].sem, 1)

        def act_start(act, i, n):
            yield 2.2
            act.wait_ge(*cols_ready[n](i, 1))
            act_turned(act, i, "ac"[n], SCORE[n][0][:, 0:T], cols_now[n][:, 1:2], cols_now[n][:, 0:1], h_t[n][:, :])
            yield 3.1
            act_qkv(act, i, n)
            for t in range(NT):
                yield 8.1 + t
                act_keys(act, i, n, t)

        def act_yt(act, i, n):
            act.wait_ge(*yt_done[n](i, 1))
            act.activation(y_nt[n][:, :], SCORE[n][0][:, 0:T], ACT.Copy).then_inc(yt_copied[n].sem, 1)

        def act_a(act, i):
            yield from act_start(act, i, 0)
            yield 19.2
            act.wait_ge(*max_turned(i, 1))
            act.activation(max_t[:, :], SCORE[0][0][:, 0:P].bitcast(BF16), ACT.Copy).then_inc(max_ready.sem, 1)
            for u in range(NU):
                yield score_at(0, u) + 0.1
                act.wait_ge(*score_done[0](i, u + 1))
                act.activation(probs[0][:, u % RING, :], SCORE[0][u % 2][:, :], ACT.Exp, scale=SCALE)\
                    .then_inc(probs_ready[0].sem, 1)
            yield GATHER_AT[0] + 2.8
            act_yt(act, i, 0)
            yield TOWARDS_EXPERTS + 3.2
            act_turned(act, i, "mix", SCORE[0][0][:, 0:T], lncol[:, 0:1], lncol[:, 1:2], h_t[0][:, :])
            yield TOWARDS_EXPERTS + 6.2
            act_turned(act, i, "moe", SCORE[0][0][:, 0:T], lncol[:, 2:3], lncol[:, 3:4], tt[:, :])

        def act_c(act, i):
            yield from act_start(act, i, 1)
            for burst in range(NU // RING):
                units = range(burst * RING, (burst + 1) * RING)
                for u in units:
                    yield score_at(1, u) + 0.1
                    act.wait_ge(*score_done[1](i, u + 1))
                    act.activation(ratio[:, u % RING, :], SCORE[1][u % 2][:, :], ACT.Square)
                    act.activation(probs[1][:, u % RING, :], SCORE[1][u % 2][:, :], ACT.Copy)\
                        .then_inc(squared.sem, 1)
                yield ROOT_AT[burst]
                for u in units:
                    act.wait_ge(*squared(i, u + 1))
                    act.activation(ratio[:, u % RING, :], ratio[:, u % RING, :], ACT.Abs_reciprocal_sqrt, bias=1.0)\
                        .then_inc(rooted.sem, 1)
                for u in units:
                    yield ROOT_AT[burst] + 0.7 + 0.25 * (u % RING)
                    act.wait_ge(*ratio_done(i, u + 1))
                    act.activation(probs[1][:, u % RING, :], probs[1][:, u % RING, :], ACT.Identity, bias=1.0)\
                        .then_inc(lifted.sem, 1)
            yield GATHER_AT[1] + 2.8
            act_yt(act, i, 1)
            yield FFN1_AT + 1.2
            act_turned(act, i, "d", SCORE[1][0][:, 0:T], cols_now[1][:, 4:5], cols_now[1][:, 3:4], h_t[1][:, :])
            yield FFN1_AT + 2.8
            act.wait_ge(*pjt_done(i, 1))
            act.activation(pj_t[:, :], SCORE[1][0][0:PROJ, 0:T], ACT.Copy).then_inc(pjt_ready.sem, 1)
            yield FFN1_AT + 3.6
            act.wait_ge(*lg4_shifted(i, 1))
            act.activation(ex4[:, :, :], lg4[:, :, :], ACT.Exp).then_inc(exp4_ready.sem, 1)
            yield FFN1_AT + 5.6
            act.wait_ge(*drt_done(i, 1))
            act.activation(dr_t[:, :], SCORE[1][0][0:RTOT, 0:T], ACT.Copy).then_inc(drt_ready.sem, 1)

        def act_k(act, i):
            for c in range(NCH):
                if c == 1:
                    yield chunk_at(1) + 0.05
                    act.wait_ge(*gap_ready(i, 1))
                    act.activation(tgap[:, :], gap[:, :], ACT.Tanh, scale=0.5).then_inc(tanh_ready.sem, 1)
                yield chunk_at(c) + 0.1
                act.wait_ge(*gu_done(i, c + 1))
                if c >= 2:
                    act.wait_ge(*hidden_ready(i, c - 1))
                act.activation(tanh_g[:, c % 2, :], GU[c % 2][:, 0:T], ACT.Tanh, scale=0.5)\
                    .then_inc(tanh_done.sem, 1)

        @block.scalar
        def _(act):
            for user in (h_ready["a"], h_ready["d"]):
                act.sem_inc(user.sem, 1)
            piece = NCH // NQ
            for k in range(2):
                act.dma_start(stage[:, k, :, :, :], a["gu"][:, :, k * piece:(k + 1) * piece, :])\
                   .then_inc(loads[f"gu{k}"], 16)
            act.wait_ge(loads["mod"], 64)
            act.activation(silu_c[:, :, :], c_t[:, :, :], ACT.Silu).then_inc(prep["silu"], 1)
            act.wait_ge(prep["temp"], 1)
            act.activation(simst[:, 2:3], simst[:, 1:2], ACT.Exp).then_inc(prep["exptemp"], 1)
            for k in range(NQ):
                act.wait_ge(loads[f"gu{k % 2}"], 16 * (k // 2 + 1))
                act.activation(gu_hi[:, :, k * piece:(k + 1) * piece, :], stage[:, k % 2, :, :, :], ACT.Copy)\
                    .then_inc(prep["hi"], 1)
                if k + 2 < NQ:
                    act.wait_ge(prep["hi"], k + 1)
                    act.wait_ge(prep["lo"], k + 1)
                    act.dma_start(stage[:, k % 2, :, :, :], a["gu"][:, :, (k + 2) * piece:(k + 3) * piece, :])\
                       .then_inc(loads[f"gu{k % 2}"], 16)
            act.wait_ge(loads["ffn"], 11 * 16)
            rounds(act, act_a, act_k, act_c)

        def pe_turn(pe, i, s):
            n = SITES[s]
            pe.wait_ge(*xn_ready[s](i, 1))
            for t in range(NT):
                last = pe.transpose(SCORE[n][0][:, t * P:(t + 1) * P], xn[n][:, t, :], identf[:, :])
            last.then_inc(xt_ready[s].sem, 1)

        def pe_spread(pe, i, n, t):
            for q in range(2):
                if t == 1:
                    pe.wait_ge(*(k_spread, q_spread)[q][n](i, 1))
                dst = SCORE[n][q][:, :].bitcast(BF16)
                for g in range(NPAIR):
                    row = (1 - q) * H + 2 * g
                    last = pe.transpose(dst[:, g * P:(g + 1) * P],
                                        stack[n][:, t, row:row + 2, :].rearrange("p h r -> p (h r)"),
                                        identb[:, :])
                last.then_inc(spread_done[n].sem, 1)

        def pe_start(pe, i, n):
            s = "ac"[n]
            w = (w_qkv0, w_qkv1)[n]
            wide = (512, 384)[n]
            yield 2
            pe_turn(pe, i, s)
            yield 3
            pe.wait_ge(*h_ready[s](i, 1))
            for t in range(NT):
                pe.matmul(SCORE[n][t][:, 0:wide], h_t[n][:, t * P:(t + 1) * P], w[:, :], start=True, stop=True)\
                    .then_inc(qkv_done[n].sem, 1)
            yield 8
            pe.wait_ge(*stack_ready[n](i, 1))
            pe_spread(pe, i, n, 0)
            yield 9
            pe_spread(pe, i, n, 1)

        def pe_maximum(pe, i, u):
            dst = SCORE[0][u % 2]
            q, k = q_t[0], k_t[0]
            if u == 0:
                pe.wait_ge(*k_spread[0](i, NT))
                pe.wait_ge(*q_spread[0](i, NT))
            if u >= 2:
                pe.wait_ge(*max_taken(i, u - 1))
            if u < 8:
                k3 = dst[:, :].rearrange("p (h k) -> p h k", h=2)
                pe.matmul(k3[:, :, P:T], identb[:, :], maskb[:, 0:1, :].to_broadcast([P, 2, P]),
                          start=True, stop=False, skip_group_check=True)
                for j in range(2):
                    last = pe.matmul(k3[:, j, :], q[:, u, j, P:T], k[:, u, :], start=False,
                                     stop=j == 1, skip_group_check=True)
            else:
                k4 = dst[:, :].rearrange("p (h k) -> p h k", h=4)
                pe.matmul(k4, identb[:, :], maskb[:, 0:1, :].to_broadcast([P, 4, P]),
                          start=True, stop=False, skip_group_check=True)
                for j in range(4):
                    g = 2 * (u - 8) + j // 2
                    last = pe.matmul(k4[:, j, :], q[:, g, j % 2, 0:P], k[:, g, 0:P], start=False,
                                     stop=j == 3, skip_group_check=True)
            last.then_inc(maxscore_done.sem, 1)

        def pe_score(pe, i, n, u):
            g, r = divmod(u, 3)
            dst = SCORE[n][u % 2]
            q, k = q_t[n], k_t[n]
            if u >= 2:
                pe.wait_ge(*(probs_ready[0] if n == 0 else squared)(i, u - 1))
            if r < 2:
                p = 2 * g + r
                q3 = dst[:, :].rearrange("p (h q) -> p h q", h=2)
                if n == 0:
                    pe.matmul(q3[:, :, 0:P], identb[:, :], maskb[:, 1:2, :].to_broadcast([P, 2, P]),
                              start=True, stop=False, skip_group_check=True)
                last = pe.matmul(dst[:, :], k[:, p, 0:P], q[:, p, :, :].rearrange("p h q -> p (h q)"),
                                 start=n == 1, stop=n == 1, skip_group_check=True)
                if n == 0:
                    for j in range(2):
                        last = pe.matmul(q3[:, j, :], selb[:, 2 * p + j:2 * p + j + 1].to_broadcast([P, P]), max_t[:, :], start=False,
                                         stop=j == 1, skip_group_check=True)
            else:
                q4 = dst[:, :].rearrange("p (h q) -> p h q", h=4)
                if n == 0:
                    pe.matmul(q4, identb[:, :], maskb[:, 1:2, :].to_broadcast([P, 4, P]),
                              start=True, stop=False, skip_group_check=True)
                for j in range(2):
                    last = pe.matmul(q4[:, 2 * j:2 * j + 2, :], k[:, 2 * g + j, P:T],
                                     q[:, 2 * g + j, :, P:T], start=n == 1, stop=n == 1,
                                     skip_group_check=True)
                if n == 0:
                    for j in range(4):
                        last = pe.matmul(q4[:, j, :], selb[:, 4 * g + j:4 * g + j + 1].to_broadcast([P, P]), max_t[:, P:T], start=False,
                                         stop=j == 3, skip_group_check=True)
            last.then_inc(score_done[n].sem, 1)

        def pe_values(pe, i, n, g):
            pe.wait_ge(*probs_ready[n](i, 3 * g + 3))
            if g == 0 and n == 0:
                base, plus = i
                pe.wait_ge(*pv_copied[1]((base, plus - 2), 2))
            if g == 2:
                pe.wait_ge(*pv_copied[n](i, 1))
            half = BV[:, (g % 2) * T:(g % 2 + 1) * T]
            for j in range(4):
                u = 3 * g + j // 2
                pe.matmul(half[VW * j:VW * j + D + 1, :], v_aug[n][:, 0, 4 * g + j, :],
                          probs[n][:, u % RING, (j % 2) * T:(j % 2 + 1) * T],
                          start=True, stop=False, skip_group_check=True)
                last = pe.matmul(half[VW * j:VW * j + D + 1, P:T], v_aug[n][:, 1, 4 * g + j, :],
                                 probs[n][:, (3 * g + 2) % RING, j * P:(j + 1) * P],
                                 start=False, stop=True, skip_group_check=True)
            if g % 2:
                last.then_inc(pv_done[n].sem, 1)

        def pe_gather(pe, i, n):
            yield GATHER_AT[n] + 0.8
            pe.wait_ge(*pv_copied[n](i, 2))
            for t in range(NT):
                for g in range(4):
                    last = pe.transpose(SCORE[n][t][:, g * P:(g + 1) * P], y_t[n][:, g, t * P:(t + 1) * P], identf[:, :])
                last.then_inc(y_back[n].sem, 1)
            yield GATHER_AT[n] + 2.4
            pe.wait_ge(*y_ready[n](i, 1))
            for t in range(NT):
                last = pe.transpose(SCORE[n][0][:, t * P:(t + 1) * P], y_n[n][:, t, :], identf[:, :])
            last.then_inc(yt_done[n].sem, 1)
            yield GATHER_AT[n] + 3.2
            pe.wait_ge(*yt_copied[n](i, 1))
            for t in range(NT):
                last = pe.matmul(SCORE[n][1][:, t * P:(t + 1) * P], y_nt[n][:, t * P:(t + 1) * P], w_o[n][:, :],
                                 start=True, stop=True)
            last.then_inc(attn_out[n].sem, 1)

        def pe_a(pe, i):
            yield from pe_start(pe, i, 0)
            for u in range(NU):
                yield maximum_at(u)
                pe_maximum(pe, i, u)
            yield 19
            pe.wait_ge(*max_stacked(i, 1))
            for t in range(NT):
                last = pe.transpose(SCORE[0][0][:, t * 64:(t + 1) * 64].bitcast(BF16), max_stack[:, t, :], identb[:, :])
            last.then_inc(max_turned.sem, 1)
            for u in range(NU):
                yield score_at(0, u)
                if u == 0:
                    pe.wait_ge(*max_ready(i, 1))
                pe_score(pe, i, 0, u)
                if u % 3 == 0 and u > 0:
                    yield values_at(0, u // 3 - 1)
                    pe_values(pe, i, 0, u // 3 - 1)
            yield values_at(0, 3)
            pe_values(pe, i, 0, 3)
            yield from pe_gather(pe, i, 0)
            yield TOWARDS_EXPERTS + 2.8
            pe_turn(pe, i, "mix")
            yield TOWARDS_EXPERTS + 3.6
            pe.wait_ge(*h_ready["mix"](i, 1))
            for t in range(NT):
                last = pe.matmul(SCORE[0][1][:, t * P:(t + 1) * P], h_t[0][:, t * P:(t + 1) * P], w_mix[:, :],
                                 start=True, stop=True)
            last.then_inc(mix_done.sem, 1)
            yield TOWARDS_EXPERTS + 5.8
            pe_turn(pe, i, "moe")
            yield TOWARDS_EXPERTS + 6.6
            pe.wait_ge(*h_ready["moe"](i, 1))
            for t in range(NT):
                last = pe.matmul(SCORE[0][1][:, t * NE:(t + 1) * NE], tt[:, t * P:(t + 1) * P], w_gate[:, :],
                                 start=True, stop=True)
            last.then_inc(logits_done.sem, 1)

        def pe_k(pe, i):
            for c in range(NCH):
                yield chunk_at(c)
                if c == 0:
                    pe.wait_ge(*parts_moe(i, 1))
                if c >= 2:
                    pe.wait_ge(*hidden_ready(i, c - 1))
                for n in range(2):
                    dst = GU[c % 2][:, n * T:(n + 1) * T]
                    pe.matmul(dst, gu_hi[:, n, c, :], tt_hi[:, :], start=True, stop=False, skip_group_check=True)
                    pe.matmul(dst, gu_hi[:, n, c, :], tt_lo[:, :], start=False, stop=False, skip_group_check=True)
                    last = pe.matmul(dst, gu_lo[:, n, c, :], tt_hi[:, :], start=False, stop=True,
                                     skip_group_check=True)
                last.then_inc(gu_done.sem, 1)
                if c >= 1:
                    pe_down(pe, i, c - 1)
            yield chunk_at(NCH - 1) + 0.8
            pe_down(pe, i, NCH - 1)

        def pe_down(pe, i, c):
            e, k = divmod(c, CH)
            pe.wait_ge(*hidden_ready(i, c + 1))
            if k == 0 and e >= 1:
                pe.wait_ge(*expert_added(i, e))
            for t in range(NT):
                last = pe.matmul(BOUT[:, t * P:(t + 1) * P], hidden[:, c % 2, t * P:(t + 1) * P],
                                 w_down[:, c, :], start=k == 0 and t == 0, stop=k == CH - 1 and t == 1,
                                 skip_group_check=True)
            if k == CH - 1:
                last.then_inc(expert_done.sem, 1)

        def pe_c(pe, i):
            yield from pe_start(pe, i, 1)
            pe.wait_ge(*k_spread[1](i, NT))
            pe.wait_ge(*q_spread[1](i, NT))
            for u in range(NU):
                if u in (6, 9):
                    yield values_at(1, u // 3 - 2)
                    pe_values(pe, i, 1, u // 3 - 2)
                yield score_at(1, u)
                pe_score(pe, i, 1, u)
            for g in (2, 3):
                yield values_at(1, g)
                pe_values(pe, i, 1, g)
            yield from pe_gather(pe, i, 1)
            small, both = SCORE[1]
            yield FFN1_AT + 0.9
            pe_turn(pe, i, "d")
            yield FFN1_AT + 1.4
            pe.wait_ge(*h_ready["d"](i, 1))
            for t in range(NT):
                last = pe.matmul(both[:, t * T:t * T + P + PROJ + RTOT], h_t[1][:, t * P:(t + 1) * P], w_ffn1[:, :],
                                 start=t == 0, stop=False, skip_group_check=True)
            last.then_inc(ffn1_done.sem, 1)
            yield FFN1_AT + 2.4
            pe.wait_ge(*pj_ready(i, 1))
            for t in range(NT):
                last = pe.transpose(small[0:PROJ, t * P:(t + 1) * P], pj[:, t, :], identf[:, :])
            last.then_inc(pjt_done.sem, 1)
            yield FFN1_AT + 3
            pe.wait_ge(*pjt_ready(i, 1))
            for t in range(NT):
                last = pe.matmul(small[:, T + t * NR:T + (t + 1) * NR], pj_t[:, t * P:(t + 1) * P], simn[:, :],
                                 start=True, stop=True)
            last.then_inc(lg4_done.sem, 1)
            yield FFN1_AT + 5.2
            pe.wait_ge(*dr_ready(i, 1))
            for t in range(NT):
                last = pe.transpose(small[0:RTOT, t * P:(t + 1) * P], dr[:, t, :], identf[:, :])
            last.then_inc(drt_done.sem, 1)
            yield FFN1_AT + 5.8
            pe.wait_ge(*drt_ready(i, 1))
            for t in range(NT):
                last = pe.matmul(both[:, t * T:t * T + P], dr_t[:, t * P:(t + 1) * P], w_up1[:, :],
                                 start=False, stop=t == 1, skip_group_check=True)
            last.then_inc(ffn1_out.sem, 1)

        @block.tensor
        def _(pe):
            pe.wait_ge(prep["silu"], 1)
            for l in range(2):
                for m in range(6):
                    last = pe.matmul(bank[0][:, (l * 6 + m) * B:(l * 6 + m + 1) * B],
                                     wmod[:, l, m * P:(m + 1) * P], silu_c[:, l, :], start=True, stop=True)
            last.then_inc(prep["modcols_pe"], 1)
            for l in range(2):
                pe.matmul(bank[1 + 2 * l][0:B, 0:512], silu_c[:, l, :], wmod[:, l, 0:512], start=True, stop=True)
                last = pe.matmul(bank[2 + 2 * l][0:B, 0:256], silu_c[:, l, :], wmod[:, l, 512:768],
                                 start=True, stop=True)
            last.then_inc(prep["modrows_pe"], 1)
            pe.wait_ge(loads["attn"], 32)
            pe.wait_ge(prep["u2"], 1)
            for n in range(3):
                for g in range(NPAIR):
                    last = pe.matmul(bank[5 + n][:, g * 24:(g + 1) * 24], wd3[:, n, g, :],
                                     u2[:, n, :, :].rearrange("p h d -> p (h d)"), start=True, stop=True)
            last.then_inc(prep["weff_pe"], 1)
            pe.wait_ge(loads["const"], 80)
            pe.wait_ge(prep["simt"], 1)
            pe.wait_ge(prep["modcols"], 1)
            pe.transpose(bank[0][0:PROJ, 0:NR], simt[:, :], identf[0:NR, 0:NR]).then_inc(prep["simn_pe"], 1)
            pe.wait_ge(loads["ffn"], 11 * 16)
            pe.wait_ge(prep["lo"], NQ)
            pe.wait_ge(prep["hi"], NQ)
            rounds(pe, pe_a, pe_k, pe_c)

        def dve_stats(dve, i, s, src, chain):
            n = SITES[s]
            for t in range(NT):
                last = dve.bn_stats(stats[n][:, t, :], src[:, t, :])
            chain(last)
            dve.sem_inc(passed["dve"], 1)
            for t in range(NT):
                last = dve.bn_aggr(meanvar[n][:, t, :], stats[n][:, t, :])
            last.then_inc(var_ready[s].sem, 1)

        def dve_norm(dve, i, s, src):
            n = SITES[s]
            dve.wait_ge(*rstd_ready[s](i, 1))
            for t in range(NT):
                last = dve.tensor_scalar(xn[n][:, t, :], src[:, t, :], meanvar[n][:, t, 0:1], rstd[n][:, t:t + 1],
                                         ALU.subtract, ALU.mult)
            last.then_inc(xn_ready[s].sem, 1)

        def rank_of(dve, chain, values, n, earlier, ca, cb, rank):
            other = values.unsqueeze(2).to_broadcast([P, NT, n, n])
            own = values.unsqueeze(3).to_broadcast([P, NT, n, n])
            grid = dict(e=n)
            dve.tensor_tensor(ca.rearrange("p t (e j) -> p t e j", **grid), other, own, ALU.is_gt)
            chain(dve.tensor_tensor(cb.rearrange("p t (e j) -> p t e j", **grid), other, own, ALU.is_ge))
            chain(dve.tensor_tensor(cb, cb, ca, ALU.subtract))
            chain(dve.tensor_tensor(cb, cb, earlier[:, :].unsqueeze(1).to_broadcast([P, NT, n * n]), ALU.mult))
            chain(dve.tensor_tensor(ca, ca, cb, ALU.add))
            chain(dve.tensor_reduce(rank, ca.rearrange("p t (e j) -> p t e j", **grid), AX.X, ALU.add))

        def dve_start(dve, i, n, chain):
            src = (x_in, x_b)[n]
            yield 0.3
            if n == 0:
                dve.wait_ge(*x_loaded(i, 16))
            else:
                dve.wait_ge(*x_b_ready(i, 1))
            dve_stats(dve, i, "ac"[n], src, chain)
            yield 1.2
            dve_norm(dve, i, "ac"[n], src)
            yield 4
            dve.wait_ge(*qkv_copied[n](i, NT))
            qk = raw[n][:, :, 0:256].rearrange("p t (h d) -> p t h d", d=D)
            if n == 0:
                e = qk[:, :, :, DE:D]
                cos, sin = (rope[:, k, :, :].unsqueeze(2).to_broadcast([P, NT, 2 * H, DE]) for k in range(2))
                dve.tensor_tensor(rot[:, :, :, :], raw[0][:, :, 384:512].rearrange("p t (h d) -> p t h d", d=DE),
                                  sin, ALU.mult)
                chain(dve.tensor_tensor(e, e, cos, ALU.mult))
                chain(dve.tensor_tensor(e, e, rot[:, :, :, :], ALU.add))
            st = stack[n]
            p1, p2 = st[:, :, :, 0:D], st[:, :, :, D:2 * D]
            chain(dve.tensor_copy(p1, qk))
            yield 5
            chain(dve.tensor_tensor(qk, qk, p1, ALU.subtract))
            dve.tensor_copy(p2, qk).then_inc(parts_ready[n].sem, 1)
            yield 6
            dve.wait_ge(*parts_ready[n](i, 1))
            chain(dve.tensor_tensor(qk, qk, p2, ALU.subtract))
            dve.tensor_copy(st[:, :, 0:H, 5 * D:6 * D], qk[:, :, 0:H, :])
            dve.tensor_copy(st[:, :, H:2 * H, 4 * D:5 * D], qk[:, :, H:2 * H, :])
            yield 7
            for side, slot, part in ((0, 2, 0), (0, 4, 0), (0, 3, 1), (1, 3, 0), (1, 5, 0), (1, 2, 1)):
                last = dve.tensor_copy(st[:, :, side * H:(side + 1) * H, slot * D:(slot + 1) * D],
                                       st[:, :, side * H:(side + 1) * H, part * D:(part + 1) * D])
            last.then_inc(stack_ready[n].sem, 1)
            for t in range(NT):
                yield 8.2 + t
                dve.wait_ge(*spread_done[n](i, 2 * t + 2))
                src_q = SCORE[n][1][:, :].bitcast(BF16).rearrange("p (g q) -> p g q", g=NPAIR)
                for j in range(2):
                    rows = slice(ROWS * j, ROWS * (j + 1))
                    last = dve.tensor_copy(q_t[n][rows, :, j, t * P:(t + 1) * P], src_q[rows, :, :])
                last.then_inc(q_spread[n].sem, 1)

        def dve_take_values(dve, i, n, k):
            dve.wait_ge(*pv_done[n](i, k + 1))
            dve.tensor_copy(y_t[n][:, 2 * k:2 * k + 2, :].rearrange("p g q -> p (g q)"), BV[:, :])\
               .then_inc(pv_copied[n].sem, 1)

        def dve_gather(dve, i, n, chain):
            yield GATHER_AT[n]
            dve_take_values(dve, i, n, 1)
            yield GATHER_AT[n] + 1.6
            for t in range(NT):
                dve.wait_ge(*y_back[n](i, t + 1))
                by_head = SCORE[n][t][:, :].rearrange("p (h v) -> p h v", v=VW)
                if n == 0:
                    chain(dve.reciprocal(den[0][:, t, :], by_head[:, :, D]))
                else:
                    chain(dve.tensor_scalar(den[1][:, t, :], by_head[:, :, D], 2 * EPS_RATIONAL, None, ALU.add))
                    chain(dve.reciprocal(den[1][:, t, :], den[1][:, t, :]))
                last = dve.tensor_tensor(y_n[n][:, t, :].rearrange("p (h d) -> p h d", d=D), by_head[:, :, 0:D],
                                         den[n][:, t, :].unsqueeze(2).to_broadcast([P, H, D]), ALU.mult)
            last.then_inc(y_ready[n].sem, 1)
            yield GATHER_AT[n] + 3.7
            gate = (rows_a, rows_c)[n]
            dve.wait_ge(*(rows_a_loaded, rows_c_loaded)[n](i, 16))
            dve.wait_ge(*attn_out[n](i, 1))
            chain(dve.tensor_tensor(xn[n][:, :, :], SCORE[n][1][:, 0:T].rearrange("p (t c) -> p t c", t=NT),
                                    gate[:, 0:1, :].to_broadcast([P, NT, P]), ALU.mult))
            dve.tensor_tensor(x_mid[n][:, :, :], xn[n][:, :, :], (x_in, x_b)[n][:, :, :], ALU.add)\
               .then_inc(x_mid_ready[n].sem, 1)

        def dve_a(dve, i):
            chain = Chain(dve, dve_self["a"], i)
            yield from dve_start(dve, i, 0, chain)
            for u in range(NU):
                yield maximum_at(u) + 0.3
                dve.wait_ge(*maxscore_done(i, u + 1))
                if u < 8:
                    dst, heads = negmax[:, 1, 2 * u:2 * u + 2], 2
                else:
                    dst, heads = negmax[:, 0, 4 * (u - 8):4 * (u - 7)], 4
                dve.tensor_reduce(dst, SCORE[0][u % 2][:, :].rearrange("p (h k) -> p h k", h=heads),
                                  AX.X, ALU.max, negate=True).then_inc(max_taken.sem, 1)
            yield 18.4
            dve.wait_ge(*max_taken(i, NU))
            chain(dve.tensor_copy(max_stack[:, :, 0:H], negmax[:, :, :]))
            chain(dve.tensor_tensor(negmax_r[:, :, :], negmax[:, :, :], max_stack[:, :, 0:H], ALU.subtract))
            dve.tensor_copy(max_stack[:, :, H:2 * H], negmax_r[:, :, :]).then_inc(max_stacked.sem, 1)
            yield values_at(0, 1) + 0.3
            dve_take_values(dve, i, 0, 0)
            yield from dve_gather(dve, i, 0, chain)
            chain.done()
            chain = Chain(dve, dve_self["head"], i)
            yield TOWARDS_EXPERTS
            dve.wait_ge(*x_mid_ready[0](i, 1))
            dve_stats(dve, i, "b", x_mid[0], chain)
            yield TOWARDS_EXPERTS + 0.8
            dve_norm(dve, i, "b", x_mid[0])
            dve.wait_ge(*xn_ready["b"](i, 1))
            dve.wait_ge(*rows_b_loaded(i, 16))
            yield TOWARDS_EXPERTS + 1.2
            chain(dve.tensor_tensor(h_ffn[:, :, :], xn[0][:, :, :], rows_b[:, 1:2, :].to_broadcast([P, NT, P]), ALU.mult))
            chain(dve.tensor_tensor(h_ffn[:, :, :], h_ffn[:, :, :], rows_b[:, 0:1, :].to_broadcast([P, NT, P]),
                                    ALU.add))
            dve_stats(dve, i, "mix", h_ffn, chain)
            yield TOWARDS_EXPERTS + 2.4
            dve_norm(dve, i, "mix", h_ffn)
            yield TOWARDS_EXPERTS + 4.1
            dve.wait_ge(*mix_done(i, 1))
            chain(dve.tensor_tensor(h2[:, :, :], SCORE[0][1][:, 0:T].rearrange("p (t c) -> p t c", t=NT),
                                    h_ffn[:, :, :], ALU.add))
            dve_stats(dve, i, "moe", h2, chain)
            yield TOWARDS_EXPERTS + 5.3
            dve_norm(dve, i, "moe", h2)
            chain.done()

        def dve_k(dve, i):
            chain = Chain(dve, dve_self["k"], i)
            yield 0
            dve.wait_ge(*h_ready["moe"](i, 1))
            chain(dve.tensor_copy(tt_hi[:, :], tt[:, :]))
            dve.tensor_tensor(tt_lo[:, :], tt[:, :], tt_hi[:, :].bitcast(F32), ALU.subtract)\
               .then_inc(parts_moe.sem, 1)
            dve.tensor_copy(x_keep[:, :, :], x_mid[0][:, :, :])
            dve.wait_ge(*logits_done(i, 1))
            chain(dve.tensor_copy(logit[:, :, :], SCORE[0][1][:, 0:NT * NE].rearrange("p (t e) -> p t e", t=NT)))
            yield 0.6
            rank_of(dve, chain, logit[:, :, :], NE, before, cmp_a[:, :, :], cmp_b[:, :, :], rank[:, :, :])
            dve.tensor_scalar(first[:, :, :], rank[:, :, :], 0.0, None, ALU.is_equal)
            chain(dve.tensor_scalar(second[:, :, :], rank[:, :, :], 1.0, None, ALU.is_equal))
            dve.tensor_tensor(comb[:, :, :], first[:, :, :], second[:, :, :], ALU.add)
            chain(dve.tensor_tensor(first[:, :, :], first[:, :, :], second[:, :, :], ALU.subtract))
            chain(dve.tensor_tensor(second[:, :, :], first[:, :, :], logit[:, :, :], ALU.mult))
            dve.tensor_reduce(gap[:, :], second[:, :, :], AX.X, ALU.add).then_inc(gap_ready.sem, 1)
            for c in range(NCH):
                yield chunk_at(c) + 0.2
                dve.wait_ge(*tanh_done(i, c + 1))
                dve.scalar_tensor_tensor(out=tanh_g[:, c % 2, :], in0=tanh_g[:, c % 2, :], scalar=1.0,
                                         in1=GU[c % 2][:, 0:T], op0=ALU.add, op1=ALU.mult)\
                   .then_inc(product_done.sem, 1)
                dve.wait_ge(*product_done(i, c + 1))
                dve.tensor_tensor(hidden[:, c % 2, :], tanh_g[:, c % 2, :], GU[c % 2][:, T:2 * T], ALU.mult)\
                   .then_inc(hidden_ready.sem, 1)
                if c == 2:
                    dve.wait_ge(*tanh_ready(i, 1))
                    chain(dve.tensor_tensor(first[:, :, :], first[:, :, :],
                                            tgap[:, :].unsqueeze(2).to_broadcast([P, NT, NE]), ALU.mult))
                    chain(dve.tensor_tensor(comb[:, :, :], comb[:, :, :], first[:, :, :], ALU.add))
                    chain(dve.tensor_scalar(comb[:, :, :], comb[:, :, :], 0.25, None, ALU.mult))
                if c % CH == 0 and c >= CH:
                    yield chunk_at(c) + 0.4
                    dve_expert(dve, i, c // CH - 1)
            yield chunk_at(NCH - 1) + 1
            dve_expert(dve, i, NE - 1)
            dve.wait_ge(*expert_added(i, NE))
            dve.wait_ge(*rows_g_loaded(i, 16))
            chain(dve.tensor_tensor(acc[:, :, :], acc[:, :, :], rows_g[:, 0:1, :].to_broadcast([P, NT, P]), ALU.mult))
            dve.tensor_tensor(x_b[:, :, :], acc[:, :, :], x_keep[:, :, :], ALU.add).then_inc(x_b_ready.sem, 1)
            chain.done()

        def dve_expert(dve, i, e):
            dve.wait_ge(*expert_done(i, e + 1))
            if e >= 1:
                dve.wait_ge(*expert_added(i, e))
            for t in range(NT):
                last = dve.scalar_tensor_tensor(out=acc[:, t, :], in0=BOUT[:, t * P:(t + 1) * P],
                                                scalar=comb[:, t, e:e + 1],
                                                in1=(h2 if e == 0 else acc)[:, t, :], op0=ALU.mult, op1=ALU.add)
            last.then_inc(expert_added.sem, 1)

        def dve_c(dve, i):
            chain = Chain(dve, dve_self["c"], i)
            yield from dve_start(dve, i, 1, chain)
            for u in range(NU):
                if u == 6:
                    yield values_at(1, 1) + 0.3
                    dve_take_values(dve, i, 1, 0)
                yield ROOT_AT[u // RING] + 0.1 + 0.2 * (u % RING)
                dve.wait_ge(*rooted(i, u + 1))
                dve.tensor_tensor(probs[1][:, u % RING, :], probs[1][:, u % RING, :], ratio[:, u % RING, :], ALU.mult)\
                   .then_inc(ratio_done.sem, 1)
            yield from dve_gather(dve, i, 1, chain)
            chain.done()
            chain = Chain(dve, dve_self["d"], i)
            small, both = SCORE[1][0], SCORE[1][1][:, :].rearrange("p (t c) -> p t c", t=NT)
            yield FFN1_AT
            dve.wait_ge(*x_mid_ready[1](i, 1))
            dve_stats(dve, i, "d", x_mid[1], chain)
            yield FFN1_AT + 0.7
            dve_norm(dve, i, "d", x_mid[1])
            yield FFN1_AT + 1.8
            dve.wait_ge(*ffn1_done(i, 1))
            dve.tensor_tensor(pj[:, :, :], both[:, :, P:P + PROJ],
                              bp_row[:, :].unsqueeze(1).to_broadcast([P, NT, PROJ]), ALU.add)\
               .then_inc(pj_ready.sem, 1)
            dve.wait_ge(*pj_ready(i, 1))
            chain(dve.tensor_tensor(pjsq[:, :, :], pj[:, :, :], pj[:, :, :], ALU.mult))
            chain(dve.tensor_reduce(pj_ss[:, :], pjsq[:, :, :], AX.X, ALU.add))
            dve.tensor_scalar(pj_ss[:, :], pj_ss[:, :], 1e-24, None, ALU.max).then_inc(pjss_ready.sem, 1)
            yield FFN1_AT + 3.3
            dve.wait_ge(*pjinv_ready(i, 1))
            dve.wait_ge(*lg4_done(i, 1))
            chain(dve.tensor_tensor(lg4[:, :, :], small[:, T:T + NT * NR].rearrange("p (t e) -> p t e", t=NT),
                                    pj_inv[:, :].unsqueeze(2).to_broadcast([P, NT, NR]), ALU.mult))
            chain(dve.tensor_reduce(st4[:, 0, :], lg4[:, :, :], AX.X, ALU.max))
            dve.tensor_tensor(lg4[:, :, :], lg4[:, :, :], st4[:, 0, :].unsqueeze(2).to_broadcast([P, NT, NR]),
                              ALU.subtract).then_inc(lg4_shifted.sem, 1)
            dve.wait_ge(*lg4_shifted(i, 1))
            yield FFN1_AT + 3.7
            rank_of(dve, chain, lg4[:, :, :], NR, before4, cmp4_a[:, :, :], cmp4_b[:, :, :], rank4[:, :, :])
            yield FFN1_AT + 4.5
            dve.tensor_scalar(ret[:, :, :], rank4[:, :, :], 0.0, None, ALU.is_equal)
            dve.wait_ge(*exp4_ready(i, 1))
            chain(dve.tensor_reduce(st4[:, 1, :], ex4[:, :, :], AX.X, ALU.add))
            chain(dve.reciprocal(st4[:, 2, :], st4[:, 1, :]))
            chain(dve.tensor_tensor(ret[:, :, :], ret[:, :, :], ex4[:, :, :], ALU.mult))
            chain(dve.tensor_tensor(ret[:, :, :], ret[:, :, :],
                                    st4[:, 2, :].unsqueeze(2).to_broadcast([P, NT, NR]), ALU.mult))
            at = 0
            for k, r in enumerate(RANKS):
                last = dve.tensor_tensor(dr[:, :, at:at + r], both[:, :, P + PROJ + at:P + PROJ + at + r],
                                         ret[:, :, k:k + 1].to_broadcast([P, NT, r]), ALU.mult)
                at += r
            last.then_inc(dr_ready.sem, 1)
            yield FFN1_AT + 6.1
            dve.wait_ge(*ffn1_out(i, 1))
            chain(dve.tensor_tensor(xn[1][:, :, :], both[:, :, 0:P], rows_c[:, 1:2, :].to_broadcast([P, NT, P]),
                                    ALU.mult))
            dve.wait_ge(*x_stored.before(i, 16))
            dve.tensor_tensor(x_out[:, :, :], xn[1][:, :, :], x_mid[1][:, :, :], ALU.add)\
               .then_inc(x_out_ready.sem, 1)
            chain.done()

        @block.vector
        def _(dve):
            steps = [0]

            def step(ins):
                steps[0] += 1
                ins.then_inc(prep["dve"], 1)
                dve.wait_ge(prep["dve"], steps[0])

            for user in (x_mid_ready[0], x_b_ready, x_out_ready, var_ready["mix"], pv_copied[1]):
                dve.sem_inc(user.sem, user.per * user.ahead)
            dve.wait_ge(loads["small"], 80)
            dve.tensor_scalar(simst[:, 1:2], tempc[:, :], CLAMP_MAX, None, ALU.min).then_inc(prep["temp"], 1)
            step(dve.tensor_tensor(simsq[:, :], simt[:, :], simt[:, :], ALU.mult))
            step(dve.tensor_reduce(simst[:, 0:1], simsq[:, :], AX.X, ALU.add))
            dve.tensor_scalar(simst[:, 0:1], simst[:, 0:1], 1e-24, None, ALU.max).then_inc(prep["simss"], 1)
            dve.wait_ge(loads["attn"], 32)
            uq = u2[:, 0:2, :, :].rearrange("p n h d -> p (n h) d")
            dve.tensor_scalar(uq[:, :, 8:12:2], uq[:, :, 5:8:2], -1.0, None, ALU.mult)
            dve.tensor_copy(uq[:, :, 9:12:2], uq[:, :, 4:8:2]).then_inc(prep["u2"], 1)
            dve.wait_ge(prep["modcols_pe"], 1)
            cols = modcols[:, :, :, :].rearrange("p b l m -> p (l m) b")
            step(dve.tensor_copy(cols, bank[0][:, 0:12 * B].rearrange("p (m b) -> p m b", b=B)))
            ones = modcols[:, :, :, :].rearrange("p b l m -> p (b l) m")[:, :, 1:5:3]
            dve.tensor_scalar(ones, ones, 1.0, None, ALU.add).then_inc(prep["modcols"], 1)
            dve.wait_ge(prep["modrows_pe"], 1)
            for l in range(2):
                dve.tensor_copy(modrow[:, l, 0:4, :].rearrange("b m c -> b (m c)"), bank[1 + 2 * l][0:B, :])
                last = dve.tensor_copy(modrow[:, l, 4:6, :].rearrange("b m c -> b (m c)"),
                                       bank[2 + 2 * l][0:B, 0:256])
            step(last)
            dve.memset(BV[:, :], 0.0)
            gates = modrow[:, :, 2:6:3, :]
            step(dve.tensor_scalar(gate_s[:, :, :, :], gates, 0.0, 2.0, ALU.is_ge, ALU.mult))
            dve.tensor_scalar(gate_s[:, :, :, :], gate_s[:, :, :, :], -1.0, None, ALU.add)
            for l in range(2):
                last = dve.scalar_tensor_tensor(out=gate_m[:, l, :, :], in0=gates[:, l, :, :], scalar=-1.0,
                                                in1=gates[:, l, :, :], op0=ALU.mult, op1=ALU.max)
            step(last)
            step(dve.tensor_scalar(gate_m[:, :, :, :], gate_m[:, :, :, :], 0.25, None, ALU.max))
            for l in range(2):
                dve.tensor_tensor(rowmods[:, 4 * l:4 * l + 2, :], gate_s[:, l, :, :], gate_m[:, l, :, :], ALU.mult)
            dve.tensor_copy(rowmods[:, 2, :], modrow[:, 0, 3, :])
            dve.tensor_scalar(rowmods[:, 3, :], modrow[:, 0, 4, :], 1.0, None, ALU.add).then_inc(prep["rows"], 1)
            dve.wait_ge(prep["weff_pe"], 1)
            for n in range(3):
                src = bank[5 + n][:, 0:192].rearrange("p (h d) -> p h d", d=12)
                last = dve.tensor_copy(w_qkv0[:, n * P:(n + 1) * P].rearrange("p (h d) -> p h d", d=D),
                                       src[:, :, 0:D])
                if n < 2:
                    last = dve.tensor_copy(w_qkv0[:, 384 + 64 * n:448 + 64 * n]
                                           .rearrange("p (h d) -> p h d", d=DE), src[:, :, D:12])
            last.then_inc(prep["wqkv0"], 1)
            dve.tensor_scalar(w_qkv1[:, 0:P], w_qkv1[:, 0:P], SCALE, None, ALU.mult).then_inc(prep["wqkv1"], 1)
            for k in range(3):
                step(dve.tensor_copy(slope_p[:, k, :], (slope if k == 0 else slope_r)[:, :]))
                if k < 2:
                    step(dve.tensor_tensor(slope_r[:, :], (slope if k == 0 else slope_r)[:, :],
                                           slope_p[:, k, :], ALU.subtract))
            dve.wait_ge(prep["cleared"], 1)
            parts = slope_p[:, :, :].rearrange("p k h -> p h k")
            for t in range(NT):
                q, k = stack[1][:, t, 0:H, :], stack[1][:, t, H:2 * H, :]
                pos = position[:, t:t + 1].unsqueeze(2).to_broadcast([P, H, 3])
                dve.tensor_scalar(q[:, :, ALIBI:ALIBI + 3], pos, -1.0, None, ALU.mult)
                dve.tensor_copy(q[:, :, ALIBI + 3:ALIBI + 6], parts)
                dve.tensor_copy(k[:, :, ALIBI:ALIBI + 3], parts)
                last = dve.tensor_copy(k[:, :, ALIBI + 3:ALIBI + 6], pos)
            last.then_inc(prep["stack1"], 1)
            dve.wait_ge(prep["siminv"], 1)
            dve.wait_ge(prep["exptemp"], 1)
            dve.tensor_scalar(simt[:, :], simt[:, :], simst[:, 3:4], simst[:, 2:3], ALU.mult, ALU.mult)\
                .then_inc(prep["simt"], 1)
            dve.wait_ge(prep["simn_pe"], 1)
            dve.tensor_copy(simn[:, :], bank[0][0:PROJ, 0:NR]).then_inc(prep["simn"], 1)
            piece = NCH // NQ
            for k in range(NQ):
                dve.wait_ge(prep["hi"], k + 1)
                rows = slice(k * piece, (k + 1) * piece)
                for n in range(2):
                    last = dve.tensor_tensor(gu_lo[:, n, rows, :], stage[:, k % 2, n, :, :],
                                             gu_hi[:, n, rows, :].bitcast(F32), ALU.subtract)
                last.then_inc(prep["lo"], 1)
            dve.wait_ge(loads["const"], 80)
            dve.wait_ge(loads["ffn"], 11 * 16)
            rounds(dve, dve_a, dve_k, dve_c)


def constants():
    def bf(x):
        return (np.ascontiguousarray(x, np.float32).view(np.uint32) >> 16).astype(np.uint16)

    r = np.arange(P)
    mask = np.zeros((P, 2, P), np.float32)
    mask[:, 0] = np.where(r[None, :] > r[:, None], MASKED, 0)
    mask[:, 1] = np.where(r[:, None] > r[None, :], MASKED, 0)
    sel = np.zeros((P, H), np.float32)
    for h in range(H):
        sel[[h, H + h], h] = 1
    inv = (1.0 / np.float32(10000.0) ** (np.arange(0, DE, 2, dtype=np.float32) / np.float32(DE))).astype(np.float32)
    f = np.arange(T, dtype=np.float32)[:, None] * inv[None, :]
    f = np.concatenate([f, f], -1).astype(np.float32)
    rope = np.stack([np.cos(f), np.sin(f)]).astype(np.float32).reshape(2, NT, P, DE).transpose(2, 0, 1, 3)
    tri = [np.broadcast_to((np.arange(n)[None, :] < np.arange(n)[:, None]).astype(np.float32).reshape(1, -1),
                           (P, n * n)) for n in (NE, NR)]
    return {"identf": np.eye(P, dtype=np.float32), "identb": bf(np.eye(P)), "maskb": bf(mask),
            "selb": bf(sel), "rope": rope, "before": tri[0], "before4": tri[1],
            "position": (np.arange(T, dtype=np.float32) - P).reshape(NT, P).T}


def kernel(**inputs):
    import concourse.bacc as bacc
    from concourse.bass_utils import run_bass_kernel_spmd

    w = {k: np.asarray(v) for k, v in inputs.items()}
    arrays = dict(constants())
    for l in range(2):
        arrays[f"L{l}_c"] = w[f"L{l}_c"].T
        arrays[f"L{l}_wmod"] = w[f"L{l}_wmod"]
    u2 = np.zeros((P, 3, 2, 12), np.float32)
    for n, parts in enumerate((("Wq_up_c", "Wq_up_e"), ("Wk_up_c", "Wk_up_e"), ("Wv_up",))):
        up = np.concatenate([w["L0_attn_" + p] for p in parts], 1)
        for h in range(2):
            u2[L * h:L * (h + 1), n, h, 0:D] = up
    arrays["u2"] = u2
    arrays["wd3"] = np.stack([w[f"L0_attn_W{x}_down"].reshape(P, NPAIR, 2 * L).transpose(2, 1, 0)
                              for x in "qkv"], 1)
    arrays["L0_attn_Wc"] = w["L0_attn_Wc"]
    arrays["L0_attn_x"] = w["L0_attn_x"]
    for name in ("L1_attn_w_qkv", "L1_attn_w_out", "L0_ffn_attn_w", "L0_ffn_gate_w", "L1_ffn_sim"):
        arrays[name] = w[name].T
    arrays["L1_attn_alibi_slopes"] = w["L1_attn_alibi_slopes"]
    arrays["L1_ffn_temp"] = w["L1_ffn_temp"]
    arrays["L1_ffn_bp"] = w["L1_ffn_bp"]
    arrays["lncol"] = np.stack([w["L0_ffn_" + k] for k in ("ln1_g", "ln1_b", "ln2_g", "ln2_b")], 1)
    arrays["gu"] = np.stack([w[f"L0_ffn_{k}_proj"].reshape(NCH * P, P).T.reshape(P, NCH, P)
                             for k in ("gate", "up")], 1)
    arrays["L0_ffn_down_proj"] = w["L0_ffn_down_proj"].reshape(NE, P, CH, P).transpose(3, 0, 2, 1)        .reshape(P, NCH, P)
    arrays["w_ffn1"] = np.concatenate([w["L1_ffn_W"].T, w["L1_ffn_Wp"].T]
                                      + [w[f"L1_ffn_Wd{k}"].T for k in range(NR)], 1)
    arrays["w_up1"] = np.concatenate([w[f"L1_ffn_Wu{k}"].T for k in range(NR)], 0)

    nc = bacc.Bacc("TRN2", target_bir_lowering=False, num_devices=1)
    fed, aps = {}, {}
    for name, x in arrays.items():
        x = np.ascontiguousarray(x)
        fed["in_" + name] = x
        aps[name] = nc.dram_tensor("in_" + name, x.shape, mybir.dt.from_np(x.dtype), kind="ExternalInput").ap()
    aps["scratch"] = nc.dram_tensor("scratch", (B, ROWMODS, P), F32, kind="Internal").ap()
    out = nc.dram_tensor("out_0", (B, T, P), F32, kind="ExternalOutput").ap()
    build(nc, aps, out)
    return run_bass_kernel_spmd(nc, [fed], core_ids=[0]).results[0]["out_0"]
```

```python
import math
from contextlib import ExitStack

import numpy as np

import concourse.bass as bass
from concourse import mybir

F32 = mybir.dt.float32
F32R = mybir.dt.float32r
BF16 = mybir.dt.bfloat16
ALU = mybir.AluOpType
ACT = mybir.ActivationFunctionType
AX = mybir.AxisListType

P = 128
B, T = 16, 256
NT = T // P
H, D = 16, 8
DE = D // 2
L = 64
NPAIR = H // 2
ROWS = 64
SLOTS = 6
ALIBI = SLOTS * D
NE, NI = 8, 512
CH = NI // P
NCH = NE * CH
NQ = 16
NR = 4
RANKS = [1, 2, 4, 8]
RTOT = sum(RANKS)
PROJ = 32
SCALE = 1.0 / math.sqrt(D)
VW = 32
MASKED = -1e30
ROWMODS = 6
EPS_LN = 1e-5
EPS_RATIONAL = 1e-6
CLAMP_MAX = float(np.log(1.0 / 0.01))


class Signal:

    def __init__(self, ctx, nc, name, per, ahead):
        self.sem, self.per, self.ahead = ctx.enter_context(nc.semaphore(name)), per, ahead

    def __call__(self, i, n):
        base, plus = i
        return self.sem, base * self.per + (n + self.per * (self.ahead + plus))

    def before(self, i, n):
        base, plus = i
        assert self.ahead
        return self.sem, base * self.per + (n + self.per * (self.ahead + plus - 1))


class Chain:

    def __init__(self, eng, steps, i):
        self.eng, self.steps, self.i, self.n = eng, steps, i, 0

    def __call__(self, ins):
        self.n += 1
        ins.then_inc(self.steps.sem, 1)

    def wait(self):
        self.eng.wait_ge(*self.steps(self.i, self.n))

    def done(self):
        assert self.n == self.steps.per, (self.n, self.steps.per)


TENSOR_ORDER = (
    "KKACAACCKKKKCCKKCCKKCCCKCKCKCKKKKKAAKKAACCKKAAKCKACCACKACAKCAKAKAKAAAKAKAAKAAKAKAKKACAKAKACK"
    "AKCACKKACAACKKAKKAACKKAKACKKKCCKKKKKKKAKAKKCCKKAA"
)
VECTOR_ORDER = (
    "KKACAKKKCKAKKCKKKKKKKKAACCCKCACCCCCCCCCKKKACKKKKCAAKKKAAAKAKAKAAKKKACAKCKKCAKKAKKAKAKAKAKKAA"
    "KAKAAAKAAAAAKCCKKKKKCKKCKKKCKKCCCACCCKKKCKCCCAKCKAKAAAKKKAKACAKACKCCKAACKAAKACCKKCKCCKACCCKC"
    "CCKCCAKAKAKKCAKKCK"
)
SCALAR_ORDER = (
    "KACKKAACCKKCKCKCCCCCCCKCCCCKCKCCCCAKKCCACCCKCCKCCCCCCKCCKCAKAAKACCCKAACCKACAKAKAKACAAKKCKAKK"
    "CKKKCAKKCA"
)
GPSIMD_ORDER = (
    "AACCCCCCCCCCCCCCCCCCCCCACAA"
)


def interleave(order, streams):
    for steps in streams.values():
        next(steps)
    for letter in order:
        if letter in streams:
            next(streams[letter], None)
    for steps in streams.values():
        assert next(steps, "end") == "end"


def build(nc, a, out):
    with ExitStack() as ctx:
        def sb(name, shape, dt=F32):
            return ctx.enter_context(nc.sbuf_tensor(name, shape, dt))

        def sem(name):
            return ctx.enter_context(nc.semaphore(name))

        def signal(name, per=1, ahead=0):
            return Signal(ctx, nc, name, per, ahead)

        identf = sb("identf", [P, P])
        identb = sb("identb", [P, P], BF16)
        maskb = sb("maskb", [P, 2, P], BF16)
        selb = sb("selb", [P, H], BF16)
        rope = sb("rope", [P, 2, NT, DE])
        before = sb("before", [P, NE * NE])
        before4 = sb("before4", [P, NR * NR])
        position = sb("position", [P, NT])
        w_qkv0 = sb("w_qkv0", [P, 512])
        w_qkv1 = sb("w_qkv1", [P, 384])
        w_o = [sb("w_o0", [P, P]), sb("w_o1", [P, P])]
        w_mix = sb("w_mix", [P, P])
        w_gate = sb("w_gate", [P, NE])
        gu_hi = sb("gu_hi", [P, 2, NCH, P], F32R)
        gu_lo = sb("gu_lo", [P, 2, NCH, P], F32R)
        w_down = sb("w_down", [P, NCH, P])
        lncol = sb("lncol", [P, 4])
        w_ffn1 = sb("w_ffn1", [P, P + PROJ + RTOT])
        w_up1 = sb("w_up1", [RTOT, P])
        bp_row = sb("bp_row", [P, PROJ])
        simn = sb("simn", [PROJ, NR])
        modcols = sb("modcols", [P, B, 2, 6])
        minus_half = sb("minus_half", [P, NT])

        NU = 12
        RING = 6
        probs = [sb(f"probs{n}", [P, RING, 512]) for n in range(2)]
        ratio = sb("ratio", [P, RING, 512])

        wd3 = probs[0][:, :, :].rearrange("p u (g c) -> p (u g) c", c=P)\
            .rearrange("p (n g) c -> p n g c", n=3)
        stage = probs[1][:, 0:2, :].rearrange("p u (g c) -> p (u g) c", c=P)\
            .rearrange("p (k n g) c -> p k n g c", k=2, n=2)
        modrow = probs[1][0:B, 2:5, :].rearrange("b u (g c) -> b (u g) c", c=P)\
            .rearrange("b (l m) c -> b l m c", l=2)
        gate_s = probs[1][0:B, 5, :].rearrange("b (l m c) -> b l m c", l=2, c=P)
        wmod = ratio[:, 0:3, :].rearrange("p u (g c) -> p (u g) c", c=P)\
            .rearrange("p (l m) c -> p l (m c)", l=2)
        rowmods = ratio[0:B, 3:5, :].rearrange("b u (g c) -> b (u g) c", c=P)[:, 0:ROWMODS, :]
        gate_m = ratio[0:B, 5, :].rearrange("b (l m c) -> b l m c", l=2, c=P)
        u2 = sb("u2", [P, 3, 2, 12])
        c_t = sb("c_t", [P, 2, B])
        silu_c = sb("silu_c", [P, 2, B])
        slope = sb("slope", [P, H])
        slope_r = sb("slope_r", [P, H])
        slope_p = sb("slope_p", [P, 3, H], BF16)
        simt = sb("simt", [NR, PROJ])
        simsq = sb("simsq", [NR, PROJ])
        simst = sb("simst", [NR, 4])
        tempc = sb("tempc", [NR, 1])

        def two(name, shape, dt=F32):
            return [sb(f"{name}{n}", shape, dt) for n in range(2)]

        x_in = sb("x_in", [P, NT, P])
        x_mid = [sb("x_a", [P, NT, P]), sb("x_c", [P, NT, P])]
        x_keep = sb("x_keep", [P, NT, P])
        x_b = sb("x_b", [P, NT, P])
        x_out = sb("x_out", [P, NT, P])
        rows_a = sb("rows_a", [P, 1, P])
        rows_g = sb("rows_g", [P, 1, P])
        rows_b = sb("rows_b", [P, 2, P])
        rows_c = sb("rows_c", [P, 2, P])
        cols_now = two("cols_now", [P, 6])
        stats = two("stats", [P, NT, 6])
        meanvar = two("meanvar", [P, NT, 2])
        vareps = two("vareps", [P, NT])
        rstd = two("rstd", [P, NT])
        xn = two("xn", [P, NT, P])
        h_t = two("h_t", [P, T])
        y_n = [h_t[n][:, :].rearrange("p (t c) -> p t c", t=NT) for n in range(2)]
        raw = two("raw", [P, NT, 512])
        y_t = [raw[n][:, :, :].rearrange("p t (g c) -> p (t g) c", g=2) for n in range(2)]
        rot = sb("rot", [P, NT, 2 * H, DE])
        v_aug = [sb("v_aug0", [P, NT, H, D + 1]), sb("v_aug1", [P, NT, H, VW])]
        stack = two("stack", [P, NT, 2 * H, ROWS], BF16)
        q_t = two("q_t", [P, NPAIR, 2, T], BF16)
        k_t = two("k_t", [P, NPAIR, T], BF16)
        negmax = sb("negmax", [P, NT, H])
        negmax_r = sb("negmax_r", [P, NT, H])
        max_stack = sb("max_stack", [P, NT, P], BF16)
        max_t = sb("max_t", [P, T], BF16)
        den = two("den", [P, NT, H])
        y_nt = two("y_nt", [P, T])
        h_ffn = y_nt[0][:, :].rearrange("p (t c) -> p t c", t=NT)
        h2 = sb("h2", [P, NT, P])
        tt = rot[:, :, :, :].rearrange("p t h d -> p (t h d)")
        tt_hi = sb("tt_hi", [P, T], F32R)
        tt_lo = sb("tt_lo", [P, T], F32R)
        logit = sb("logit", [P, NT, NE])
        cmp_a = sb("cmp_a", [P, NT, NE * NE])
        cmp_b = sb("cmp_b", [P, NT, NE * NE])
        rank = sb("rank", [P, NT, NE])
        first = sb("first", [P, NT, NE])
        second = sb("second", [P, NT, NE])
        gap = sb("gap", [P, NT])
        tgap = sb("tgap", [P, NT])
        comb = sb("comb", [P, NT, NE])
        tanh_g = sb("tanh_g", [P, 2, T])
        hidden = sb("hidden", [P, 2, T])
        acc = sb("acc", [P, NT, P])
        pj = sb("pj", [P, NT, PROJ])
        pjsq = sb("pjsq", [P, NT, PROJ])
        pj_ss = sb("pj_ss", [P, NT])
        pj_inv = sb("pj_inv", [P, NT])
        pj_t = y_nt[1][0:PROJ, :]
        lg4 = sb("lg4", [P, NT, NR])
        ex4 = sb("ex4", [P, NT, NR])
        cmp4_a = sb("cmp4_a", [P, NT, NR * NR])
        cmp4_b = sb("cmp4_b", [P, NT, NR * NR])
        rank4 = sb("rank4", [P, NT, NR])
        st4 = sb("st4", [P, 3, NT])
        ret = sb("ret", [P, NT, NR])
        dr = sb("dr", [P, NT, RTOT])
        dr_t = y_nt[1][0:RTOT, :]

        bank = [ctx.enter_context(nc.psum_tensor(f"bank{n}", [P, 512], F32)) for n in range(8)]
        SCORE = [bank[0:2], bank[2:4]]
        BV = [bank[4], bank[3]]
        GU = bank[5:7]
        BOUT = bank[7]

        loads = {n: sem("ld_" + n) for n in ("const", "mod", "attn", "gu0", "gu1", "ffn", "small")}
        prep = {n: sem("prep_" + n) for n in (
            "silu", "temp", "exptemp", "u2", "simss", "siminv", "modcols_pe", "modcols", "modrows_pe", "rows",
            "weff_pe", "wqkv0", "wqkv1", "cleared", "stack1", "hi", "lo", "simt", "simn_pe",
            "simn", "dve", "pool")}
        scratch_written = sem("scratch_written")

        passed = {e: sem("passed_" + e) for e in ("pool", "dve")}

        x_loaded = signal("x_loaded", 16)
        rows_a_loaded = signal("rows_a_loaded", 16)
        rows_b_loaded = signal("rows_b_loaded", 16)
        rows_g_loaded = signal("rows_g_loaded", 16)
        rows_c_loaded = signal("rows_c_loaded", 16)
        x_stored = signal("x_stored", 16, ahead=1)
        SITES = {"a": 0, "b": 0, "mix": 0, "moe": 0, "c": 1, "d": 1}
        var_ready = {s: signal("var_" + s, 1, int(s == "mix")) for s in SITES}
        rstd_ready = {s: signal("rstd_" + s) for s in SITES}
        xn_ready = {s: signal("xn_" + s) for s in SITES}
        xt_ready = {s: signal("xt_" + s) for s in SITES if s != "b"}
        h_ready = {s: signal("h_" + s, 1, int(s in "ad")) for s in SITES if s != "b"}
        pool_self = {s: signal("pself_" + s) for s in SITES}
        dve_self = {p: signal("dself_" + p, n) for p, n in
                    (("a", 11), ("head", 6), ("k", 14), ("c", 9), ("d", 15))}

        def pair(name, per=1, ahead=(0, 0)):
            return [signal(f"{name}{n}", per, ahead[n]) for n in range(2)]

        cols_ready = pair("cols_ready")
        qkv_done = pair("qkv_done", NT)
        qkv_copied = pair("qkv_copied", NT)
        parts_ready = pair("parts_ready")
        stack_ready = pair("stack_ready")
        spread_done = pair("spread_done", 4)
        k_spread = pair("k_spread", NT)
        q_spread = pair("q_spread", NT)
        maxscore_done = signal("maxscore_done", NU)
        max_taken = signal("max_taken", NU)
        max_stacked = signal("max_stacked")
        max_turned = signal("max_turned")
        max_ready = signal("max_ready")
        score_done = pair("score_done", NU)
        taken = signal("taken", NU)
        squared = signal("squared", NU)
        rooted = signal("rooted", NU)
        ratio_done = pair("ratio_done", NU // 2)
        lifted = signal("lifted", NU)
        probs_ready = pair("probs_ready", NU)
        pv_done = pair("pv_done", 2)
        pv_copied = pair("pv_copied", 2)
        y_back = pair("y_back", NT)
        y_ready = pair("y_ready")
        yt_done = pair("yt_done")
        yt_copied = pair("yt_copied")
        attn_out = pair("attn_out")
        x_mid_ready = [signal("x_a_ready", 1, ahead=1), signal("x_c_ready")]
        mix_done = signal("mix_done")
        parts_moe = signal("parts_moe")
        logits_done = signal("logits_done")
        gap_ready = signal("gap_ready")
        tanh_ready = signal("tanh_ready")
        gu_done = signal("gu_done", NCH)
        tanh_done = signal("tanh_done", NCH)
        product_done = signal("product_done", NCH)
        hidden_ready = signal("hidden_ready", NCH)
        expert_done = signal("expert_done", NE)
        expert_added = signal("expert_added", NE)
        x_b_ready = signal("x_b_ready", 1, ahead=1)
        ffn1_done = signal("ffn1_done")
        pj_ready = signal("pj_ready")
        pjss_ready = signal("pjss_ready")
        pjinv_ready = signal("pjinv_ready")
        pjt_done = signal("pjt_done")
        pjt_ready = signal("pjt_ready")
        lg4_done = signal("lg4_done")
        lg4_shifted = signal("lg4_shifted")
        exp4_ready = signal("exp4_ready")
        dr_ready = signal("dr_ready")
        drt_done = signal("drt_done")
        drt_ready = signal("drt_ready")
        ffn1_out = signal("ffn1_out")
        x_out_ready = signal("x_out_ready", 1, ahead=1)

        def score_bank(n, u):
            return SCORE[n][u % 2 if n == 0 or u < RING else 0]

        def rounds(eng, order, streams, weights=None):
            def one(base, letters):
                interleave(order, {x: streams[x](eng, (base, "CKA".index(x))) for x in letters if x in streams})

            first = {"A": streams["A"](eng, (-2, 2))}
            if weights is not None:
                first["K"] = weights(eng)
            interleave(order, first)
            one(-1, "KA")
            with eng.Fori(0, B - 2) as r:
                one(r, "KAC")
            one(B - 2, "KC")
            one(B - 1, "C")

        scratch = a["scratch"]
        block = ctx.enter_context(nc.Block())

        def load_x(sp, i):
            sp.wait_ge(*x_mid_ready[0].before(i, 1))
            sp.dma_start(x_in[:, :, :], a["L0_attn_x"][bass.ds(i[0] + i[1], 1)]
                         .rearrange("o (n p) c -> p (o n) c", p=P)).then_inc(x_loaded.sem, 16)

        def load_rows(sp, i, dst, lo, n, loaded, used):
            sp.wait_ge(*used.before(i, 1))
            sp.dma_start(dst[:, :, :].rearrange("p n c -> p (n c)"),
                         scratch[bass.ds(i[0] + i[1], 1), lo:lo + n, :]
                         .rearrange("o n c -> o (n c)").to_broadcast([P, n * P])).then_inc(loaded.sem, 16)

        def sp_round(sp, r, streams):
            if "C" in streams:
                load_rows(sp, (r, 0), rows_c, 4, 2, rows_c_loaded, x_out_ready)
            if "A" in streams:
                load_rows(sp, (r, 2), rows_a, 0, 1, rows_a_loaded, x_mid_ready[0])
                load_rows(sp, (r, 2), rows_b, 2, 2, rows_b_loaded, var_ready["mix"])
            if "K" in streams:
                load_rows(sp, (r, 1), rows_g, 1, 1, rows_g_loaded, x_b_ready)
            if "x" in streams:
                load_x(sp, (r, 3))
            if "C" in streams:
                sp.wait_ge(*x_out_ready((r, 0), 1))
                sp.dma_start(out[bass.ds(r, 1)].rearrange("o (n p) c -> p (o n) c", p=P),
                             x_out[:, :, :]).then_inc(x_stored.sem, 16)

        @block.sync
        def _(sp):
            for name, dst, src in (
                ("const", identf[:, :], a["identf"]), ("const", identb[:, :], a["identb"].bitcast(BF16)),
                ("mod", c_t[:, 0, :], a["L0_c"]), ("mod", c_t[:, 1, :], a["L1_c"]),
                ("mod", wmod[:, 0, :], a["L0_wmod"]), ("mod", wmod[:, 1, :], a["L1_wmod"]),
                ("attn", u2[:, :, :, :], a["u2"]), ("attn", wd3[:, :, :, :], a["wd3"]),
                ("const", maskb[:, :, :], a["maskb"].bitcast(BF16)), ("const", selb[:, :], a["selb"].bitcast(BF16)),
                ("const", rope[:, :, :, :], a["rope"]),
                ("small", slope[:, :], a["L1_attn_alibi_slopes"].partition_broadcast(P)),
                ("small", position[:, :], a["position"]), ("small", simt[:, :], a["L1_ffn_sim"]),
                ("small", tempc[:, :], a["L1_ffn_temp"].partition_broadcast(NR)),
                ("small", w_qkv1[:, :], a["L1_attn_w_qkv"]),
                ("ffn", w_o[0][:, :], a["L0_attn_Wc"]), ("ffn", w_o[1][:, :], a["L1_attn_w_out"]),
                ("ffn", w_mix[:, :], a["L0_ffn_attn_w"]), ("ffn", w_gate[:, :], a["L0_ffn_gate_w"]),
                ("ffn", lncol[:, :], a["lncol"]), ("ffn", before[:, :], a["before"]),
                ("ffn", before4[:, :], a["before4"]), ("ffn", w_ffn1[:, :], a["w_ffn1"]),
                ("ffn", w_up1[:, :], a["w_up1"]), ("ffn", bp_row[:, :], a["L1_ffn_bp"].partition_broadcast(P)),
                ("ffn", w_down[:, :, :], a["L0_ffn_down_proj"]),
            ):
                sp.dma_start(dst, src).then_inc(loads[name], 16)
            sp.sem_inc(x_stored.sem, 16)
            sp.wait_ge(prep["rows"], 1)
            sp.dma_start(scratch, rowmods[:, :, :]).then_inc(scratch_written, 16)
            sp.wait_ge(scratch_written, 16)
            load_x(sp, (-2, 2))
            sp_round(sp, -2, "Ax")
            sp_round(sp, -1, "AKx")
            with sp.Fori(0, B - 3) as r:
                sp_round(sp, r, "AKCx")
            sp_round(sp, B - 3, "AKC")
            sp_round(sp, B - 2, "KC")
            sp_round(sp, B - 1, "C")
            sp.wait_ge(*x_stored((B - 1, 0), 16))

        def pool_cols(pool, i, n):
            pool.wait_ge(*h_ready["ad"[n]].before(i, 1))
            pool.sem_inc(passed["pool"], 1)
            pool.tensor_copy(cols_now[n][:, :], modcols[:, bass.ds(i[0] + i[1], 1), n, :]
                             .rearrange("p o m -> p (o m)")).then_inc(cols_ready[n].sem, 1)

        def pool_rstd(pool, i, s):
            n = SITES[s]
            pool.wait_ge(*var_ready[s](i, 1))
            pool.sem_inc(passed["pool"], 1)
            pool.tensor_scalar(vareps[n][:, :], meanvar[n][:, :, 1], EPS_LN, None, ALU.add)\
                .then_inc(pool_self[s].sem, 1)
            pool.wait_ge(*pool_self[s](i, 1))
            pool.tensor_tensor(rstd[n][:, :], vareps[n][:, :], minus_half[:, :], ALU.pow)\
                .then_inc(rstd_ready[s].sem, 1)

        def pool_a(pool, i):
            yield
            pool_cols(pool, i, 0)
            yield
            pool_rstd(pool, i, "a")
            for k, s in enumerate(("b", "mix", "moe")):
                yield
                pool_rstd(pool, i, s)

        def pool_c(pool, i):
            yield
            pool_cols(pool, i, 1)
            yield
            pool_rstd(pool, i, "c")
            for u in range(NU):
                if u % 2 == 0:
                    yield
                    pool.wait_ge(*rooted(i, u + 2))
                    pool.tensor_tensor(probs[1][:, (u + 1) % RING, :], probs[1][:, (u + 1) % RING, :],
                                       ratio[:, (u + 1) % RING, :], ALU.mult).then_inc(ratio_done[1].sem, 1)
                yield
                pool.wait_ge(*lifted(i, u + 1))
                pool.sem_inc(passed["pool"], 1)
                heads, cols = (2, 256) if u % 3 < 2 else (4, 128)
                v = probs[1][:, u % RING, :].rearrange("p (h q) -> p h q", h=heads)[:, :, 0:P]
                pool.affine_select(out=v, in_=v, compare_op=ALU.is_ge, fill=0.0, base=0,
                                   pattern=[[0, heads], [1, P]], channel_multiplier=-1)\
                    .then_inc(probs_ready[1].sem, 1)
            yield
            pool_rstd(pool, i, "d")
            yield
            pool.wait_ge(*pjss_ready(i, 1))
            pool.tensor_tensor(pj_inv[:, :], pj_ss[:, :], minus_half[:, :], ALU.pow)\
                .then_inc(pjinv_ready.sem, 1)

        @block.gpsimd
        def _(pool):
            steps = [0]

            def step(ins):
                steps[0] += 1
                ins.then_inc(prep["pool"], 1)
                pool.wait_ge(prep["pool"], steps[0])

            step(pool.memset(minus_half[:, :], -0.5))
            for n in range(2):
                pool.memset(stack[n][:, :, :, :], 0.0)
            pool.memset(max_stack[:, :, :], 0.0)
            for n in range(2):
                pool.memset(q_t[n][:, :, :, :], 0.0)
                last = pool.memset(v_aug[n][:, :, :, :], 0.0)
            step(last)
            for n in range(2):
                last = pool.memset(v_aug[n][:, :, :, D:D + 1], 1.0)
            last.then_inc(prep["cleared"], 1)
            pool.wait_ge(prep["simss"], 1)
            pool.tensor_tensor(simst[:, 3:4], simst[:, 0:1], minus_half[0:NR, 0:1], ALU.pow)\
                .then_inc(prep["siminv"], 1)
            pool.wait_ge(prep["modcols"], 1)
            rounds(pool, GPSIMD_ORDER, {"A": pool_a, "C": pool_c})

        def act_turned(act, i, s, src, scale, bias, dst):
            act.wait_ge(*xt_ready[s](i, 1))
            act.activation(dst, src, ACT.Identity, scale=scale, bias=bias).then_inc(h_ready[s].sem, 1)

        def act_qkv(act, i, n):
            for t in range(NT):
                if t:
                    yield
                act.wait_ge(*qkv_done[n](i, t + 1))
                src = SCORE[n][t]
                act.activation(raw[n][:, t, 0:256], src[:, 0:256], ACT.Copy)
                if n == 0:
                    act.activation(raw[0][:, t, 384:512], src[:, 384:512], ACT.Copy)
                act.activation(v_aug[n][:, t, :, 0:D], src[:, 256:384].rearrange("p (h d) -> p h d", h=H),
                               ACT.Copy).then_inc(qkv_copied[n].sem, 1)

        def act_keys(act, i, n, t):
            act.wait_ge(*spread_done[n](i, 2 * t + 1))
            act.activation(k_t[n][:, :, t * P:(t + 1) * P],
                           SCORE[n][0][:, :].bitcast(BF16).rearrange("p (g q) -> p g q", g=NPAIR),
                           ACT.Copy).then_inc(k_spread[n].sem, 1)

        def act_start(act, i, n):
            yield
            act.wait_ge(*cols_ready[n](i, 1))
            act_turned(act, i, "ac"[n], SCORE[n][0][:, 0:T], cols_now[n][:, 1:2], cols_now[n][:, 0:1], h_t[n][:, :])
            yield
            yield from act_qkv(act, i, n)
            for t in range(NT):
                yield
                act_keys(act, i, n, t)

        def act_yt(act, i, n):
            act.wait_ge(*yt_done[n](i, 1))
            act.activation(y_nt[n][:, :], SCORE[n][0][:, 0:T], ACT.Copy).then_inc(yt_copied[n].sem, 1)

        def act_a(act, i):
            yield from act_start(act, i, 0)
            yield
            act.wait_ge(*max_turned(i, 1))
            act.activation(max_t[:, :], SCORE[0][0][:, 0:P].bitcast(BF16), ACT.Copy).then_inc(max_ready.sem, 1)
            for u in range(NU):
                yield
                act.wait_ge(*score_done[0](i, u + 1))
                act.activation(probs[0][:, u % RING, :], SCORE[0][u % 2][:, :], ACT.Exp, scale=SCALE)\
                    .then_inc(probs_ready[0].sem, 1)
            yield
            act_yt(act, i, 0)
            yield
            act_turned(act, i, "mix", SCORE[0][0][:, 0:T], lncol[:, 0:1], lncol[:, 1:2], h_t[0][:, :])
            yield
            act_turned(act, i, "moe", SCORE[0][0][:, 0:T], lncol[:, 2:3], lncol[:, 3:4], tt[:, :])

        def act_c(act, i):
            yield from act_start(act, i, 1)
            for burst in range(NU // RING):
                units = range(burst * RING, (burst + 1) * RING)
                for u in units:
                    yield
                    act.wait_ge(*score_done[1](i, u + 1))
                    act.activation(probs[1][:, u % RING, :], score_bank(1, u)[:, :], ACT.Copy)\
                        .then_inc(taken.sem, 1)
                    yield
                    act.wait_ge(*taken(i, u + 1))
                    act.activation(ratio[:, u % RING, :], probs[1][:, u % RING, :], ACT.Square)\
                        .then_inc(squared.sem, 1)
                yield
                for u in units:
                    act.wait_ge(*squared(i, u + 1))
                    act.activation(ratio[:, u % RING, :], ratio[:, u % RING, :], ACT.Abs_reciprocal_sqrt, bias=1.0)\
                        .then_inc(rooted.sem, 1)
                for u in units:
                    yield
                    act.wait_ge(*ratio_done[u % 2](i, u // 2 + 1))
                    act.activation(probs[1][:, u % RING, :], probs[1][:, u % RING, :], ACT.Identity, bias=1.0)\
                        .then_inc(lifted.sem, 1)
            yield
            act_yt(act, i, 1)
            yield
            act_turned(act, i, "d", SCORE[1][0][:, 0:T], cols_now[1][:, 4:5], cols_now[1][:, 3:4], h_t[1][:, :])
            yield
            act.wait_ge(*pjt_done(i, 1))
            act.activation(pj_t[:, :], SCORE[1][0][0:PROJ, 0:T], ACT.Copy).then_inc(pjt_ready.sem, 1)
            yield
            act.wait_ge(*lg4_shifted(i, 1))
            act.activation(ex4[:, :, :], lg4[:, :, :], ACT.Exp).then_inc(exp4_ready.sem, 1)
            yield
            act.wait_ge(*drt_done(i, 1))
            act.activation(dr_t[:, :], SCORE[1][0][0:RTOT, 0:T], ACT.Copy).then_inc(drt_ready.sem, 1)

        def act_k(act, i):
            for c in range(NCH):
                if c == 1:
                    yield
                    act.wait_ge(*gap_ready(i, 1))
                    act.activation(tgap[:, :], gap[:, :], ACT.Tanh, scale=0.5).then_inc(tanh_ready.sem, 1)
                yield
                act.wait_ge(*gu_done(i, c + 1))
                if c >= 2:
                    act.wait_ge(*hidden_ready(i, c - 1))
                act.activation(tanh_g[:, c % 2, :], GU[c % 2][:, 0:T], ACT.Tanh, scale=0.5)\
                    .then_inc(tanh_done.sem, 1)

        def act_g(act):
            piece = NCH // NQ
            for k in range(NQ):
                yield
                if 1 <= k < NQ - 1:
                    act.wait_ge(prep["hi"], k)
                    act.wait_ge(prep["lo"], k)
                    act.dma_start(stage[:, (k + 1) % 2, :, :, :], a["gu"][:, :, (k + 1) * piece:(k + 2) * piece, :])\
                       .then_inc(loads[f"gu{(k + 1) % 2}"], 16)
                act.wait_ge(loads[f"gu{k % 2}"], 16 * (k // 2 + 1))
                act.activation(gu_hi[:, :, k * piece:(k + 1) * piece, :], stage[:, k % 2, :, :, :], ACT.Copy)\
                    .then_inc(prep["hi"], 1)
                for _ in range(2 if k == 0 else 1):
                    yield

        @block.scalar
        def _(act):
            for user in (h_ready["a"], h_ready["d"]):
                act.sem_inc(user.sem, 1)
            piece = NCH // NQ
            for k in range(2):
                act.dma_start(stage[:, k, :, :, :], a["gu"][:, :, k * piece:(k + 1) * piece, :])\
                   .then_inc(loads[f"gu{k}"], 16)
            act.wait_ge(loads["mod"], 64)
            act.activation(silu_c[:, :, :], c_t[:, :, :], ACT.Silu).then_inc(prep["silu"], 1)
            act.wait_ge(prep["temp"], 1)
            act.activation(simst[:, 2:3], simst[:, 1:2], ACT.Exp).then_inc(prep["exptemp"], 1)
            act.wait_ge(loads["ffn"], 11 * 16)
            rounds(act, SCALAR_ORDER, {"K": act_k, "A": act_a, "C": act_c}, act_g)

        def pe_turn(pe, i, s):
            n = SITES[s]
            pe.wait_ge(*xn_ready[s](i, 1))
            for t in range(NT):
                last = pe.transpose(SCORE[n][0][:, t * P:(t + 1) * P], xn[n][:, t, :], identf[:, :])
            last.then_inc(xt_ready[s].sem, 1)

        def pe_spread(pe, i, n, t):
            for q in range(2):
                if t == 1:
                    pe.wait_ge(*(k_spread, q_spread)[q][n](i, 1))
                dst = SCORE[n][q][:, :].bitcast(BF16)
                for g in range(NPAIR):
                    row = (1 - q) * H + 2 * g
                    last = pe.transpose(dst[:, g * P:(g + 1) * P],
                                        stack[n][:, t, row:row + 2, :].rearrange("p h r -> p (h r)"),
                                        identb[:, :])
                last.then_inc(spread_done[n].sem, 1)
                if q == 0:
                    yield

        def pe_start(pe, i, n):
            s = "ac"[n]
            w = (w_qkv0, w_qkv1)[n]
            wide = (512, 384)[n]
            yield
            pe_turn(pe, i, s)
            yield
            pe.wait_ge(*h_ready[s](i, 1))
            for t in range(NT):
                if t:
                    yield
                pe.matmul(SCORE[n][t][:, 0:wide], h_t[n][:, t * P:(t + 1) * P], w[:, :], start=True, stop=True)\
                    .then_inc(qkv_done[n].sem, 1)
            yield
            pe.wait_ge(*stack_ready[n](i, 1))
            yield from pe_spread(pe, i, n, 0)
            yield
            yield from pe_spread(pe, i, n, 1)

        def pe_maximum(pe, i, u):
            dst = SCORE[0][u % 2]
            q, k = q_t[0], k_t[0]
            if u == 0:
                pe.wait_ge(*k_spread[0](i, NT))
                pe.wait_ge(*q_spread[0](i, NT))
            if u >= 2:
                pe.wait_ge(*max_taken(i, u - 1))
            if u < 8:
                k3 = dst[:, :].rearrange("p (h k) -> p h k", h=2)
                pe.matmul(k3[:, :, P:T], identb[:, :], maskb[:, 0:1, :].to_broadcast([P, 2, P]),
                          start=True, stop=False, skip_group_check=True)
                for j in range(2):
                    last = pe.matmul(k3[:, j, :], q[:, u, j, P:T], k[:, u, :], start=False,
                                     stop=j == 1, skip_group_check=True)
            else:
                k4 = dst[:, :].rearrange("p (h k) -> p h k", h=4)
                pe.matmul(k4, identb[:, :], maskb[:, 0:1, :].to_broadcast([P, 4, P]),
                          start=True, stop=False, skip_group_check=True)
                for j in range(4):
                    g = 2 * (u - 8) + j // 2
                    last = pe.matmul(k4[:, j, :], q[:, g, j % 2, 0:P], k[:, g, 0:P], start=False,
                                     stop=j == 3, skip_group_check=True)
            last.then_inc(maxscore_done.sem, 1)

        def pe_score(pe, i, n, u):
            g, r = divmod(u, 3)
            dst = score_bank(n, u)
            q, k = q_t[n], k_t[n]
            if u >= 2:
                pe.wait_ge(*(probs_ready[0] if n == 0 else taken)(i, u if n == 1 and u > RING else u - 1))
            if r < 2:
                p = 2 * g + r
                q3 = dst[:, :].rearrange("p (h q) -> p h q", h=2)
                if n == 0:
                    pe.matmul(q3[:, :, 0:P], identb[:, :], maskb[:, 1:2, :].to_broadcast([P, 2, P]),
                              start=True, stop=False, skip_group_check=True)
                last = pe.matmul(dst[:, :], k[:, p, 0:P], q[:, p, :, :].rearrange("p h q -> p (h q)"),
                                 start=n == 1, stop=n == 1, skip_group_check=True)
                if n == 0:
                    for j in range(2):
                        last = pe.matmul(q3[:, j, :], selb[:, 2 * p + j:2 * p + j + 1].to_broadcast([P, P]), max_t[:, :], start=False,
                                         stop=j == 1, skip_group_check=True)
            else:
                q4 = dst[:, :].rearrange("p (h q) -> p h q", h=4)
                if n == 0:
                    pe.matmul(q4, identb[:, :], maskb[:, 1:2, :].to_broadcast([P, 4, P]),
                              start=True, stop=False, skip_group_check=True)
                for j in range(2):
                    last = pe.matmul(q4[:, 2 * j:2 * j + 2, :], k[:, 2 * g + j, P:T],
                                     q[:, 2 * g + j, :, P:T], start=n == 1, stop=n == 1,
                                     skip_group_check=True)
                if n == 0:
                    for j in range(4):
                        last = pe.matmul(q4[:, j, :], selb[:, 4 * g + j:4 * g + j + 1].to_broadcast([P, P]), max_t[:, P:T], start=False,
                                         stop=j == 3, skip_group_check=True)
            last.then_inc(score_done[n].sem, 1)

        def pe_values(pe, i, n, g):
            pe.wait_ge(*probs_ready[n](i, 3 * g + 3))
            if g == 2:
                pe.wait_ge(*pv_copied[n](i, 1))
            half = BV[n][:, (g % 2) * T:(g % 2 + 1) * T]
            for j in range(4):
                u = 3 * g + j // 2
                to = VW * j + (D + 1, VW)[n]
                pe.matmul(half[VW * j:to, :], v_aug[n][:, 0, 4 * g + j, :],
                          probs[n][:, u % RING, (j % 2) * T:(j % 2 + 1) * T],
                          start=True, stop=False, skip_group_check=True)
                last = pe.matmul(half[VW * j:to, P:T], v_aug[n][:, 1, 4 * g + j, :],
                                 probs[n][:, (3 * g + 2) % RING, j * P:(j + 1) * P],
                                 start=False, stop=True, skip_group_check=True)
            if g % 2:
                last.then_inc(pv_done[n].sem, 1)

        def pe_gather(pe, i, n):
            yield
            pe.wait_ge(*pv_copied[n](i, 2))
            for t in range(NT):
                if t:
                    yield
                for g in range(4):
                    last = pe.transpose(SCORE[n][t][:, g * P:(g + 1) * P], y_t[n][:, g, t * P:(t + 1) * P], identf[:, :])
                last.then_inc(y_back[n].sem, 1)
            yield
            pe.wait_ge(*y_ready[n](i, 1))
            for t in range(NT):
                last = pe.transpose(SCORE[n][0][:, t * P:(t + 1) * P], y_n[n][:, t, :], identf[:, :])
            last.then_inc(yt_done[n].sem, 1)
            yield
            pe.wait_ge(*yt_copied[n](i, 1))
            for t in range(NT):
                last = pe.matmul(SCORE[n][1][:, t * P:(t + 1) * P], y_nt[n][:, t * P:(t + 1) * P], w_o[n][:, :],
                                 start=True, stop=True)
            last.then_inc(attn_out[n].sem, 1)

        def pe_a(pe, i):
            yield from pe_start(pe, i, 0)
            for u in range(NU):
                yield
                pe_maximum(pe, i, u)
            yield
            pe.wait_ge(*max_stacked(i, 1))
            for t in range(NT):
                last = pe.transpose(SCORE[0][0][:, t * 64:(t + 1) * 64].bitcast(BF16), max_stack[:, t, :], identb[:, :])
            last.then_inc(max_turned.sem, 1)
            for u in range(NU):
                yield
                if u == 0:
                    pe.wait_ge(*max_ready(i, 1))
                pe_score(pe, i, 0, u)
                if u % 3 == 0 and u > 0:
                    yield
                    pe_values(pe, i, 0, u // 3 - 1)
            yield
            pe_values(pe, i, 0, 3)
            yield from pe_gather(pe, i, 0)
            yield
            pe_turn(pe, i, "mix")
            yield
            pe.wait_ge(*h_ready["mix"](i, 1))
            for t in range(NT):
                last = pe.matmul(SCORE[0][1][:, t * P:(t + 1) * P], h_t[0][:, t * P:(t + 1) * P], w_mix[:, :],
                                 start=True, stop=True)
            last.then_inc(mix_done.sem, 1)
            yield
            pe_turn(pe, i, "moe")
            yield
            pe.wait_ge(*h_ready["moe"](i, 1))
            for t in range(NT):
                last = pe.matmul(SCORE[0][1][:, t * NE:(t + 1) * NE], tt[:, t * P:(t + 1) * P], w_gate[:, :],
                                 start=True, stop=True)
            last.then_inc(logits_done.sem, 1)

        def pe_k(pe, i):
            for c in range(NCH):
                yield
                if c == 0:
                    pe.wait_ge(*parts_moe(i, 1))
                    pe.wait_ge(prep["hi"], NQ)
                    pe.wait_ge(prep["lo"], NQ)
                if c >= 2:
                    pe.wait_ge(*hidden_ready(i, c - 1))
                for n in range(2):
                    dst = GU[c % 2][:, n * T:(n + 1) * T]
                    pe.matmul(dst, gu_hi[:, n, c, :], tt_hi[:, :], start=True, stop=False, skip_group_check=True)
                    pe.matmul(dst, gu_hi[:, n, c, :], tt_lo[:, :], start=False, stop=False, skip_group_check=True)
                    last = pe.matmul(dst, gu_lo[:, n, c, :], tt_hi[:, :], start=False, stop=True,
                                     skip_group_check=True)
                last.then_inc(gu_done.sem, 1)
                if c >= 1:
                    yield
                    pe_down(pe, i, c - 1)
            yield
            pe_down(pe, i, NCH - 1)

        def pe_down(pe, i, c):
            e, k = divmod(c, CH)
            pe.wait_ge(*hidden_ready(i, c + 1))
            if k == 0 and e >= 1:
                pe.wait_ge(*expert_added(i, e))
            for t in range(NT):
                last = pe.matmul(BOUT[:, t * P:(t + 1) * P], hidden[:, c % 2, t * P:(t + 1) * P],
                                 w_down[:, c, :], start=k == 0 and t == 0, stop=k == CH - 1 and t == 1,
                                 skip_group_check=True)
            if k == CH - 1:
                last.then_inc(expert_done.sem, 1)

        def pe_c(pe, i):
            yield from pe_start(pe, i, 1)
            for u in range(NU):
                if u in (6, 9):
                    yield
                    pe_values(pe, i, 1, u // 3 - 2)
                yield
                if u == 0:
                    pe.wait_ge(*k_spread[1](i, NT))
                    pe.wait_ge(*q_spread[1](i, NT))
                pe_score(pe, i, 1, u)
            for g in (2, 3):
                yield
                pe_values(pe, i, 1, g)
            yield from pe_gather(pe, i, 1)
            small, both = SCORE[1]
            yield
            pe_turn(pe, i, "d")
            yield
            pe.wait_ge(*h_ready["d"](i, 1))
            for t in range(NT):
                last = pe.matmul(both[:, t * T:t * T + P + PROJ + RTOT], h_t[1][:, t * P:(t + 1) * P], w_ffn1[:, :],
                                 start=t == 0, stop=False, skip_group_check=True)
            last.then_inc(ffn1_done.sem, 1)
            yield
            pe.wait_ge(*pj_ready(i, 1))
            for t in range(NT):
                last = pe.transpose(small[0:PROJ, t * P:(t + 1) * P], pj[:, t, :], identf[:, :])
            last.then_inc(pjt_done.sem, 1)
            yield
            pe.wait_ge(*pjt_ready(i, 1))
            for t in range(NT):
                last = pe.matmul(small[:, T + t * NR:T + (t + 1) * NR], pj_t[:, t * P:(t + 1) * P], simn[:, :],
                                 start=True, stop=True)
            last.then_inc(lg4_done.sem, 1)
            yield
            pe.wait_ge(*dr_ready(i, 1))
            for t in range(NT):
                last = pe.transpose(small[0:RTOT, t * P:(t + 1) * P], dr[:, t, :], identf[:, :])
            last.then_inc(drt_done.sem, 1)
            yield
            pe.wait_ge(*drt_ready(i, 1))
            for t in range(NT):
                last = pe.matmul(both[:, t * T:t * T + P], dr_t[:, t * P:(t + 1) * P], w_up1[:, :],
                                 start=False, stop=t == 1, skip_group_check=True)
            last.then_inc(ffn1_out.sem, 1)

        @block.tensor
        def _(pe):
            pe.wait_ge(prep["silu"], 1)
            for l in range(2):
                for m in range(6):
                    last = pe.matmul(bank[0][:, (l * 6 + m) * B:(l * 6 + m + 1) * B],
                                     wmod[:, l, m * P:(m + 1) * P], silu_c[:, l, :], start=True, stop=True)
            last.then_inc(prep["modcols_pe"], 1)
            for l in range(2):
                pe.matmul(bank[1 + 2 * l][0:B, 0:512], silu_c[:, l, :], wmod[:, l, 0:512], start=True, stop=True)
                last = pe.matmul(bank[2 + 2 * l][0:B, 0:256], silu_c[:, l, :], wmod[:, l, 512:768],
                                 start=True, stop=True)
            last.then_inc(prep["modrows_pe"], 1)
            pe.wait_ge(loads["attn"], 32)
            pe.wait_ge(prep["u2"], 1)
            for n in range(3):
                for g in range(NPAIR):
                    last = pe.matmul(bank[5 + n][:, g * 24:(g + 1) * 24], wd3[:, n, g, :],
                                     u2[:, n, :, :].rearrange("p h d -> p (h d)"), start=True, stop=True)
            last.then_inc(prep["weff_pe"], 1)
            pe.wait_ge(loads["const"], 80)
            pe.wait_ge(prep["simt"], 1)
            pe.wait_ge(prep["modcols"], 1)
            pe.transpose(bank[0][0:PROJ, 0:NR], simt[:, :], identf[0:NR, 0:NR]).then_inc(prep["simn_pe"], 1)
            pe.wait_ge(loads["ffn"], 11 * 16)
            rounds(pe, TENSOR_ORDER, {"K": pe_k, "A": pe_a, "C": pe_c})

        def dve_stats(dve, i, s, src, chain):
            n = SITES[s]
            for t in range(NT):
                last = dve.bn_stats(stats[n][:, t, :], src[:, t, :])
            chain(last)
            yield
            chain.wait()
            dve.sem_inc(passed["dve"], 1)
            for t in range(NT):
                last = dve.bn_aggr(meanvar[n][:, t, :], stats[n][:, t, :])
            last.then_inc(var_ready[s].sem, 1)

        def dve_norm(dve, i, s, src):
            n = SITES[s]
            dve.wait_ge(*rstd_ready[s](i, 1))
            for t in range(NT):
                last = dve.tensor_scalar(xn[n][:, t, :], src[:, t, :], meanvar[n][:, t, 0:1], rstd[n][:, t:t + 1],
                                         ALU.subtract, ALU.mult)
            last.then_inc(xn_ready[s].sem, 1)

        def rank_of(dve, chain, values, n, earlier, ca, cb, rank):
            other = values.unsqueeze(2).to_broadcast([P, NT, n, n])
            own = values.unsqueeze(3).to_broadcast([P, NT, n, n])
            grid = dict(e=n)
            dve.tensor_tensor(ca.rearrange("p t (e j) -> p t e j", **grid), other, own, ALU.is_gt)
            chain(dve.tensor_tensor(cb.rearrange("p t (e j) -> p t e j", **grid), other, own, ALU.is_ge))
            yield
            chain.wait()
            chain(dve.tensor_tensor(cb, cb, ca, ALU.subtract))
            yield
            chain.wait()
            chain(dve.tensor_tensor(cb, cb, earlier[:, :].unsqueeze(1).to_broadcast([P, NT, n * n]), ALU.mult))
            yield
            chain.wait()
            chain(dve.tensor_tensor(ca, ca, cb, ALU.add))
            yield
            chain.wait()
            chain(dve.tensor_reduce(rank, ca.rearrange("p t (e j) -> p t e j", **grid), AX.X, ALU.add))
            yield
            chain.wait()

        def dve_start(dve, i, n, chain):
            src = (x_in, x_b)[n]
            yield
            if n == 0:
                dve.wait_ge(*x_loaded(i, 16))
            else:
                dve.wait_ge(*x_b_ready(i, 1))
            yield from dve_stats(dve, i, "ac"[n], src, chain)
            yield
            dve_norm(dve, i, "ac"[n], src)
            yield
            dve.wait_ge(*qkv_copied[n](i, NT))
            qk = raw[n][:, :, 0:256].rearrange("p t (h d) -> p t h d", d=D)
            if n == 0:
                e = qk[:, :, :, DE:D]
                cos, sin = (rope[:, k, :, :].unsqueeze(2).to_broadcast([P, NT, 2 * H, DE]) for k in range(2))
                dve.tensor_tensor(rot[:, :, :, :], raw[0][:, :, 384:512].rearrange("p t (h d) -> p t h d", d=DE),
                                  sin, ALU.mult)
                chain(dve.tensor_tensor(e, e, cos, ALU.mult))
                yield
                chain.wait()
                chain(dve.tensor_tensor(e, e, rot[:, :, :, :], ALU.add))
                yield
                chain.wait()
            st = stack[n]
            p1, p2 = st[:, :, :, 0:D], st[:, :, :, D:2 * D]
            chain(dve.tensor_copy(p1, qk))
            yield
            chain.wait()
            yield
            chain(dve.tensor_tensor(qk, qk, p1, ALU.subtract))
            yield
            chain.wait()
            dve.tensor_copy(p2, qk).then_inc(parts_ready[n].sem, 1)
            yield
            dve.wait_ge(*parts_ready[n](i, 1))
            chain(dve.tensor_tensor(qk, qk, p2, ALU.subtract))
            yield
            chain.wait()
            dve.tensor_copy(st[:, :, 0:H, 5 * D:6 * D], qk[:, :, 0:H, :])
            yield
            dve.tensor_copy(st[:, :, H:2 * H, 4 * D:5 * D], qk[:, :, H:2 * H, :])
            yield
            last = None
            for side, slot, part in ((0, 2, 0), (0, 4, 0), (0, 3, 1), (1, 3, 0), (1, 5, 0), (1, 2, 1)):
                if last is not None:
                    yield
                last = dve.tensor_copy(st[:, :, side * H:(side + 1) * H, slot * D:(slot + 1) * D],
                                       st[:, :, side * H:(side + 1) * H, part * D:(part + 1) * D])
            last.then_inc(stack_ready[n].sem, 1)
            for t in range(NT):
                yield
                dve.wait_ge(*spread_done[n](i, 2 * t + 2))
                src_q = SCORE[n][1][:, :].bitcast(BF16).rearrange("p (g q) -> p g q", g=NPAIR)
                for j in range(2):
                    rows = slice(ROWS * j, ROWS * (j + 1))
                    last = dve.tensor_copy(q_t[n][rows, :, j, t * P:(t + 1) * P], src_q[rows, :, :])
                last.then_inc(q_spread[n].sem, 1)

        def dve_take_values(dve, i, n, k):
            dve.wait_ge(*pv_done[n](i, k + 1))
            dve.tensor_copy(y_t[n][:, 2 * k:2 * k + 2, :].rearrange("p g q -> p (g q)"), BV[n][:, :])\
               .then_inc(pv_copied[n].sem, 1)

        def dve_gather(dve, i, n, chain):
            yield
            dve_take_values(dve, i, n, 1)
            yield
            for t in range(NT):
                if t:
                    yield
                dve.wait_ge(*y_back[n](i, t + 1))
                by_head = SCORE[n][t][:, :].rearrange("p (h v) -> p h v", v=VW)
                if n == 0:
                    chain(dve.reciprocal(den[0][:, t, :], by_head[:, :, D]))
                    yield
                    chain.wait()
                else:
                    chain(dve.tensor_scalar(den[1][:, t, :], by_head[:, :, D], 2 * EPS_RATIONAL, None, ALU.add))
                    yield
                    chain.wait()
                    chain(dve.reciprocal(den[1][:, t, :], den[1][:, t, :]))
                    yield
                    chain.wait()
                last = dve.tensor_tensor(y_n[n][:, t, :].rearrange("p (h d) -> p h d", d=D), by_head[:, :, 0:D],
                                         den[n][:, t, :].unsqueeze(2).to_broadcast([P, H, D]), ALU.mult)
            last.then_inc(y_ready[n].sem, 1)
            yield
            gate = (rows_a, rows_c)[n]
            dve.wait_ge(*(rows_a_loaded, rows_c_loaded)[n](i, 16))
            dve.wait_ge(*attn_out[n](i, 1))
            chain(dve.tensor_tensor(xn[n][:, :, :], SCORE[n][1][:, 0:T].rearrange("p (t c) -> p t c", t=NT),
                                    gate[:, 0:1, :].to_broadcast([P, NT, P]), ALU.mult))
            yield
            chain.wait()
            dve.tensor_tensor(x_mid[n][:, :, :], xn[n][:, :, :], (x_in, x_b)[n][:, :, :], ALU.add)\
               .then_inc(x_mid_ready[n].sem, 1)

        def dve_a(dve, i):
            chain = Chain(dve, dve_self["a"], i)
            yield from dve_start(dve, i, 0, chain)
            for u in range(NU):
                yield
                dve.wait_ge(*maxscore_done(i, u + 1))
                if u < 8:
                    dst, heads = negmax[:, 1, 2 * u:2 * u + 2], 2
                else:
                    dst, heads = negmax[:, 0, 4 * (u - 8):4 * (u - 7)], 4
                dve.tensor_reduce(dst, SCORE[0][u % 2][:, :].rearrange("p (h k) -> p h k", h=heads),
                                  AX.X, ALU.max, negate=True).then_inc(max_taken.sem, 1)
            yield
            dve.wait_ge(*max_taken(i, NU))
            chain(dve.tensor_copy(max_stack[:, :, 0:H], negmax[:, :, :]))
            yield
            chain.wait()
            chain(dve.tensor_tensor(negmax_r[:, :, :], negmax[:, :, :], max_stack[:, :, 0:H], ALU.subtract))
            yield
            chain.wait()
            dve.tensor_copy(max_stack[:, :, H:2 * H], negmax_r[:, :, :]).then_inc(max_stacked.sem, 1)
            yield
            dve_take_values(dve, i, 0, 0)
            yield from dve_gather(dve, i, 0, chain)
            chain.done()
            chain = Chain(dve, dve_self["head"], i)
            yield
            dve.wait_ge(*x_mid_ready[0](i, 1))
            yield from dve_stats(dve, i, "b", x_mid[0], chain)
            yield
            dve_norm(dve, i, "b", x_mid[0])
            yield
            dve.wait_ge(*xn_ready["b"](i, 1))
            dve.wait_ge(*rows_b_loaded(i, 16))
            chain(dve.tensor_tensor(h_ffn[:, :, :], xn[0][:, :, :], rows_b[:, 1:2, :].to_broadcast([P, NT, P]), ALU.mult))
            yield
            chain.wait()
            chain(dve.tensor_tensor(h_ffn[:, :, :], h_ffn[:, :, :], rows_b[:, 0:1, :].to_broadcast([P, NT, P]),
                                    ALU.add))
            yield
            chain.wait()
            yield from dve_stats(dve, i, "mix", h_ffn, chain)
            yield
            dve_norm(dve, i, "mix", h_ffn)
            yield
            dve.wait_ge(*mix_done(i, 1))
            chain(dve.tensor_tensor(h2[:, :, :], SCORE[0][1][:, 0:T].rearrange("p (t c) -> p t c", t=NT),
                                    h_ffn[:, :, :], ALU.add))
            yield
            chain.wait()
            yield from dve_stats(dve, i, "moe", h2, chain)
            yield
            dve_norm(dve, i, "moe", h2)
            chain.done()

        def dve_k(dve, i):
            chain = Chain(dve, dve_self["k"], i)
            yield
            dve.wait_ge(*h_ready["moe"](i, 1))
            chain(dve.tensor_copy(tt_hi[:, :], tt[:, :]))
            yield
            chain.wait()
            dve.tensor_tensor(tt_lo[:, :], tt[:, :], tt_hi[:, :].bitcast(F32), ALU.subtract)\
               .then_inc(parts_moe.sem, 1)
            yield
            dve.tensor_copy(x_keep[:, :, :], x_mid[0][:, :, :])
            dve.wait_ge(*logits_done(i, 1))
            chain(dve.tensor_copy(logit[:, :, :], SCORE[0][1][:, 0:NT * NE].rearrange("p (t e) -> p t e", t=NT)))
            yield
            chain.wait()
            yield
            yield from rank_of(dve, chain, logit[:, :, :], NE, before, cmp_a[:, :, :], cmp_b[:, :, :], rank[:, :, :])
            dve.tensor_scalar(first[:, :, :], rank[:, :, :], 0.0, None, ALU.is_equal)
            chain(dve.tensor_scalar(second[:, :, :], rank[:, :, :], 1.0, None, ALU.is_equal))
            yield
            chain.wait()
            dve.tensor_tensor(comb[:, :, :], first[:, :, :], second[:, :, :], ALU.add)
            chain(dve.tensor_tensor(first[:, :, :], first[:, :, :], second[:, :, :], ALU.subtract))
            yield
            chain.wait()
            chain(dve.tensor_tensor(second[:, :, :], first[:, :, :], logit[:, :, :], ALU.mult))
            yield
            chain.wait()
            dve.tensor_reduce(gap[:, :], second[:, :, :], AX.X, ALU.add).then_inc(gap_ready.sem, 1)
            for c in range(NCH):
                yield
                dve.wait_ge(*tanh_done(i, c + 1))
                dve.scalar_tensor_tensor(out=tanh_g[:, c % 2, :], in0=tanh_g[:, c % 2, :], scalar=1.0,
                                         in1=GU[c % 2][:, 0:T], op0=ALU.add, op1=ALU.mult)\
                   .then_inc(product_done.sem, 1)
                yield
                dve.wait_ge(*product_done(i, c + 1))
                dve.tensor_tensor(hidden[:, c % 2, :], tanh_g[:, c % 2, :], GU[c % 2][:, T:2 * T], ALU.mult)\
                   .then_inc(hidden_ready.sem, 1)
                if c == 2:
                    dve.wait_ge(*tanh_ready(i, 1))
                    chain(dve.tensor_tensor(first[:, :, :], first[:, :, :],
                                            tgap[:, :].unsqueeze(2).to_broadcast([P, NT, NE]), ALU.mult))
                    yield
                    chain.wait()
                    chain(dve.tensor_tensor(comb[:, :, :], comb[:, :, :], first[:, :, :], ALU.add))
                    yield
                    chain.wait()
                    chain(dve.tensor_scalar(comb[:, :, :], comb[:, :, :], 0.25, None, ALU.mult))
                    yield
                    chain.wait()
                if c % CH == 0 and c >= CH:
                    yield
                    dve_expert(dve, i, c // CH - 1)
            yield
            dve_expert(dve, i, NE - 1)
            yield
            dve.wait_ge(*expert_added(i, NE))
            dve.wait_ge(*rows_g_loaded(i, 16))
            chain(dve.tensor_tensor(acc[:, :, :], acc[:, :, :], rows_g[:, 0:1, :].to_broadcast([P, NT, P]), ALU.mult))
            yield
            chain.wait()
            dve.tensor_tensor(x_b[:, :, :], acc[:, :, :], x_keep[:, :, :], ALU.add).then_inc(x_b_ready.sem, 1)
            chain.done()

        def dve_expert(dve, i, e):
            dve.wait_ge(*expert_done(i, e + 1))
            if e >= 1:
                dve.wait_ge(*expert_added(i, e))
            for t in range(NT):
                last = dve.scalar_tensor_tensor(out=acc[:, t, :], in0=BOUT[:, t * P:(t + 1) * P],
                                                scalar=comb[:, t, e:e + 1],
                                                in1=(h2 if e == 0 else acc)[:, t, :], op0=ALU.mult, op1=ALU.add)
            last.then_inc(expert_added.sem, 1)

        def dve_c(dve, i):
            chain = Chain(dve, dve_self["c"], i)
            yield from dve_start(dve, i, 1, chain)
            for u in range(NU):
                if u == 6:
                    yield
                    dve_take_values(dve, i, 1, 0)
                if u % 2:
                    continue
                yield
                dve.wait_ge(*rooted(i, u + 1))
                dve.tensor_tensor(probs[1][:, u % RING, :], probs[1][:, u % RING, :], ratio[:, u % RING, :], ALU.mult)\
                   .then_inc(ratio_done[0].sem, 1)
            yield from dve_gather(dve, i, 1, chain)
            chain.done()
            chain = Chain(dve, dve_self["d"], i)
            small, both = SCORE[1][0], SCORE[1][1][:, :].rearrange("p (t c) -> p t c", t=NT)
            yield
            dve.wait_ge(*x_mid_ready[1](i, 1))
            yield from dve_stats(dve, i, "d", x_mid[1], chain)
            yield
            dve_norm(dve, i, "d", x_mid[1])
            yield
            dve.wait_ge(*ffn1_done(i, 1))
            dve.tensor_tensor(pj[:, :, :], both[:, :, P:P + PROJ],
                              bp_row[:, :].unsqueeze(1).to_broadcast([P, NT, PROJ]), ALU.add)\
               .then_inc(pj_ready.sem, 1)
            yield
            dve.wait_ge(*pj_ready(i, 1))
            chain(dve.tensor_tensor(pjsq[:, :, :], pj[:, :, :], pj[:, :, :], ALU.mult))
            yield
            chain.wait()
            chain(dve.tensor_reduce(pj_ss[:, :], pjsq[:, :, :], AX.X, ALU.add))
            yield
            chain.wait()
            dve.tensor_scalar(pj_ss[:, :], pj_ss[:, :], 1e-24, None, ALU.max).then_inc(pjss_ready.sem, 1)
            yield
            dve.wait_ge(*pjinv_ready(i, 1))
            dve.wait_ge(*lg4_done(i, 1))
            chain(dve.tensor_tensor(lg4[:, :, :], small[:, T:T + NT * NR].rearrange("p (t e) -> p t e", t=NT),
                                    pj_inv[:, :].unsqueeze(2).to_broadcast([P, NT, NR]), ALU.mult))
            yield
            chain.wait()
            chain(dve.tensor_reduce(st4[:, 0, :], lg4[:, :, :], AX.X, ALU.max))
            yield
            chain.wait()
            dve.tensor_tensor(lg4[:, :, :], lg4[:, :, :], st4[:, 0, :].unsqueeze(2).to_broadcast([P, NT, NR]),
                              ALU.subtract).then_inc(lg4_shifted.sem, 1)
            yield
            dve.wait_ge(*lg4_shifted(i, 1))
            yield from rank_of(dve, chain, lg4[:, :, :], NR, before4, cmp4_a[:, :, :], cmp4_b[:, :, :], rank4[:, :, :])
            yield
            dve.tensor_scalar(ret[:, :, :], rank4[:, :, :], 0.0, None, ALU.is_equal)
            dve.wait_ge(*exp4_ready(i, 1))
            chain(dve.tensor_reduce(st4[:, 1, :], ex4[:, :, :], AX.X, ALU.add))
            yield
            chain.wait()
            chain(dve.reciprocal(st4[:, 2, :], st4[:, 1, :]))
            yield
            chain.wait()
            chain(dve.tensor_tensor(ret[:, :, :], ret[:, :, :], ex4[:, :, :], ALU.mult))
            yield
            chain.wait()
            chain(dve.tensor_tensor(ret[:, :, :], ret[:, :, :],
                                    st4[:, 2, :].unsqueeze(2).to_broadcast([P, NT, NR]), ALU.mult))
            yield
            chain.wait()
            at = 0
            for k, r in enumerate(RANKS):
                last = dve.tensor_tensor(dr[:, :, at:at + r], both[:, :, P + PROJ + at:P + PROJ + at + r],
                                         ret[:, :, k:k + 1].to_broadcast([P, NT, r]), ALU.mult)
                at += r
            last.then_inc(dr_ready.sem, 1)
            yield
            dve.wait_ge(*ffn1_out(i, 1))
            chain(dve.tensor_tensor(xn[1][:, :, :], both[:, :, 0:P], rows_c[:, 1:2, :].to_broadcast([P, NT, P]),
                                    ALU.mult))
            yield
            chain.wait()
            dve.wait_ge(*x_stored.before(i, 16))
            dve.tensor_tensor(x_out[:, :, :], xn[1][:, :, :], x_mid[1][:, :, :], ALU.add)\
               .then_inc(x_out_ready.sem, 1)
            chain.done()

        def dve_g(dve):
            piece = NCH // NQ
            for _ in range(13):
                yield
            for k in range(NQ):
                yield
                dve.wait_ge(prep["hi"], k + 1)
                rows = slice(k * piece, (k + 1) * piece)
                for n in range(2):
                    last = dve.tensor_tensor(gu_lo[:, n, rows, :], stage[:, k % 2, n, :, :],
                                             gu_hi[:, n, rows, :].bitcast(F32), ALU.subtract)
                last.then_inc(prep["lo"], 1)
                for _ in range(3 + 3 * (k == 1) + (k > 0 and k % 2 == 0)):
                    yield

        @block.vector
        def _(dve):
            steps = [0]

            def step(ins):
                steps[0] += 1
                ins.then_inc(prep["dve"], 1)
                dve.wait_ge(prep["dve"], steps[0])

            for user in (x_mid_ready[0], x_b_ready, x_out_ready, var_ready["mix"]):
                dve.sem_inc(user.sem, user.per * user.ahead)
            dve.wait_ge(loads["small"], 80)
            dve.tensor_scalar(simst[:, 1:2], tempc[:, :], CLAMP_MAX, None, ALU.min).then_inc(prep["temp"], 1)
            step(dve.tensor_tensor(simsq[:, :], simt[:, :], simt[:, :], ALU.mult))
            step(dve.tensor_reduce(simst[:, 0:1], simsq[:, :], AX.X, ALU.add))
            dve.tensor_scalar(simst[:, 0:1], simst[:, 0:1], 1e-24, None, ALU.max).then_inc(prep["simss"], 1)
            dve.wait_ge(loads["attn"], 32)
            uq = u2[:, 0:2, :, :].rearrange("p n h d -> p (n h) d")
            dve.tensor_scalar(uq[:, :, 8:12:2], uq[:, :, 5:8:2], -1.0, None, ALU.mult)
            dve.tensor_copy(uq[:, :, 9:12:2], uq[:, :, 4:8:2]).then_inc(prep["u2"], 1)
            dve.wait_ge(prep["modcols_pe"], 1)
            cols = modcols[:, :, :, :].rearrange("p b l m -> p (l m) b")
            step(dve.tensor_copy(cols, bank[0][:, 0:12 * B].rearrange("p (m b) -> p m b", b=B)))
            ones = modcols[:, :, :, :].rearrange("p b l m -> p (b l) m")[:, :, 1:5:3]
            dve.tensor_scalar(ones, ones, 1.0, None, ALU.add).then_inc(prep["modcols"], 1)
            dve.wait_ge(prep["modrows_pe"], 1)
            for l in range(2):
                dve.tensor_copy(modrow[:, l, 0:4, :].rearrange("b m c -> b (m c)"), bank[1 + 2 * l][0:B, :])
                last = dve.tensor_copy(modrow[:, l, 4:6, :].rearrange("b m c -> b (m c)"),
                                       bank[2 + 2 * l][0:B, 0:256])
            step(last)
            dve.memset(BV[0][:, :], 0.0)
            gates = modrow[:, :, 2:6:3, :]
            step(dve.tensor_scalar(gate_s[:, :, :, :], gates, 0.0, 2.0, ALU.is_ge, ALU.mult))
            dve.tensor_scalar(gate_s[:, :, :, :], gate_s[:, :, :, :], -1.0, None, ALU.add)
            for l in range(2):
                last = dve.scalar_tensor_tensor(out=gate_m[:, l, :, :], in0=gates[:, l, :, :], scalar=-1.0,
                                                in1=gates[:, l, :, :], op0=ALU.mult, op1=ALU.max)
            step(last)
            step(dve.tensor_scalar(gate_m[:, :, :, :], gate_m[:, :, :, :], 0.25, None, ALU.max))
            for l in range(2):
                dve.tensor_tensor(rowmods[:, 4 * l:4 * l + 2, :], gate_s[:, l, :, :], gate_m[:, l, :, :], ALU.mult)
            dve.tensor_copy(rowmods[:, 2, :], modrow[:, 0, 3, :])
            dve.tensor_scalar(rowmods[:, 3, :], modrow[:, 0, 4, :], 1.0, None, ALU.add).then_inc(prep["rows"], 1)
            dve.wait_ge(prep["weff_pe"], 1)
            for n in range(3):
                src = bank[5 + n][:, 0:192].rearrange("p (h d) -> p h d", d=12)
                last = dve.tensor_copy(w_qkv0[:, n * P:(n + 1) * P].rearrange("p (h d) -> p h d", d=D),
                                       src[:, :, 0:D])
                if n < 2:
                    last = dve.tensor_copy(w_qkv0[:, 384 + 64 * n:448 + 64 * n]
                                           .rearrange("p (h d) -> p h d", d=DE), src[:, :, D:12])
            last.then_inc(prep["wqkv0"], 1)
            dve.tensor_scalar(w_qkv1[:, 0:P], w_qkv1[:, 0:P], SCALE, None, ALU.mult).then_inc(prep["wqkv1"], 1)
            for k in range(3):
                step(dve.tensor_copy(slope_p[:, k, :], (slope if k == 0 else slope_r)[:, :]))
                if k < 2:
                    step(dve.tensor_tensor(slope_r[:, :], (slope if k == 0 else slope_r)[:, :],
                                           slope_p[:, k, :], ALU.subtract))
            dve.wait_ge(prep["cleared"], 1)
            parts = slope_p[:, :, :].rearrange("p k h -> p h k")
            for t in range(NT):
                q, k = stack[1][:, t, 0:H, :], stack[1][:, t, H:2 * H, :]
                pos = position[:, t:t + 1].unsqueeze(2).to_broadcast([P, H, 3])
                dve.tensor_scalar(q[:, :, ALIBI:ALIBI + 3], pos, -1.0, None, ALU.mult)
                dve.tensor_copy(q[:, :, ALIBI + 3:ALIBI + 6], parts)
                dve.tensor_copy(k[:, :, ALIBI:ALIBI + 3], parts)
                last = dve.tensor_copy(k[:, :, ALIBI + 3:ALIBI + 6], pos)
            last.then_inc(prep["stack1"], 1)
            dve.wait_ge(prep["siminv"], 1)
            dve.wait_ge(prep["exptemp"], 1)
            dve.tensor_scalar(simt[:, :], simt[:, :], simst[:, 3:4], simst[:, 2:3], ALU.mult, ALU.mult)\
                .then_inc(prep["simt"], 1)
            dve.wait_ge(prep["simn_pe"], 1)
            dve.tensor_copy(simn[:, :], bank[0][0:PROJ, 0:NR]).then_inc(prep["simn"], 1)
            dve.wait_ge(loads["const"], 80)
            dve.wait_ge(loads["ffn"], 11 * 16)
            rounds(dve, VECTOR_ORDER, {"K": dve_k, "A": dve_a, "C": dve_c}, dve_g)


def constants():
    def bf(x):
        return (np.ascontiguousarray(x, np.float32).view(np.uint32) >> 16).astype(np.uint16)

    r = np.arange(P)
    mask = np.zeros((P, 2, P), np.float32)
    mask[:, 0] = np.where(r[None, :] > r[:, None], MASKED, 0)
    mask[:, 1] = np.where(r[:, None] > r[None, :], MASKED, 0)
    sel = np.zeros((P, H), np.float32)
    for h in range(H):
        sel[[h, H + h], h] = 1
    inv = (1.0 / np.float32(10000.0) ** (np.arange(0, DE, 2, dtype=np.float32) / np.float32(DE))).astype(np.float32)
    f = np.arange(T, dtype=np.float32)[:, None] * inv[None, :]
    f = np.concatenate([f, f], -1).astype(np.float32)
    rope = np.stack([np.cos(f), np.sin(f)]).astype(np.float32).reshape(2, NT, P, DE).transpose(2, 0, 1, 3)
    tri = [np.broadcast_to((np.arange(n)[None, :] < np.arange(n)[:, None]).astype(np.float32).reshape(1, -1),
                           (P, n * n)) for n in (NE, NR)]
    return {"identf": np.eye(P, dtype=np.float32), "identb": bf(np.eye(P)), "maskb": bf(mask),
            "selb": bf(sel), "rope": rope, "before": tri[0], "before4": tri[1],
            "position": (np.arange(T, dtype=np.float32) - P).reshape(NT, P).T}


def kernel(**inputs):
    import concourse.bacc as bacc
    from concourse.bass_utils import run_bass_kernel_spmd

    w = {k: np.asarray(v) for k, v in inputs.items()}
    arrays = dict(constants())
    for l in range(2):
        arrays[f"L{l}_c"] = w[f"L{l}_c"].T
        arrays[f"L{l}_wmod"] = w[f"L{l}_wmod"]
    u2 = np.zeros((P, 3, 2, 12), np.float32)
    for n, parts in enumerate((("Wq_up_c", "Wq_up_e"), ("Wk_up_c", "Wk_up_e"), ("Wv_up",))):
        up = np.concatenate([w["L0_attn_" + p] for p in parts], 1)
        for h in range(2):
            u2[L * h:L * (h + 1), n, h, 0:D] = up
    arrays["u2"] = u2
    arrays["wd3"] = np.stack([w[f"L0_attn_W{x}_down"].reshape(P, NPAIR, 2 * L).transpose(2, 1, 0)
                              for x in "qkv"], 1)
    arrays["L0_attn_Wc"] = w["L0_attn_Wc"]
    arrays["L0_attn_x"] = w["L0_attn_x"]
    for name in ("L1_attn_w_qkv", "L1_attn_w_out", "L0_ffn_attn_w", "L0_ffn_gate_w", "L1_ffn_sim"):
        arrays[name] = w[name].T
    arrays["L1_attn_alibi_slopes"] = w["L1_attn_alibi_slopes"]
    arrays["L1_ffn_temp"] = w["L1_ffn_temp"]
    arrays["L1_ffn_bp"] = w["L1_ffn_bp"]
    arrays["lncol"] = np.stack([w["L0_ffn_" + k] for k in ("ln1_g", "ln1_b", "ln2_g", "ln2_b")], 1)
    arrays["gu"] = np.stack([w[f"L0_ffn_{k}_proj"].reshape(NCH * P, P).T.reshape(P, NCH, P)
                             for k in ("gate", "up")], 1)
    arrays["L0_ffn_down_proj"] = w["L0_ffn_down_proj"].reshape(NE, P, CH, P).transpose(3, 0, 2, 1)        .reshape(P, NCH, P)
    arrays["w_ffn1"] = np.concatenate([w["L1_ffn_W"].T, w["L1_ffn_Wp"].T]
                                      + [w[f"L1_ffn_Wd{k}"].T for k in range(NR)], 1)
    arrays["w_up1"] = np.concatenate([w[f"L1_ffn_Wu{k}"].T for k in range(NR)], 0)

    nc = bacc.Bacc("TRN2", target_bir_lowering=False, num_devices=1)
    fed, aps = {}, {}
    for name, x in arrays.items():
        x = np.ascontiguousarray(x)
        fed["in_" + name] = x
        aps[name] = nc.dram_tensor("in_" + name, x.shape, mybir.dt.from_np(x.dtype), kind="ExternalInput").ap()
    aps["scratch"] = nc.dram_tensor("scratch", (B, ROWMODS, P), F32, kind="Internal").ap()
    out = nc.dram_tensor("out_0", (B, T, P), F32, kind="ExternalOutput").ap()
    build(nc, aps, out)
    return run_bass_kernel_spmd(nc, [fed], core_ids=[0]).results[0]["out_0"]
```
